# Optimizing a Trainium2 kernel written in Bass

```python
import numpy as np
import jax
import jax.numpy as jnp

def _softmax(x, axis=-1):
    return jax.nn.softmax(x, axis=axis)

def _gelu(x):
    return jax.nn.gelu(x, approximate=True)

def _silu(x):
    return jax.nn.silu(x)

def _sigmoid(x):
    return jax.nn.sigmoid(x)

def _layernorm(x, axis=-1, eps=1e-05):
    m = jnp.mean(x, axis=axis, keepdims=True)
    v = jnp.var(x, axis=axis, keepdims=True)
    return (x - m) / jnp.sqrt(v + eps)

def _scatter_add(tgt, idx, src, axis=0):
    return tgt.at[idx].add(src)

def _segment_sum(src, seg, n):
    return jax.ops.segment_sum(src, seg, n)
kernel_name = 'mk_adj_ffn_d4_adj_r2_b9a106'

def setup_inputs(seed: int=0):
    np.random.seed(seed)
    _w = jnp.asarray

    def _rec_inputs():
        import jax
        import jax.numpy as jnp
        _gk = jax.random.key(seed)
        x = -0.0002928 + 1 * jax.random.normal(jax.random.fold_in(_gk, 1), (1354, 256), jnp.float32)
        _a = jax.random.bernoulli(jax.random.fold_in(_gk, 2), 0.00590842, (1354, 1354))
        _a = jnp.logical_or(_a, jnp.swapaxes(_a, -1, -2))
        _a = jnp.logical_or(_a, jnp.eye(1354, dtype=bool))
        _af = _a.astype(jnp.float32)
        _af = _af * jax.random.uniform(jax.random.fold_in(_gk, 3), (1354, 1354), jnp.float32, 0.05, 0.0541998)
        adj = _af
        return (x, adj)
    x, adj = _rec_inputs()

    def _L0_gnn_setup():
        import jax, jax.numpy as jnp
        import numpy as np
        import math
        N = 4096
        D_IN = 256
        D_H = 256

        def _layer(x, cooccur, wq, bq, wk, bk, wv, bv, scale):
            q = x @ wq.T + bq
            k = x @ wk.T + bk
            v = x @ wv.T + bv
            att = jax.nn.softmax(jnp.einsum('ac,bc->ab', q, k) * scale, axis=-1)
            att = att + cooccur
            return jax.nn.relu(att @ v)
        key = jax.random.key(seed)
        ks = jax.random.split(key, 18)
        s_in = 1.0 / math.sqrt(D_IN)
        s_h = 1.0 / math.sqrt(D_H)
        f32 = jnp.float32
        return {'x': jax.random.normal(ks[0], (N, D_IN), dtype=f32), 'cooccur': jax.random.normal(ks[1], (N, N), dtype=f32) * 0.01, 'wq0': jax.random.normal(ks[2], (D_H, D_IN), dtype=f32) * s_in, 'bq0': jnp.zeros((D_H,), dtype=f32), 'wk0': jax.random.normal(ks[3], (D_H, D_IN), dtype=f32) * s_in, 'bk0': jnp.zeros((D_H,), dtype=f32), 'wv0': jax.random.normal(ks[4], (D_H, D_IN), dtype=f32) * s_in, 'bv0': jnp.zeros((D_H,), dtype=f32), 'wres': jax.random.normal(ks[5], (D_H, D_IN), dtype=f32) * s_in, 'bres': jnp.zeros((D_H,), dtype=f32), 'wq1': jax.random.normal(ks[6], (D_H, D_H), dtype=f32) * s_h, 'bq1': jnp.zeros((D_H,), dtype=f32), 'wk1': jax.random.normal(ks[7], (D_H, D_H), dtype=f32) * s_h, 'bk1': jnp.zeros((D_H,), dtype=f32), 'wv1': jax.random.normal(ks[8], (D_H, D_H), dtype=f32) * s_h, 'bv1': jnp.zeros((D_H,), dtype=f32)}
    _L0_gnn_all = _L0_gnn_setup()
    _L0_gnn_in = {k: v for k, v in _L0_gnn_all.items() if k in ('wq0', 'bq0', 'wk0', 'bk0', 'wv0', 'bv0', 'wres', 'bres', 'wq1', 'bq1', 'wk1', 'bk1', 'wv1', 'bv1')}
    del _L0_gnn_all

    def _L0_ffn_setup():
        import jax, jax.numpy as jnp
        import numpy as np
        B, S, D, H, E, K = (2, 1024, 256, 1024, 16, 2)
        LN_EPS = 1e-05
        key = jax.random.key(seed)
        ks = jax.random.split(key, 9)
        s_in = 1.0 / np.sqrt(D)
        s_hid = 1.0 / np.sqrt(H)
        return {'x': jax.random.normal(ks[0], (B, S, D), dtype=jnp.float32), 'Wg': jax.random.normal(ks[1], (D, E), dtype=jnp.float32) * s_in, 'bg': jax.random.normal(ks[2], (E,), dtype=jnp.float32) * 0.01, 'W1': jax.random.normal(ks[3], (E, D, H), dtype=jnp.float32) * s_in, 'b1': jax.random.normal(ks[4], (E, H), dtype=jnp.float32) * 0.01, 'W2': jax.random.normal(ks[5], (E, H, D), dtype=jnp.float32) * s_hid, 'b2': jax.random.normal(ks[6], (E, D), dtype=jnp.float32) * 0.01, 'gamma': jnp.ones((D,), dtype=jnp.float32), 'beta': jnp.zeros((D,), dtype=jnp.float32)}
    _L0_ffn_all = _L0_ffn_setup()
    _L0_ffn_in = {k: v for k, v in _L0_ffn_all.items() if k in ('Wg', 'bg', 'W1', 'b1', 'W2', 'b2', 'gamma', 'beta')}
    del _L0_ffn_all

    def _L1_gnn_setup():
        import jax, jax.numpy as jnp
        import numpy as np
        N = 4096
        D_IN = 256
        HEADS = 8
        DPH = 256 // HEADS
        EDGE_P = 0.01
        key = jax.random.key(seed)
        k1, k2, k3 = jax.random.split(key, 3)
        H = jax.random.normal(k1, (N, D_IN), dtype=jnp.float32)
        adj = (jax.random.uniform(k2, (N, N)) < EDGE_P).astype(jnp.float32)
        limit = float(np.sqrt(6.0 / (D_IN + DPH)))
        W = jax.random.uniform(k3, (HEADS, D_IN, DPH), jnp.float32, -limit, limit)
        b = jnp.zeros((HEADS, DPH), jnp.float32)
        return {'H': H, 'adj': adj, 'W': W, 'b': b}
    _L1_gnn_all = _L1_gnn_setup()
    _L1_gnn_in = {k: v for k, v in _L1_gnn_all.items() if k in ('W', 'b')}
    del _L1_gnn_all

    def _L1_ffn_setup():
        import jax, jax.numpy as jnp
        import numpy as np
        MARK_AX = 0
        OPCODE_BASE = 16
        OP_SHL = OPCODE_BASE + 23
        OP_SHR = OPCODE_BASE + 24
        ALU_LO = 64
        ALU_HI = 80
        AX_CARRY_LO = 96
        OUTPUT_LO = 128
        OUTPUT_HI = 144
        B, SEQ, D = (8, 16384, 256)
        key = jax.random.key(seed)
        ks = jax.random.split(key, 6)
        x = jax.random.uniform(ks[0], (B, SEQ, D), dtype=jnp.float32) * 0.4
        mark = (jax.random.uniform(ks[1], (B, SEQ)) < 0.75).astype(jnp.float32)
        op_sel = jax.random.randint(ks[2], (B, SEQ), 0, 3)
        lo = jax.random.randint(ks[3], (B, SEQ), 0, 16)
        hi = jax.random.randint(ks[4], (B, SEQ), 0, 16)
        sa = jax.random.randint(ks[5], (B, SEQ), 0, 16)
        oh = lambda idx: jax.nn.one_hot(idx, 16, dtype=jnp.float32)
        x = x.at[..., MARK_AX].set(mark)
        x = x.at[..., OP_SHL].set((op_sel == 1).astype(jnp.float32))
        x = x.at[..., OP_SHR].set((op_sel == 2).astype(jnp.float32))
        x = x.at[..., ALU_LO:ALU_LO + 16].set(oh(lo))
        x = x.at[..., ALU_HI:ALU_HI + 16].set(oh(hi))
        x = x.at[..., AX_CARRY_LO:AX_CARRY_LO + 16].set(oh(sa))
        return {'x_bd': x}
    _L1_ffn_all = _L1_ffn_setup()
    _L1_ffn_in = {k: v for k, v in _L1_ffn_all.items() if k in ()}
    del _L1_ffn_all

    def _L2_gnn_setup():
        import jax, jax.numpy as jnp
        import numpy as np
        N = 2048
        INPUT_DIM = 256
        KEY_DIM = 64
        OUT_DIM = 256
        N_HEADS = 8

        def _xavier_normal(key, shape, gain):
            fan_in, fan_out = (shape[-2], shape[-1])
            std = gain * (2.0 / (fan_in + fan_out)) ** 0.5
            return jax.random.normal(key, shape, dtype=jnp.float32) * std
        key = jax.random.key(seed)
        kx, ka, kk, kq, kv, ko = jax.random.split(key, 6)
        gain = 2.0 ** 0.5
        node_matrix = jax.random.normal(kx, (N, INPUT_DIM), dtype=jnp.float32)
        adjacency_matrix = jax.random.randint(ka, (N, N), 0, 2).astype(jnp.float32)
        Wks = _xavier_normal(kk, (N_HEADS, INPUT_DIM, KEY_DIM), gain)
        Wqs = _xavier_normal(kq, (N_HEADS, INPUT_DIM, KEY_DIM), gain)
        Wvs = _xavier_normal(kv, (N_HEADS, INPUT_DIM, KEY_DIM), gain)
        Wo = _xavier_normal(ko, (N_HEADS, KEY_DIM, OUT_DIM), gain)
        return {'node_matrix': node_matrix, 'adjacency_matrix': adjacency_matrix, 'Wks': Wks, 'Wqs': Wqs, 'Wvs': Wvs, 'Wo': Wo}
    _L2_gnn_all = _L2_gnn_setup()
    _L2_gnn_in = {k: v for k, v in _L2_gnn_all.items() if k in ('Wks', 'Wqs', 'Wvs', 'Wo')}
    del _L2_gnn_all

    def _L2_ffn_setup():
        import jax, jax.numpy as jnp
        import numpy as np
        D = 256
        H = 1024
        E = 8
        TOPK = 2
        key = jax.random.key(seed)
        ks = jax.random.split(key, 5)
        s = 0.02
        x = jax.random.normal(ks[0], (4, 4096, D), dtype=jnp.float32)
        gate_w = jax.random.normal(ks[1], (D, E), dtype=jnp.float32) * s
        W1 = jax.random.normal(ks[2], (E, D, H), dtype=jnp.float32) * s
        W3 = jax.random.normal(ks[3], (E, D, H), dtype=jnp.float32) * s
        W2 = jax.random.normal(ks[4], (E, H, D), dtype=jnp.float32) * s
        return {'x': x, 'gate_w': gate_w, 'W1': W1, 'W2': W2, 'W3': W3}
    _L2_ffn_all = _L2_ffn_setup()
    _L2_ffn_in = {k: v for k, v in _L2_ffn_all.items() if k in ('gate_w', 'W1', 'W2', 'W3')}
    del _L2_ffn_all

    def _L3_gnn_setup():
        import jax, jax.numpy as jnp
        import numpy as np
        N = 3072
        D_IN = 256
        D_OUT = 256
        DENSITY = 0.005
        key = jax.random.key(seed)
        ks = jax.random.split(key, 12)
        x = jax.random.normal(ks[0], (N, D_IN), dtype=jnp.float32)
        adj_a = (jax.random.uniform(ks[1], (N, N)) < DENSITY).astype(jnp.float32)
        adj_b = (jax.random.uniform(ks[2], (N, N)) < DENSITY).astype(jnp.float32)
        W_sa = jax.random.normal(ks[3], (D_IN, D_OUT), dtype=jnp.float32) * (1.414 / np.sqrt(D_IN + D_OUT))
        a_sa = jax.random.normal(ks[4], (1, 2 * D_OUT), dtype=jnp.float32) * (1.414 / np.sqrt(1 + 2 * D_OUT))
        stdv = 1.0 / np.sqrt(D_OUT)
        W_gcnb = jax.random.uniform(ks[5], (D_IN, D_OUT), minval=-stdv, maxval=stdv, dtype=jnp.float32)
        b_gcnb = jax.random.uniform(ks[6], (D_OUT,), minval=-stdv, maxval=stdv, dtype=jnp.float32)
        s = 1.0 / np.sqrt(2 * D_IN)
        Wa = jax.random.uniform(ks[7], (1, 2 * D_IN), minval=-s, maxval=s, dtype=jnp.float32)
        ba = jax.random.uniform(ks[8], (1,), minval=-s, maxval=s, dtype=jnp.float32)
        Wb = jax.random.uniform(ks[9], (1, 2 * D_IN), minval=-s, maxval=s, dtype=jnp.float32)
        bb = jax.random.uniform(ks[10], (1,), minval=-s, maxval=s, dtype=jnp.float32)
        return {'x': x, 'adj_a': adj_a, 'adj_b': adj_b, 'W_sa': W_sa, 'a_sa': a_sa, 'W_gcnb': W_gcnb, 'b_gcnb': b_gcnb, 'Wa': Wa, 'ba': ba, 'Wb': Wb, 'bb': bb}
    _L3_gnn_all = _L3_gnn_setup()
    _L3_gnn_in = {k: v for k, v in _L3_gnn_all.items() if k in ('W_sa', 'a_sa', 'W_gcnb', 'b_gcnb', 'Wa', 'ba', 'Wb', 'bb')}
    del _L3_gnn_all

    def _L3_ffn_setup():
        import jax, jax.numpy as jnp
        import numpy as np
        NUM_EXPERTS = 8
        TOP_K = 2
        key = jax.random.key(seed)
        ks = jax.random.split(key, 5)
        B, T, D, H, E = (8, 2048, 256, 768, NUM_EXPERTS)
        scale = 0.02
        x = jax.random.normal(ks[0], (B, T, D), dtype=jnp.float32)
        gate_w = jax.random.normal(ks[1], (E, D), dtype=jnp.float32) * scale
        w1 = jax.random.normal(ks[2], (E, H, D), dtype=jnp.float32) * scale
        w3 = jax.random.normal(ks[3], (E, H, D), dtype=jnp.float32) * scale
        w2 = jax.random.normal(ks[4], (E, D, H), dtype=jnp.float32) * scale
        return {'x': x, 'gate_w': gate_w, 'w1': w1, 'w3': w3, 'w2': w2}
    _L3_ffn_all = _L3_ffn_setup()
    _L3_ffn_in = {k: v for k, v in _L3_ffn_all.items() if k in ('gate_w', 'w1', 'w3', 'w2')}
    del _L3_ffn_all
    return {'x': x, 'adj': adj, 'L0_gnn_wq0': _L0_gnn_in['wq0'], 'L0_gnn_bq0': _L0_gnn_in['bq0'], 'L0_gnn_wk0': _L0_gnn_in['wk0'], 'L0_gnn_bk0': _L0_gnn_in['bk0'], 'L0_gnn_wv0': _L0_gnn_in['wv0'], 'L0_gnn_bv0': _L0_gnn_in['bv0'], 'L0_gnn_wres': _L0_gnn_in['wres'], 'L0_gnn_bres': _L0_gnn_in['bres'], 'L0_gnn_wq1': _L0_gnn_in['wq1'], 'L0_gnn_bq1': _L0_gnn_in['bq1'], 'L0_gnn_wk1': _L0_gnn_in['wk1'], 'L0_gnn_bk1': _L0_gnn_in['bk1'], 'L0_gnn_wv1': _L0_gnn_in['wv1'], 'L0_gnn_bv1': _L0_gnn_in['bv1'], 'L0_ffn_Wg': _L0_ffn_in['Wg'], 'L0_ffn_bg': _L0_ffn_in['bg'], 'L0_ffn_W1': _L0_ffn_in['W1'], 'L0_ffn_b1': _L0_ffn_in['b1'], 'L0_ffn_W2': _L0_ffn_in['W2'], 'L0_ffn_b2': _L0_ffn_in['b2'], 'L0_ffn_gamma': _L0_ffn_in['gamma'], 'L0_ffn_beta': _L0_ffn_in['beta'], 'L1_gnn_W': _L1_gnn_in['W'], 'L1_gnn_b': _L1_gnn_in['b'], 'L2_gnn_Wks': _L2_gnn_in['Wks'], 'L2_gnn_Wqs': _L2_gnn_in['Wqs'], 'L2_gnn_Wvs': _L2_gnn_in['Wvs'], 'L2_gnn_Wo': _L2_gnn_in['Wo'], 'L2_ffn_gate_w': _L2_ffn_in['gate_w'], 'L2_ffn_W1': _L2_ffn_in['W1'], 'L2_ffn_W2': _L2_ffn_in['W2'], 'L2_ffn_W3': _L2_ffn_in['W3'], 'L3_gnn_W_sa': _L3_gnn_in['W_sa'], 'L3_gnn_a_sa': _L3_gnn_in['a_sa'], 'L3_gnn_W_gcnb': _L3_gnn_in['W_gcnb'], 'L3_gnn_b_gcnb': _L3_gnn_in['b_gcnb'], 'L3_gnn_Wa': _L3_gnn_in['Wa'], 'L3_gnn_ba': _L3_gnn_in['ba'], 'L3_gnn_Wb': _L3_gnn_in['Wb'], 'L3_gnn_bb': _L3_gnn_in['bb'], 'L3_ffn_gate_w': _L3_ffn_in['gate_w'], 'L3_ffn_w1': _L3_ffn_in['w1'], 'L3_ffn_w3': _L3_ffn_in['w3'], 'L3_ffn_w2': _L3_ffn_in['w2']}

def reference(x, adj, L0_gnn_wq0, L0_gnn_bq0, L0_gnn_wk0, L0_gnn_bk0, L0_gnn_wv0, L0_gnn_bv0, L0_gnn_wres, L0_gnn_bres, L0_gnn_wq1, L0_gnn_bq1, L0_gnn_wk1, L0_gnn_bk1, L0_gnn_wv1, L0_gnn_bv1, L0_ffn_Wg, L0_ffn_bg, L0_ffn_W1, L0_ffn_b1, L0_ffn_W2, L0_ffn_b2, L0_ffn_gamma, L0_ffn_beta, L1_gnn_W, L1_gnn_b, L2_gnn_Wks, L2_gnn_Wqs, L2_gnn_Wvs, L2_gnn_Wo, L2_ffn_gate_w, L2_ffn_W1, L2_ffn_W2, L2_ffn_W3, L3_gnn_W_sa, L3_gnn_a_sa, L3_gnn_W_gcnb, L3_gnn_b_gcnb, L3_gnn_Wa, L3_gnn_ba, L3_gnn_Wb, L3_gnn_bb, L3_ffn_gate_w, L3_ffn_w1, L3_ffn_w3, L3_ffn_w2):
    import jax
    import jax.numpy as jnp

    def _L0_gnn_ref(x, cooccur, wq0, bq0, wk0, bk0, wv0, bv0, wres, bres, wq1, bq1, wk1, bk1, wv1, bv1):
        import jax, jax.numpy as jnp
        import numpy as np
        import math
        N = 4096
        D_IN = 256
        D_H = 256

        def _layer(x, cooccur, wq, bq, wk, bk, wv, bv, scale):
            q = x @ wq.T + bq
            k = x @ wk.T + bk
            v = x @ wv.T + bv
            att = jax.nn.softmax(jnp.einsum('ac,bc->ab', q, k) * scale, axis=-1)
            att = att + cooccur
            return jax.nn.relu(att @ v)
        scale = 1.0 / math.sqrt(D_H)
        x = _layer(x, cooccur, wq0, bq0, wk0, bk0, wv0, bv0, scale) + (x @ wres.T + bres)
        x = _layer(x, cooccur, wq1, bq1, wk1, bk1, wv1, bv1, scale) + x
        return x

    def _L0_ffn_ref(x, Wg, bg, W1, b1, W2, b2, gamma, beta):
        import jax, jax.numpy as jnp
        import numpy as np
        B, S, D, H, E, K = (2, 1024, 256, 1024, 16, 2)
        LN_EPS = 1e-05
        logits = jnp.einsum('bsd,de->bse', x, Wg) + bg
        probs = jax.nn.softmax(logits, axis=-1)
        topk_vals, topk_idx = jax.lax.top_k(probs, K)
        sparse = (jax.nn.one_hot(topk_idx, E, dtype=probs.dtype) * topk_vals[..., None]).sum(axis=-2)
        h = jax.nn.relu(jnp.einsum('bsd,edh->ebsh', x, W1) + b1[:, None, None, :])
        ex = jnp.einsum('ebsh,ehd->ebsd', h, W2) + b2[:, None, None, :]
        out = jnp.einsum('bse,ebsd->bsd', sparse, ex) + x
        mu = out.mean(axis=-1, keepdims=True)
        var = ((out - mu) ** 2).mean(axis=-1, keepdims=True)
        out = (out - mu) * jax.lax.rsqrt(var + LN_EPS) * gamma + beta
        return out

    def _L1_gnn_ref(H, adj, W, b):
        import jax, jax.numpy as jnp
        import numpy as np
        N = 4096
        D_IN = 256
        HEADS = 8
        DPH = 256 // HEADS
        EDGE_P = 0.01
        H_ = jnp.einsum('nd,hde->hne', H, W)
        out = jnp.einsum('nm,hme->hne', adj, H_) + b[:, None, :]
        return jnp.transpose(out, (1, 0, 2)).reshape(H.shape[0], HEADS * DPH)

    def _L1_ffn_ref(x_bd):
        import jax, jax.numpy as jnp
        import numpy as np
        MARK_AX = 0
        OPCODE_BASE = 16
        OP_SHL = OPCODE_BASE + 23
        OP_SHR = OPCODE_BASE + 24
        ALU_LO = 64
        ALU_HI = 80
        AX_CARRY_LO = 96
        OUTPUT_LO = 128
        OUTPUT_HI = 144
        B, SEQ, D = (8, 16384, 256)
        hot = x_bd > 0.5
        first16 = lambda off: jnp.argmax(hot[..., off:off + 16], axis=-1).astype(jnp.int32)
        lo = first16(ALU_LO)
        hi = first16(ALU_HI)
        sa = first16(AX_CARRY_LO)
        val = lo + 16 * hi
        shl = jnp.left_shift(val, sa) & 255
        shr = jnp.right_shift(val, sa)
        mark = hot[..., MARK_AX]
        is_shl = hot[..., OP_SHL]
        is_shr = jnp.logical_and(hot[..., OP_SHR], jnp.logical_not(is_shl))
        act_shl = jnp.logical_and(mark, is_shl)
        act_shr = jnp.logical_and(mark, is_shr)
        active = jnp.logical_or(act_shl, act_shr)
        res = jnp.where(act_shl, shl, jnp.where(act_shr, shr, 0))
        res = jnp.clip(res, 0, 255)
        rlo = res & 15
        rhi = res >> 4
        amp = 2.0 * active.astype(x_bd.dtype)
        add_lo = amp[..., None] * jax.nn.one_hot(rlo, 16, dtype=x_bd.dtype)
        add_hi = amp[..., None] * jax.nn.one_hot(rhi, 16, dtype=x_bd.dtype)
        out = x_bd.at[..., OUTPUT_LO:OUTPUT_LO + 16].add(add_lo)
        out = out.at[..., OUTPUT_HI:OUTPUT_HI + 16].add(add_hi)
        return out

    def _L2_gnn_ref(node_matrix, adjacency_matrix, Wks, Wqs, Wvs, Wo):
        import jax, jax.numpy as jnp
        import numpy as np
        N = 2048
        INPUT_DIM = 256
        KEY_DIM = 64
        OUT_DIM = 256
        N_HEADS = 8

        def _xavier_normal(key, shape, gain):
            fan_in, fan_out = (shape[-2], shape[-1])
            std = gain * (2.0 / (fan_in + fan_out)) ** 0.5
            return jax.random.normal(key, shape, dtype=jnp.float32) * std
        n = adjacency_matrix.shape[0]
        adj = jnp.maximum(adjacency_matrix, jnp.eye(n, dtype=adjacency_matrix.dtype))
        keys = jnp.einsum('nj,hjk->hnk', node_matrix, Wks)
        queries = jnp.einsum('nj,hjk->hnk', node_matrix, Wqs)
        values = jnp.einsum('nj,hjk->hnk', node_matrix, Wvs)
        key_dim = Wks.shape[-1]
        atts = jnp.einsum('hqk,hmk->hqm', queries, keys) / key_dim ** 0.5
        atts = atts - 1e+16 * (1.0 - adj)[None, :, :]
        atts = jax.nn.softmax(atts, axis=-1)
        return jnp.einsum('hqm,hmk,hko->qo', atts, values, Wo)

    def _L2_ffn_ref(x, gate_w, W1, W2, W3):
        import jax, jax.numpy as jnp
        import numpy as np
        D = 256
        H = 1024
        E = 8
        TOPK = 2
        B, S, _ = x.shape
        xt = x.reshape(-1, D)
        T = xt.shape[0]
        gate_logits = xt @ gate_w
        w, idx = jax.lax.top_k(gate_logits, TOPK)
        w = jax.nn.softmax(w, axis=1).astype(xt.dtype)
        comb = jnp.zeros((T, E), dtype=xt.dtype).at[jnp.arange(T)[:, None], idx].add(w)
        out = jnp.zeros_like(xt)
        for e in range(E):
            h = jax.nn.silu(xt @ W1[e]) * (xt @ W3[e])
            out = out + h @ W2[e] * comb[:, e:e + 1]
        return out.reshape(B, S, D)

    def _L3_gnn_ref(x, adj_a, adj_b, W_sa, a_sa, W_gcnb, b_gcnb, Wa, ba, Wb, bb):
        import jax, jax.numpy as jnp
        import numpy as np
        N = 3072
        D_IN = 256
        D_OUT = 256
        DENSITY = 0.005
        type_sum_a = adj_a @ x
        type_sum_b = adj_b @ x
        attn_a = jax.nn.sigmoid(jnp.concatenate([type_sum_a, x], axis=1) @ Wa.T + ba)
        attn_b = jax.nn.sigmoid(jnp.concatenate([type_sum_b, x], axis=1) @ Wb.T + bb)
        h = x @ W_sa
        Hd = h.shape[1]
        s_left = h @ a_sa[0, :Hd]
        s_right = h @ a_sa[0, Hd:]
        scores = s_left[:, None] + s_right[None, :]
        e = jnp.where(adj_a != 0, jnp.exp(-jax.nn.leaky_relu(scores, 0.01)), 0.0)
        attn = e / (jnp.sum(e, axis=1, keepdims=True) + 1e-05)
        x_a = attn @ h
        x_b = adj_b @ (x @ W_gcnb) + b_gcnb
        return jax.nn.sigmoid(attn_a * x_a + attn_b * x_b)

    def _L3_ffn_ref(x, gate_w, w1, w3, w2):
        import jax, jax.numpy as jnp
        import numpy as np
        NUM_EXPERTS = 8
        TOP_K = 2
        B, T, D = x.shape
        E = gate_w.shape[0]
        xf = x.reshape(-1, D)
        N = xf.shape[0]
        gate_logits = xf @ gate_w.T
        weights, indices = jax.lax.top_k(gate_logits, TOP_K)
        weights = jax.nn.softmax(weights, axis=-1)
        combine = jnp.zeros((N, E), dtype=xf.dtype).at[jnp.arange(N)[:, None], indices].add(weights)
        out = jnp.zeros_like(xf)
        for e in range(E):
            h = jax.nn.silu(xf @ w1[e].T) * (xf @ w3[e].T)
            y = h @ w2[e].T
            out = out + combine[:, e:e + 1] * y
        return out.reshape(B, T, D)
    x = x + _L0_gnn_ref(_layernorm(x, axis=-1), adj, L0_gnn_wq0, L0_gnn_bq0, L0_gnn_wk0, L0_gnn_bk0, L0_gnn_wv0, L0_gnn_bv0, L0_gnn_wres, L0_gnn_bres, L0_gnn_wq1, L0_gnn_bq1, L0_gnn_wk1, L0_gnn_bk1, L0_gnn_wv1, L0_gnn_bv1)
    x = x + _L0_ffn_ref(_layernorm(x, axis=-1)[None], L0_ffn_Wg, L0_ffn_bg, L0_ffn_W1, L0_ffn_b1, L0_ffn_W2, L0_ffn_b2, L0_ffn_gamma, L0_ffn_beta)[0]
    x = x + _L1_gnn_ref(_layernorm(x, axis=-1), adj, L1_gnn_W, L1_gnn_b)
    x = x + _L1_ffn_ref(_layernorm(x, axis=-1)[None])[0]
    x = x + _L2_gnn_ref(_layernorm(x, axis=-1), adj, L2_gnn_Wks, L2_gnn_Wqs, L2_gnn_Wvs, L2_gnn_Wo)
    x = x + _L2_ffn_ref(_layernorm(x, axis=-1)[None], L2_ffn_gate_w, L2_ffn_W1, L2_ffn_W2, L2_ffn_W3)[0]
    x = x + _L3_gnn_ref(_layernorm(x, axis=-1), adj, adj, L3_gnn_W_sa, L3_gnn_a_sa, L3_gnn_W_gcnb, L3_gnn_b_gcnb, L3_gnn_Wa, L3_gnn_ba, L3_gnn_Wb, L3_gnn_bb)
    x = x + _L3_ffn_ref(_layernorm(x, axis=-1)[None], L3_ffn_gate_w, L3_ffn_w1, L3_ffn_w3, L3_ffn_w2)[0]
    return x

_drawn_inputs = setup_inputs


def setup_inputs(seed=0):
    import zlib

    import numpy as np

    out = dict(_drawn_inputs(seed))
    spreads = {'L0_gnn_bq0': (0.0, 0.8),
     'L0_gnn_bk0': (0.0, 2.0),
     'L0_gnn_bv0': (0.0, 0.1),
     'L0_gnn_bres': (0.0, 0.1),
     'L0_gnn_bq1': (0.0, 0.784),
     'L0_gnn_bk1': (0.0, 2.0),
     'L0_gnn_bv1': (0.0, 0.1),
     'L0_ffn_gamma': (1.0, 0.2),
     'L0_ffn_beta': (0.0, 0.1),
     'L1_gnn_b': (0.0, 0.1)}
    factors = {'L0_ffn_bg': 8.0,
     'L0_ffn_b1': 8.0,
     'L0_ffn_b2': 8.0,
     'L2_ffn_gate_w': 8.0,
     'L2_ffn_W1': 8.0,
     'L2_ffn_W2': 8.0,
     'L2_ffn_W3': 8.0,
     'L3_gnn_W_sa': 7.707,
     'L3_gnn_a_sa': 8.0,
     'L3_gnn_W_gcnb': 26.192,
     'L3_gnn_b_gcnb': 64.0,
     'L3_gnn_Wa': 25.344,
     'L3_gnn_Wb': 35.421,
     'L3_ffn_gate_w': 8.0,
     'L3_ffn_w1': 8.0,
     'L3_ffn_w3': 8.0,
     'L3_ffn_w2': 8.0}
    for name, (base, spread) in spreads.items():
        noise = np.random.default_rng([zlib.crc32(name.encode()), seed]).standard_normal(out[name].shape)
        drawn = base * np.exp(spread * noise) if base else spread * noise
        out[name] = jnp.asarray(drawn.astype(out[name].dtype))
    for name, factor in factors.items():
        out[name] = (out[name] * factor).astype(out[name].dtype)
    return out
```

```python
from contextlib import ExitStack

import concourse.bass as bass
from concourse import mybir

F32 = mybir.dt.float32
F32R = mybir.dt.float32r
I32 = mybir.dt.int32
U32 = mybir.dt.uint32
ALU = mybir.AluOpType
ACT = mybir.ActivationFunctionType
AX = mybir.AxisListType.X

P = 128
N = 1354
NT = -(-N // P)
TAIL = N - (NT - 1) * P
NP = NT * P
D = 256
DC = D // P
BANK = 512
EPS = 1e-5
COLS = [(0, BANK), (BANK, BANK), (2 * BANK, N - 2 * BANK)]
GROUPS = [(0, 4), (4, 8), (8, NT)]
HEADS, HD = 8, 64
MASK = 1e16
IOTA = 48
EXPERTS = (16, 8, 8)
HIDDEN = (1024, 1024, 768)
SLOTS = [2 * N // P + e for e in EXPERTS]


def rows_of(k):
    return TAIL if k == NT - 1 else P


def tiles(eng, count, body):
    last = (count - 1) // 2
    body((0, 0, 0), None)
    body((1, 0, 1), (0, 0, 0))
    body((2, 1, 0), (1, 0, 1))
    with eng.Fori(1, last - 1) as s:
        body((2 * s + 1, s, 1), (2 * s, s, 0))
        body((2 * s + 2, s + 1, 0), (2 * s + 1, s, 1))
    body((2 * last - 1, last - 1, 1), (2 * last - 2, last - 1, 0))
    body((2 * last, last, 0), (2 * last - 1, last - 1, 1))
    return 2 * last, last, 0


class Shared:

    def __init__(self, x, ident, ones, before, iota, past_end):
        self.x, self.ident, self.ones = x, ident, ones
        self.before, self.iota, self.past_end = before, iota, past_end


class Routing:

    def __init__(self, slot, weight, expert):
        self.slot, self.weight, self.expert = slot, weight, expert


class Stage:

    def __init__(self, nc, name):
        self.nc, self.name = nc, name

    def __enter__(self):
        self.ctx, self.taken = ExitStack(), []
        return self

    def __exit__(self, *a):
        self.ctx.close()
        self.nc.clear_and_free_semaphores(self.taken)
        self.nc.all_engine_barrier()

    def sb(self, name, shape, dt=F32):
        return self.ctx.enter_context(self.nc.sbuf_tensor(f"{self.name}_{name}", shape, dt))

    def banks(self, name, n):
        return self.ctx.enter_context(self.nc.psum_tensor(f"{self.name}_{name}", [P, n * BANK], F32))

    def sem(self, name):
        self.taken.append(self.nc.alloc_semaphore(f"{self.name}_{name}"))
        return self.taken[-1]

    def sems(self, name):
        return [self.sem(f"{name}{u}") for u in range(2)]

    def block(self):
        return self.ctx.enter_context(self.nc.Block())


def start_stage(nc, g, d):
    with Stage(nc, "start") as st:
        zeros = st.sb("zeros", [P, 1024])
        rows_i = st.sb("rows_i", [P, IOTA], I32)
        loaded, made, filled, cleared = (st.sem(x) for x in ("loaded", "made", "filled", "cleared"))
        block = st.block()

        @block.sync
        def _(sp):
            sp.dma_start(g.x[:, :, :], d["x"]).then_inc(loaded, 16)
            sp.wait_ge(made, 1)
            slots = [s.rearrange("(n a) d -> a n d", a=P) for s in d["slot_rows"]]
            for s in slots:
                n = s.shape[1]
                for a in range(0, n, 4):
                    b = min(a + 4, n)
                    sp.dma_start(s[:, a:b, :], zeros[:, 0:(b - a) * D].rearrange("p (n d) -> p n d", d=D)) \
                      .then_inc(cleared, 16)
            sp.wait_ge(loaded, 16)
            sp.wait_ge(cleared, 16 * sum(-(-s.shape[1] // 4) for s in slots))

        @block.gpsimd
        def _(pool):
            pool.iota(rows_i[:, :], pattern=[[1, IOTA]], base=0, channel_multiplier=0).then_inc(filled, 1)
            pool.memset(g.ident[:, :], 0.0).then_inc(filled, 1)
            pool.memset(g.before[:, :], 1.0).then_inc(filled, 1)
            pool.memset(g.past_end[:, :], 0.0).then_inc(filled, 1)
            pool.wait_ge(filled, 4)
            pool.affine_select(out=g.past_end[:, NT - 1:NT], in_=g.past_end[:, NT - 1:NT], compare_op=ALU.is_gt,
                               fill=100.0, base=TAIL, pattern=[[0, 1]], channel_multiplier=-1).then_inc(filled, 1)
            pool.tensor_copy(g.iota[:, :], rows_i[:, :]).then_inc(filled, 1)
            pool.affine_select(out=g.ident[:, :], in_=g.ident[:, :], compare_op=ALU.not_equal, fill=1.0,
                               base=0, pattern=[[-1, P]], channel_multiplier=1).then_inc(filled, 1)
            pool.affine_select(out=g.before[:, :], in_=g.before[:, :], compare_op=ALU.is_gt, fill=0.0,
                               base=0, pattern=[[1, P]], channel_multiplier=-1).then_inc(filled, 1)
            pool.wait_ge(filled, 8)

        @block.vector
        def _(dve):
            dve.memset(zeros[:, :], 0.0).then_inc(made, 1)
            dve.memset(g.ones[:, :], 1.0).then_inc(made, 1)
            dve.wait_ge(made, 2)


def inverse_root(dve, rstd, variance, root, asked, ready, step):
    v, half, sq = root[:, 0, :], root[:, 1, :], root[:, 2, :]
    dve.tensor_scalar(v, variance, EPS, None, ALU.add).then_inc(asked, 1)
    dve.wait_ge(ready, 1)
    dve.reciprocal(half, half).then_inc(step, 1)
    dve.wait_ge(step, 1)
    dve.tensor_tensor(sq, half, half, ALU.mult).then_inc(step, 1)
    dve.wait_ge(step, 2)
    dve.tensor_tensor(sq, sq, v, ALU.mult).then_inc(step, 1)
    dve.wait_ge(step, 3)
    dve.tensor_scalar(sq, sq, -0.5, 1.5, ALU.mult, ALU.add).then_inc(step, 1)
    dve.wait_ge(step, 4)
    dve.tensor_tensor(rstd[:, :], half, sq, ALU.mult).then_inc(step, 1)
    dve.wait_ge(step, 5)


def project_stage(nc, g, name, src, normalise, d_w, width, dest, d_bias=None, xn=None, xt=None,
                  d_extra=None, extra=None, d_cols=None, cols=()):
    with Stage(nc, name) as st:
        w = st.sb("w", [P, DC, width])
        bias = st.sb("bias", [1, width]) if d_bias is not None else None
        wx = st.sb("wx", [P, DC, extra.shape[2]]) if extra is not None else None
        wc = st.sb("wc", [P, DC, d_cols[0].shape[2]]) if d_cols else None
        bc = st.sb("bc", [P, d_cols[1].shape[1]]) if d_cols and d_cols[1] is not None else None
        stats = st.sb("stats", [P, NT, 6])
        mv = st.sb("mv", [P, NT, 2])
        rstd = st.sb("rstd", [P, NT])
        xb = [st.sb(f"xb{u}", [P, D]) for u in range(2)]
        xtb = [st.sb(f"xtb{u}", [P, DC, P]) for u in range(2)]
        turned = [st.banks(f"turned{u}", 1) for u in range(2)]
        prod = [st.banks(f"prod{u}", 1) for u in range(2)]
        ring = [st.banks(f"ring{u}", 1) for u in range(4)]
        w_in = st.sem("w_in")
        stats_done, root_asked, root_ready, rstd_step = (
            st.sem(x) for x in ("stats_done", "root_asked", "root_ready", "rstd_step"))
        root = st.sb("root", [P, 3, NT])
        rows_ready, turn_ready, xt_ready, prod_ready, prod_taken, kept = (
            st.sems(x) for x in ("rows_ready", "turn_ready", "xt_ready", "prod_ready", "prod_taken", "kept"))
        kept_all, ring_ready, split_high = (st.sem(x) for x in ("kept_all", "ring_ready", "split_high"))
        ring_free = [st.sem(f"ring_free{n}") for n in range(4)]
        n_loads = 1 + (d_bias is not None) + (extra is not None) + (
            0 if not d_cols else 1 + (d_cols[1] is not None))
        keeps = xn is not None or xt is not None
        jobs = []
        m = 0
        for dst, tokens, biased, split in cols:
            for c in range(dst.shape[1] // (2 if split else 1)):
                for a in range(0, tokens, BANK):
                    jobs.append((m, dst, c, a, min(BANK, tokens - a), biased, split))
                m += 1
        split_at = [n for n, job in enumerate(jobs) if job[-1]]

        def halves(n):
            _, dst, c, a, size, _, _ = jobs[n]
            for e in range(2):
                yield (ring[n % 4][e * HD:(e + 1) * HD, 0:size], dst[0:HD, 2 * c + e, a:a + size],
                       dst[HD:2 * HD, 2 * c + e, a:a + size])

        block = st.block()

        @block.sync
        def _(sp):
            sp.dma_start(w[:, :, :], d_w).then_inc(w_in, 16)
            if bias is not None:
                sp.dma_start(bias[:, :], d_bias).then_inc(w_in, 16)
            if extra is not None:
                sp.dma_start(wx[:, :, :], d_extra).then_inc(w_in, 16)
            if d_cols:
                sp.dma_start(wc[:, :, :], d_cols[0]).then_inc(w_in, 16)
                if d_cols[1] is not None:
                    sp.dma_start(bc[:, :], d_cols[1]).then_inc(w_in, 16)
            sp.wait_ge(w_in, 16 * n_loads)

        @block.vector
        def _(dve):
            if normalise:
                for i in range(NT):
                    dve.bn_stats(stats[:, i, :], src[:, i, :]).then_inc(stats_done, 1)
                for i in range(NT):
                    dve.wait_ge(stats_done, i + 1)
                    dve.bn_aggr(mv[:, i, :], stats[:, i, :]).then_inc(stats_done, 1)
                dve.wait_ge(stats_done, 2 * NT)
                inverse_root(dve, rstd, mv[:, :, 1], root, root_asked, root_ready, rstd_step)

            def rows(t, _):
                i, s, u = t
                dve.wait_ge(turn_ready[u], s)
                if keeps:
                    dve.wait_ge(kept[u], s)
                if normalise:
                    dve.tensor_scalar(xb[u][:, :], src[:, i, :], mv[:, i, 0:1], rstd[:, bass.ds(i, 1)],
                                      ALU.subtract, ALU.mult).then_inc(rows_ready[u], 1)
                else:
                    dve.tensor_copy(xb[u][:, :], src[:, i, :]).then_inc(rows_ready[u], 1)

            tiles(dve, NT, rows)
            for n, (m, dst, c, a, size, biased, split) in enumerate(jobs):
                if split:
                    dve.wait_ge(split_high, split_at.index(n) + 1)
                    for rows_, high, low in halves(n):
                        ins = dve.tensor_tensor(low, rows_, high.bitcast(F32), ALU.subtract)
                    ins.then_inc(ring_free[n % 4], 1)
                elif n % 2:
                    dve.wait_ge(ring_ready, n + 1)
                    into = dst[:, c, a:a + size]
                    if biased is None:
                        ins = dve.tensor_copy(into, ring[n % 4][:, 0:size])
                    else:
                        dve.wait_ge(w_in, 16 * n_loads)
                        ins = dve.tensor_scalar(into, ring[n % 4][:, 0:size], bc[:, m:m + 1], None, ALU.add)
                    ins.then_inc(ring_free[n % 4], 1)

        @block.gpsimd
        def _(pool):
            if keeps:
                def keep(t, _):
                    i, s, u = t
                    if xn is not None:
                        pool.wait_ge(rows_ready[u], s + 1)
                        ins = pool.tensor_copy(xn[:, i, :], xb[u][:, :])
                    if xt is not None:
                        pool.wait_ge(xt_ready[u], s + 1)
                        ins = pool.tensor_copy(xt[:, :, bass.ts(i, P)], xtb[u][:, :, :])
                    ins.then_inc(kept[u], 1)

                tiles(pool, NT, keep)
                pool.wait_ge(kept[0], NT - NT // 2)
                pool.wait_ge(kept[1], NT // 2)
                pool.sem_inc(kept_all, 1)

        @block.tensor
        def _(pe):
            pe.wait_ge(w_in, 16 * n_loads)

            def turn(t):
                i, s, u = t
                pe.wait_ge(rows_ready[u], s + 1)
                pe.wait_ge(xt_ready[u], s)
                for c in range(DC):
                    ins = pe.transpose(turned[u][:, c * P:(c + 1) * P], xb[u][:, c * P:(c + 1) * P], g.ident[:, :])
                ins.then_inc(turn_ready[u], 1)

            def product(t):
                i, s, u = t
                pe.wait_ge(xt_ready[u], s + 1)
                pe.wait_ge(prod_taken[u], s)
                if bias is not None:
                    pe.matmul(prod[u][:, 0:width], g.ones[0:1, :], bias[:, :], start=True, stop=False)
                for c in range(DC):
                    ins = pe.matmul(prod[u][:, 0:width], xtb[u][:, c, :], w[:, c, :],
                                    start=(c == 0 and bias is None), stop=(c == DC - 1))
                if extra is not None:
                    m = extra.shape[2]
                    for c in range(DC):
                        ins = pe.matmul(ring[u][:, 0:m], xtb[u][:, c, :], wx[:, c, :],
                                        start=(c == 0), stop=(c == DC - 1))
                ins.then_inc(prod_ready[u], 1)

            def body(t, prev):
                turn(t)
                if prev is not None:
                    product(prev)

            product(tiles(pe, NT, body))
            if jobs:
                pe.wait_ge(kept_all, 1)
                if extra is not None:
                    pe.wait_ge(prod_taken[0], NT - NT // 2)
                    pe.wait_ge(prod_taken[1], NT // 2)
            for n, (m, dst, col, a, size, biased, split) in enumerate(jobs):
                pe.wait_ge(ring_free[n % 4], n // 4)
                for c in range(DC):
                    ins = pe.matmul(ring[n % 4][:, 0:size], wc[:, c, m * P:(m + 1) * P], xt[:, c, a:a + size],
                                    start=(c == 0), stop=(c == DC - 1))
                ins.then_inc(ring_ready, 1)

        @block.scalar
        def _(act):
            if normalise:
                act.wait_ge(root_asked, 1)
                act.activation(root[:, 1, :], root[:, 0, :], ACT.Sqrt).then_inc(root_ready, 1)

            def turn_out(t):
                i, s, u = t
                act.wait_ge(turn_ready[u], s + 1)
                act.wait_ge(prod_ready[u], s)
                if xt is not None:
                    act.wait_ge(kept[u], s)
                act.copy(xtb[u][:, :, :], turned[u][:, 0:D].rearrange("p (c n) -> p c n", c=DC)) \
                   .then_inc(xt_ready[u], 1)

            def product_out(t):
                i, s, u = t
                act.wait_ge(prod_ready[u], s + 1)
                ins = act.copy(dest[:, i, :], prod[u][:, 0:width])
                if extra is not None:
                    ins = act.copy(extra[:, i, :], ring[u][:, 0:extra.shape[2]])
                ins.then_inc(prod_taken[u], 1)

            def body(t, prev):
                turn_out(t)
                if prev is not None:
                    product_out(prev)

            product_out(tiles(act, NT, body))
            for n, (m, dst, c, a, size, biased, split) in enumerate(jobs):
                if split:
                    act.wait_ge(ring_ready, n + 1)
                    for rows_, high, low in halves(n):
                        ins = act.copy(high, rows_)
                    ins.then_inc(split_high, 1)
                elif n % 2 == 0:
                    act.wait_ge(ring_ready, n + 1)
                    into = dst[:, c, a:a + size]
                    if biased is None:
                        ins = act.copy(into, ring[n % 4][:, 0:size])
                    else:
                        act.wait_ge(w_in, 16 * n_loads)
                        ins = act.activation(into, ring[n % 4][:, 0:size], ACT.Identity, bias=bc[:, m:m + 1])
                    ins.then_inc(ring_free[n % 4], 1)


def attention_stage(nc, g, d, name, qt, kt, v, res, layer):
    scale = float(D) ** -0.5
    with Stage(nc, name) as st:
        adj = [st.sb(f"adj{u}", [P, NP]) for u in range(2)]
        qs = [st.sb(f"qs{u}", [P, DC, P]) for u in range(2)]
        att = st.sb("att", [P, N])
        att_t = st.sb("att_t", [P, NT, P])
        top, neg, total, inv = (st.sb(x, [P, 1]) for x in ("top", "neg", "total", "inv"))
        scores = st.banks("scores", 3)
        turned = [st.banks(f"turned{b}", 1) for b in range(3)]
        out = st.banks("out", 1)
        adj_in, adj_used, qs_ready = st.sems("adj_in"), st.sems("adj_used"), st.sems("qs_ready")
        (scores_ready, top_ready, neg_ready, exp_done, inv_ready, att_ready, out_ready, out_used, res_ready,
         copied_act, copied_dve) = (st.sem(x) for x in (
             "scores_ready", "top_ready", "neg_ready", "exp_done", "inv_ready", "att_ready", "out_ready",
             "out_used", "res_ready", "copied_act", "copied_dve"))
        turn_ready = [st.sem(f"turn_ready{b}") for b in range(3)]
        block = st.block()

        @block.sync
        def _(sp):
            def body(t, _):
                i, s, u = t
                sp.wait_ge(adj_used[u], s)
                sp.dma_start(adj[u][:, :], d["adj_rows"][bass.ds(i, 1), :, :].rearrange("a p n -> (a p) n")) \
                  .then_inc(adj_in[u], 16)

            tiles(sp, NT, body)

        @block.gpsimd
        def _(pool):
            if layer == 1:
                pool.tensor_tensor(g.x[:, :, :], g.x[:, :, :], res[:, :, :], ALU.add).then_inc(res_ready, 1)

            def body(t, _):
                i, s, u = t
                pool.wait_ge(scores_ready, 2 * s)
                pool.tensor_copy(qs[u][:, :, :], qt[:, :, bass.ts(i, P)]).then_inc(qs_ready[u], 1)

            tiles(pool, NT, body)

        @block.tensor
        def _(pe):
            def score(t):
                i, s, u = t
                pe.wait_ge(qs_ready[u], s + 1)
                pe.wait_ge(exp_done, i)
                for a, size in COLS:
                    for c in range(DC):
                        ins = pe.matmul(scores[:, a:a + size], qs[u][:, c, :], kt[:, c, a:a + size],
                                        start=(c == 0), stop=(c == DC - 1))
                ins.then_inc(scores_ready, 1)

            def turn(t):
                i, s, u = t
                pe.wait_ge(att_ready, i + 1)
                pe.wait_ge(copied_act, 2 * i)
                pe.wait_ge(copied_dve, i)
                for b, (k0, k1) in enumerate(GROUPS):
                    for k in range(k0, k1):
                        n = rows_of(k)
                        ins = pe.transpose(turned[b][0:n, (k - k0) * P:(k - k0 + 1) * P],
                                           att[:, k * P:k * P + n], g.ident[:, :])
                    ins.then_inc(turn_ready[b], 1)

            def values(t):
                i, s, u = t
                pe.wait_ge(copied_act, 2 * i + 2)
                pe.wait_ge(copied_dve, i + 1)
                pe.wait_ge(out_used, i)
                for k in range(NT):
                    n = rows_of(k)
                    ins = pe.matmul(out[:, 0:D], att_t[0:n, k, :], v[0:n, k, 0:D],
                                    start=(k == 0), stop=(k == NT - 1))
                ins.then_inc(out_ready, 1)

            def body(t, prev):
                score(t)
                if prev is not None:
                    values(prev)
                turn(t)

            values(tiles(pe, NT, body))

        def copy_group(copy, b, k0, k1, sem):
            full = k1 - (k1 == NT)
            src = turned[b][:, 0:(full - k0) * P].rearrange("p (k n) -> p k n", n=P)
            ins = copy(att_t[:, k0:full, :], src)
            if full < k1:
                ins = copy(att_t[0:TAIL, full, :], turned[b][0:TAIL, (full - k0) * P:(full - k0 + 1) * P])
            ins.then_inc(sem, 1)

        @block.scalar
        def _(act):
            def body(t, _):
                i, s, u = t
                act.wait_ge(neg_ready, i + 1)
                act.activation(att[:, :], scores[:, 0:N], ACT.Exp, bias=neg[:, :], scale=scale,
                               accum_out=total[:, :]).then_inc(exp_done, 1)
                for b in (0, 2):
                    k0, k1 = GROUPS[b]
                    act.wait_ge(turn_ready[b], i + 1)
                    copy_group(act.copy, b, k0, k1, copied_act)

            tiles(act, NT, body)

        @block.vector
        def _(dve):
            def result(t):
                i, s, u = t
                dve.wait_ge(out_ready, i + 1)
                into = res if layer == 0 else g.x
                dve.scalar_tensor_tensor(into[:, i, :], out[:, 0:D], 0.0, into[:, i, :],
                                         ALU.max, ALU.add).then_inc(out_used, 1)

            if layer == 1:
                dve.wait_ge(res_ready, 1)

            def body(t, prev):
                i, s, u = t
                dve.wait_ge(scores_ready, i + 1)
                dve.tensor_reduce(top[:, :], scores[:, 0:N], AX, ALU.max).then_inc(top_ready, 1)
                dve.wait_ge(top_ready, i + 1)
                dve.tensor_scalar(neg[:, :], top[:, :], -scale, None, ALU.mult).then_inc(neg_ready, 1)
                dve.wait_ge(exp_done, i + 1)
                dve.reciprocal(inv[:, :], total[:, :]).then_inc(inv_ready, 1)
                dve.wait_ge(inv_ready, i + 1)
                dve.wait_ge(adj_in[u], 16 * (s + 1))
                dve.scalar_tensor_tensor(att[:, :], att[:, :], inv[:, 0:1], adj[u][:, 0:N],
                                         ALU.mult, ALU.add).then_inc(att_ready, 1)
                dve.wait_ge(att_ready, i + 1)
                dve.sem_inc(adj_used[u], 1)
                if prev is not None:
                    result(prev)
                dve.wait_ge(turn_ready[1], i + 1)
                copy_group(dve.tensor_copy, 1, *GROUPS[1], copied_dve)

            result(tiles(dve, NT, body))


def norm_rows(dve, src, dst, stats, mv, rstd, root, sems):
    stats_done, root_asked, root_ready, rstd_step, rows_done = sems
    for i in range(NT):
        dve.bn_stats(stats[:, i, :], src[:, i, :]).then_inc(stats_done, 1)
    for i in range(NT):
        dve.wait_ge(stats_done, i + 1)
        dve.bn_aggr(mv[:, i, :], stats[:, i, :]).then_inc(stats_done, 1)
    dve.wait_ge(stats_done, 2 * NT)
    inverse_root(dve, rstd, mv[:, :, 1], root, root_asked, root_ready, rstd_step)
    for i in range(NT):
        dve.tensor_scalar(dst[:, i, :], src[:, i, :], mv[:, i, 0:1], rstd[:, i:i + 1],
                          ALU.subtract, ALU.mult).then_inc(rows_done, 1)
    dve.wait_ge(rows_done, NT)


def norm_memory(st):
    return (st.sb("stats", [P, NT, 6]), st.sb("mv", [P, NT, 2]), st.sb("rstd", [P, NT]), st.sb("root", [P, 3, NT]),
            [st.sem(x) for x in ("stats_done", "root_asked", "root_ready", "rstd_step", "rows_done")])


def over(ap, n):
    return ap.unsqueeze(2).to_broadcast([ap.shape[0], ap.shape[1], n])


def each(ap, n):
    return ap.unsqueeze(1).to_broadcast([ap.shape[0], n, ap.shape[1]])


def route_stage(nc, g, name, experts, slots, logits, xn, slot_rows, r, over_all):
    E = experts
    with Stage(nc, name) as st:
        best = st.sb("best", [P, NT, 8])
        at = st.sb("at", [P, NT, 8], U32)
        atf = st.sb("atf", [P, NT, 2])
        hot = [st.sb(f"hot{k}", [P, NT, E]) for k in range(2)]
        either = st.sb("either", [P, NT, E])
        pos = st.sb("pos", [P, NT, E])
        pick = [st.sb(f"pick{k}", [P, NT, E]) for k in range(2)]
        part = st.sb("part", [P, NT, E])
        base = st.sb("base", [P, NT + 1, E])
        cnt_i = st.sb("cnt_i", [P, E], I32)
        cnt, upto, first = (st.sb(x, [P, E]) for x in ("cnt", "upto", "first"))
        slot_f = st.sb("slot_f", [P, 2, NT])
        below = st.sb("below", [1, slots, E])
        own = st.sb("own", [1, slots])
        shifted = st.sb("shifted", [P, NT, E])
        gap, den = st.sb("gap", [P, NT]), st.sb("den", [P, NT])
        rank, total = st.banks("rank", 1), st.banks("total", 1)
        step, picked, counted, exp_asked, exp_done, slots_ready, sent = (
            st.sem(x) for x in ("step", "picked", "counted", "exp_asked", "exp_done", "slots_ready", "sent"))
        block = st.block()

        @block.vector
        def _(dve):
            done = [0]

            def then(ins):
                done[0] += 1
                ins.then_inc(step, 1)
                dve.wait_ge(step, done[0])

            for i in range(NT):
                done[0] += 1
                dve.max(best[:, i, :], logits[:, i, :]).then_inc(step, 1)
            for i in range(NT):
                dve.wait_ge(step, i + 1)
                done[0] += 1
                dve.max_index(at[:, i, :], best[:, i, :], logits[:, i, :]).then_inc(step, 1)
            dve.wait_ge(step, done[0])
            then(dve.tensor_copy(atf[:, :, :], at[:, :, 0:2]))
            then(dve.tensor_tensor(atf[:, :, :], atf[:, :, :], over(g.past_end[:, :], 2), ALU.add))
            for k in range(2):
                then(dve.tensor_tensor(hot[k][:, :, :], each(g.iota[:, 0:E], NT), over(atf[:, :, k], E),
                                       ALU.is_equal))
            dve.tensor_tensor(either[:, :, :], hot[0][:, :, :], hot[1][:, :, :], ALU.add).then_inc(picked, 1)
            dve.tensor_tensor(gap[:, :], best[:, :, 1], best[:, :, 0], ALU.subtract).then_inc(exp_asked, 1)
            if over_all:
                dve.tensor_tensor(shifted[:, :, :], logits[:, :, :], over(best[:, :, 0], E), ALU.subtract) \
                   .then_inc(exp_asked, 1)
            then(dve.memset(base[:, 0, :], 0.0))
            dve.wait_ge(counted, 1)
            for i in range(NT):
                then(dve.tensor_tensor(base[:, i + 1, :], base[:, i, :], total[:, i * E:(i + 1) * E], ALU.add))
            then(dve.tensor_scalar(cnt_i[:, :], base[:, NT, :], float(P - 1), None, ALU.add))
            then(dve.tensor_scalar(cnt_i[:, :], cnt_i[:, :], P.bit_length() - 1, None, ALU.arith_shift_right))
            then(dve.tensor_copy(cnt[:, :], cnt_i[:, :]))
            then(dve.tensor_tensor_scan(upto[:, :], g.ones[:, 0:E], cnt[:, :], 0.0, ALU.mult, ALU.add))
            then(dve.tensor_tensor(first[:, :], upto[:, :], cnt[:, :], ALU.subtract))
            then(dve.scalar_tensor_tensor(pos[:, :, :], each(first[:, :], NT), float(P), base[:, 0:NT, :],
                                          ALU.mult, ALU.add))
            then(dve.tensor_tensor(pos[:, :, :], pos[:, :, :],
                                   rank[:, 0:NT * E].rearrange("p (n e) -> p n e", e=E), ALU.add))
            for k in range(2):
                then(dve.tensor_tensor(pick[k][:, :, :], hot[k][:, :, :], pos[:, :, :], ALU.mult))
                then(dve.tensor_reduce(slot_f[:, k, :], pick[k][:, :, :], AX, ALU.add))
            dve.tensor_copy(r.slot[:, :, :], slot_f[:, :, :]).then_inc(slots_ready, 1)
            then(dve.tensor_tensor(below[:, :, :], each(upto[0:1, :], slots), over(g.iota[0:1, 0:slots], E), ALU.is_le))
            then(dve.tensor_reduce(own[:, :], below[:, :, :], AX, ALU.add))
            then(dve.tensor_scalar(r.expert[:, :], own[:, :], float(E - 1), None, ALU.min))
            dve.wait_ge(exp_done, 1 + over_all)
            if over_all:
                then(dve.tensor_reduce(den[:, :], shifted[:, :, :], AX, ALU.add))
            else:
                then(dve.tensor_scalar(den[:, :], gap[:, :], 1.0, None, ALU.add))
            then(dve.reciprocal(r.weight[:, 0, :], den[:, :]))
            then(dve.tensor_tensor(r.weight[:, 1, :], r.weight[:, 0, :], gap[:, :], ALU.mult))

        @block.scalar
        def _(act):
            act.wait_ge(exp_asked, 1 + over_all)
            act.activation(gap[:, :], gap[:, :], ACT.Exp).then_inc(exp_done, 1)
            if over_all:
                act.activation(shifted[:, :, :], shifted[:, :, :], ACT.Exp).then_inc(exp_done, 1)

        @block.tensor
        def _(pe):
            pe.wait_ge(picked, 1)
            flat = either[:, :, :].rearrange("p n e -> p (n e)")
            pe.matmul(rank[:, 0:NT * E], g.before[:, :], flat, start=True, stop=True)
            pe.matmul(total[:, 0:NT * E], g.ones[:, :], flat, start=True, stop=True).then_inc(counted, 1)

        @block.gpsimd
        def _(pool):
            pool.wait_ge(slots_ready, 1)
            for i in range(NT):
                n = rows_of(i)
                for k in range(2):
                    pool.indirect_dma_start(
                        out=slot_rows[:, :], out_offset=bass.IndirectOffsetOnAxis(ap=r.slot[0:n, k, i:i + 1], axis=0),
                        in_=xn[0:n, i, :], in_offset=None).then_inc(sent, 16)
            pool.wait_ge(sent, 32 * NT)


def expert_stage(nc, g, name, experts, hidden, gated, slots, slot_rows, slot_out, d_up, d_down, d_bias, r):
    H = hidden
    U = 2 * H if gated else H
    KH = H // P
    UP = [(a, min(BANK, U - a)) for a in range(0, U, BANK)]
    TURN = [(0, 4), (4, KH)]
    with Stage(nc, name) as st:
        up = [st.sb(f"up{u}", [P, DC, U]) for u in range(2)]
        down = [st.sb(f"down{u}", [P, KH, D]) for u in range(2)]
        bias = [st.sb(f"bias{u}", [1, U + D]) for u in range(2)] if d_bias is not None else None
        rows = [st.sb(f"rows{u}", [P, D]) for u in range(2)]
        rows_t = [st.sb(f"rows_t{u}", [P, DC, P]) for u in range(2)]
        half = st.sb("half", [P, H]) if gated else None
        h = st.sb("h", [P, H])
        h_t = st.sb("h_t", [P, KH, P])
        y = [st.sb(f"y{u}", [P, D]) for u in range(2)]
        pup = st.banks("pup", len(UP))
        pturn = [st.banks(f"pturn{b}", 1) for b in range(2)]
        prow, pout = st.banks("prow", 1), st.banks("pout", 1)
        up_in, down_in, rows_in, up_used, down_used, rows_used, y_stored = (st.sems(x) for x in (
            "up_in", "down_in", "rows_in", "up_used", "down_used", "rows_used", "y_stored"))
        rows_t_ready, half_ready, h_ready, turn0, turn1, copied0, copied1, out_ready, y_ready = (st.sem(x) for x in (
            "rows_t_ready", "half_ready", "h_ready", "turn0", "turn1", "copied0", "copied1", "out_ready", "y_ready"))
        block = st.block()
        up_parts = 2 if bias is not None else 1

        @block.sync
        def _(sp):
            def body(t, _):
                j, s, u = t
                e = sp.value_load(r.expert[0:1, bass.ds(j, 1)], min_val=0, max_val=experts - 1)
                sp.wait_ge(rows_used[u], s)
                sp.dma_start(rows[u][:, :], slot_rows.rearrange("(n p) d -> n p d", p=P)[bass.ds(j, 1), :, :]
                             .rearrange("a p d -> (a p) d")).then_inc(rows_in[u], 16)
                sp.wait_ge(up_used[u], s)
                sp.dma_start(up[u][:, :, :], d_up[bass.ds(e, 1), :, :, :].rearrange("a p c m -> (a p) c m")) \
                  .then_inc(up_in[u], 16)
                sp.wait_ge(down_used[u], s)
                if bias is not None:
                    sp.dma_start(bias[u][:, :], d_bias[bass.ds(e, 1), :]).then_inc(up_in[u], 16)
                sp.dma_start(down[u][:, :, :], d_down[bass.ds(e, 1), :, :, :].rearrange("a p c m -> (a p) c m")) \
                  .then_inc(down_in[u], 16)

            tiles(sp, slots, body)

        @block.tensor
        def _(pe):
            def turn_rows(t):
                j, s, u = t
                pe.wait_ge(rows_in[u], 16 * (s + 1))
                pe.wait_ge(rows_t_ready, j)
                for c in range(DC):
                    ins = pe.transpose(prow[:, c * P:(c + 1) * P], rows[u][:, c * P:(c + 1) * P], g.ident[:, :])
                ins.then_inc(rows_used[u], 1)

            def go_up(t):
                j, s, u = t
                pe.wait_ge(rows_t_ready, j + 1)
                pe.wait_ge(up_in[u], 16 * up_parts * (s + 1))
                pe.wait_ge(h_ready, j)
                for a, size in UP:
                    if bias is not None:
                        pe.matmul(pup[:, a:a + size], g.ones[0:1, :], bias[u][:, a:a + size], start=True, stop=False)
                    for c in range(DC):
                        ins = pe.matmul(pup[:, a:a + size], rows_t[u][:, c, :], up[u][:, c, a:a + size],
                                        start=(c == 0 and bias is None), stop=(c == DC - 1))
                ins.then_inc(up_used[u], 1)

            def turn_hidden(t):
                j, s, u = t
                pe.wait_ge(h_ready, j + 1)
                for b, (k0, k1) in enumerate(TURN):
                    pe.wait_ge((copied0, copied1)[b], j)
                    for k in range(k0, k1):
                        ins = pe.transpose(pturn[b][:, (k - k0) * P:(k - k0 + 1) * P], h[:, k * P:(k + 1) * P],
                                           g.ident[:, :])
                    ins.then_inc((turn0, turn1)[b], 1)

            def go_down(t):
                j, s, u = t
                pe.wait_ge(down_in[u], 16 * (s + 1))
                pe.wait_ge(y_ready, j)
                if bias is not None:
                    pe.matmul(pout[:, 0:D], g.ones[0:1, :], bias[u][:, U:U + D], start=True, stop=False)
                for k in range(KH):
                    if k in (0, 4):
                        pe.wait_ge((copied0, copied1)[k // 4], j + 1)
                    ins = pe.matmul(pout[:, 0:D], h_t[:, k, :], down[u][:, k, :],
                                    start=(k == 0 and bias is None), stop=(k == KH - 1))
                ins.then_inc(down_used[u], 1)

            def body(t, prev):
                if prev is None:
                    turn_rows(t)
                go_up(t)
                if prev is not None:
                    go_down(prev)
                j, s, u = t
                if not (isinstance(j, int) and j == slots - 1):
                    turn_rows((j + 1, s + u, 1 - u))
                turn_hidden(t)

            go_down(tiles(pe, slots, body))

        def wait_pe_pair(eng, sems, t):
            j, s, u = t
            eng.wait_ge(sems[u], s + 1)

        @block.scalar
        def _(act):
            def rows_out(t):
                j, s, u = t
                wait_pe_pair(act, rows_used, t)
                act.wait_ge(up_used[u], s)
                act.copy(rows_t[u][:, :, :], prow[:, 0:D].rearrange("p (c n) -> p c n", c=DC)) \
                   .then_inc(rows_t_ready, 1)

            def result_out(t):
                j, s, u = t
                wait_pe_pair(act, down_used, t)
                act.wait_ge(y_stored[u], 16 * s)
                act.copy(y[u][:, :], pout[:, 0:D]).then_inc(y_ready, 1)

            def body(t, prev):
                j, s, u = t
                if prev is None:
                    rows_out(t)
                wait_pe_pair(act, up_used, t)
                if gated:
                    act.activation(half[:, :], pup[:, 0:H], ACT.Silu).then_inc(half_ready, 1)
                else:
                    if prev is not None:
                        act.wait_ge(turn1, j)
                    act.activation(h[:, :], pup[:, 0:H], ACT.Relu).then_inc(h_ready, 1)
                if prev is not None:
                    result_out(prev)
                if not (isinstance(j, int) and j == slots - 1):
                    rows_out((j + 1, s + u, 1 - u))
                act.wait_ge(turn0, j + 1)
                act.copy(h_t[:, 0:4, :], pturn[0][:, :].rearrange("p (k n) -> p k n", n=P)).then_inc(copied0, 1)

            result_out(tiles(act, slots, body))

        @block.vector
        def _(dve):
            def body(t, prev):
                j, s, u = t
                if gated:
                    dve.wait_ge(half_ready, j + 1)
                    if prev is not None:
                        dve.wait_ge(turn1, j)
                    dve.tensor_tensor(h[:, :], half[:, :], pup[:, H:2 * H], ALU.mult).then_inc(h_ready, 1)
                dve.wait_ge(turn1, j + 1)
                dve.tensor_copy(h_t[:, 4:KH, :], pturn[1][:, 0:(KH - 4) * P].rearrange("p (k n) -> p k n", n=P)) \
                   .then_inc(copied1, 1)

            tiles(dve, slots, body)

        @block.gpsimd
        def _(pool):
            def body(t, _):
                j, s, u = t
                pool.wait_ge(y_ready, j + 1)
                pool.dma_start(slot_out.rearrange("(n p) d -> n p d", p=P)[bass.ds(j, 1), :, :]
                               .rearrange("a p d -> (a p) d"), y[u][:, :]).then_inc(y_stored[u], 16)

            tiles(pool, slots, body)
            pool.wait_ge(y_stored[0], 16 * (slots - slots // 2))
            pool.wait_ge(y_stored[1], 16 * (slots // 2))


def combine_stage(nc, g, name, slot_out, r, xn=None, d_gain=None, d_offset=None):
    with Stage(nc, name) as st:
        got = st.sb("got", [P, 2, NT, D])
        stats, mv, rstd, root, sems = norm_memory(st)
        gain, offset = (st.sb("gain", [P, D]), st.sb("offset", [P, D])) if xn is not None else (None, None)
        fetched = [st.sem(f"fetched{i}") for i in range(NT)]
        step, loaded = st.sem("step"), st.sem("loaded")
        block = st.block()
        into = xn if xn is not None else g.x

        @block.gpsimd
        def _(pool):
            for i in range(NT):
                for k in range(2):
                    pool.indirect_dma_start(
                        out=got[:, k, i, :], out_offset=None, in_=slot_out[:, :],
                        in_offset=bass.IndirectOffsetOnAxis(ap=r.slot[:, k, i:i + 1], axis=0)) \
                        .then_inc(fetched[i], 16)
            for i in range(NT):
                pool.wait_ge(fetched[i], 32)

        @block.sync
        def _(sp):
            if xn is not None:
                sp.dma_start(gain[:, :], d_gain.to_broadcast([P, D])).then_inc(loaded, 16)
                sp.dma_start(offset[:, :], d_offset.to_broadcast([P, D])).then_inc(loaded, 16)

        @block.scalar
        def _(act):
            if xn is not None:
                act.wait_ge(sems[1], 1)
                act.activation(root[:, 1, :], root[:, 0, :], ACT.Sqrt).then_inc(sems[2], 1)

        @block.vector
        def _(dve):
            for i in range(NT):
                dve.wait_ge(fetched[i], 32)
                for k in range(2):
                    dve.scalar_tensor_tensor(into[:, i, :], got[:, k, i, :], r.weight[:, k, i:i + 1], into[:, i, :],
                                             ALU.mult, ALU.add).then_inc(step, 1)
                    dve.wait_ge(step, 2 * i + k + 1)
            if xn is not None:
                out = got[:, 0, :, :]
                norm_rows(dve, xn, out, stats, mv, rstd, root, sems)
                dve.wait_ge(loaded, 32)
                n = 2 * NT
                for other, op in ((each(gain[:, :], NT), ALU.mult), (each(offset[:, :], NT), ALU.add)):
                    dve.tensor_tensor(out, out, other, op).then_inc(step, 1)
                    n += 1
                    dve.wait_ge(step, n)
                dve.tensor_tensor(g.x[:, :, :], g.x[:, :, :], out, ALU.add).then_inc(step, 1)
                dve.wait_ge(step, n + 1)


def spread_stage(nc, g, d, name, hidden, d_bias):
    with Stage(nc, name) as st:
        adj = [st.sb(f"adj{u}", [P, NT, P]) for u in range(2)]
        bias = st.sb("bias", [1, D])
        out = [st.banks(f"out{u}", 1) for u in range(2)]
        adj_in, out_ready, out_used = st.sems("adj_in"), st.sems("out_ready"), st.sems("out_used")
        bias_in = st.sem("bias_in")
        block = st.block()

        @block.sync
        def _(sp):
            sp.dma_start(bias[:, :], d_bias).then_inc(bias_in, 16)

            def body(t, _):
                i, s, u = t
                sp.wait_ge(out_ready[u], s)
                sp.dma_start(adj[u][:, :, :], d["adj_t"][bass.ds(i, 1), :, :, :].rearrange("a p k n -> (a p) k n")) \
                  .then_inc(adj_in[u], 16)

            tiles(sp, NT, body)

        @block.tensor
        def _(pe):
            pe.wait_ge(bias_in, 16)

            def body(t, _):
                i, s, u = t
                pe.wait_ge(adj_in[u], 16 * (s + 1))
                pe.wait_ge(out_used[u], s)
                pe.matmul(out[u][:, 0:D], g.ones[0:1, :], bias[:, :], start=True, stop=False)
                for k in range(NT):
                    n = rows_of(k)
                    ins = pe.matmul(out[u][:, 0:D], adj[u][0:n, k, :], hidden[0:n, k, :], start=False,
                                    stop=(k == NT - 1))
                ins.then_inc(out_ready[u], 1)

            tiles(pe, NT, body)

        @block.vector
        def _(dve):
            def body(t, _):
                i, s, u = t
                dve.wait_ge(out_ready[u], s + 1)
                dve.tensor_tensor(g.x[:, i, :], g.x[:, i, :], out[u][:, 0:D], ALU.add).then_inc(out_used[u], 1)

            tiles(dve, NT, body)


def shift_stage(nc, g, name):
    MARK, SHL, SHR, FIELDS, OUT = 0, 39, 40, 64, 128
    W = 16
    with Stage(nc, name) as st:
        y = st.sb("y", [P, NT, D])
        stats, mv, rstd, root, sems = norm_memory(st)
        fall = st.sb("fall", [P, 3, W])
        hot = st.sb("hot", [P, NT, 3, W])
        top = st.sb("top", [P, NT, 3])
        none = st.sb("none", [P, NT, 3])
        value = st.sb("value", [P, NT])
        value_i, by_i, left_i, right_i, low_i, high_i = (
            st.sb(x, [P, NT], I32) for x in ("value_i", "by_i", "left_i", "right_i", "low_i", "high_i"))
        left, right, mark, is_left, is_right, height = (
            st.sb(x, [P, NT]) for x in ("left", "right", "mark", "is_left", "is_right", "height"))
        nibble = st.sb("nibble", [P, 2, NT])
        spot = st.sb("spot", [P, NT, 2, W])
        step = st.sem("step")
        block = st.block()

        @block.scalar
        def _(act):
            act.wait_ge(sems[1], 1)
            act.activation(root[:, 1, :], root[:, 0, :], ACT.Sqrt).then_inc(sems[2], 1)

        @block.vector
        def _(dve):
            norm_rows(dve, g.x, y, stats, mv, rstd, root, sems)
            done = [0]

            def then(ins):
                done[0] += 1
                ins.then_inc(step, 1)
                dve.wait_ge(step, done[0])

            for f in range(3):
                then(dve.tensor_scalar(fall[:, f, :], g.iota[:, 0:W], -1.0, float(W), ALU.mult, ALU.add))
            then(dve.scalar_tensor_tensor(hot[:, :, :, :].rearrange("p n f w -> p n (f w)"),
                                          y[:, :, FIELDS:FIELDS + 3 * W], 0.5,
                                          each(fall[:, :, :].rearrange("p f w -> p (f w)"), NT), ALU.is_gt, ALU.mult))
            then(dve.tensor_reduce(top[:, :, :].rearrange("p n f -> p (n f)"),
                                   hot[:, :, :, :].rearrange("p n f w -> p (n f) w"), AX, ALU.max))
            then(dve.tensor_scalar(none[:, :, :], top[:, :, :], 0.0, float(W), ALU.is_equal, ALU.mult))
            then(dve.tensor_tensor(top[:, :, :], top[:, :, :], none[:, :, :], ALU.add))
            then(dve.tensor_scalar(top[:, :, :], top[:, :, :], -1.0, float(W), ALU.mult, ALU.add))
            then(dve.scalar_tensor_tensor(value[:, :], top[:, :, 1], float(W), top[:, :, 0], ALU.mult, ALU.add))
            then(dve.tensor_copy(value_i[:, :], value[:, :]))
            then(dve.tensor_copy(by_i[:, :], top[:, :, 2]))
            then(dve.tensor_tensor(left_i[:, :], value_i[:, :], by_i[:, :], ALU.logical_shift_left))
            then(dve.tensor_scalar(left_i[:, :], left_i[:, :], W * W - 1, None, ALU.bitwise_and))
            then(dve.tensor_tensor(right_i[:, :], value_i[:, :], by_i[:, :], ALU.logical_shift_right))
            then(dve.tensor_copy(left[:, :], left_i[:, :]))
            then(dve.tensor_copy(right[:, :], right_i[:, :]))
            then(dve.tensor_scalar(mark[:, :], y[:, :, MARK], 0.5, None, ALU.is_gt))
            then(dve.scalar_tensor_tensor(is_left[:, :], y[:, :, SHL], 0.5, mark[:, :], ALU.is_gt, ALU.mult))
            then(dve.scalar_tensor_tensor(is_right[:, :], y[:, :, SHR], 0.5, mark[:, :], ALU.is_gt, ALU.mult))
            then(dve.tensor_tensor(height[:, :], is_left[:, :], is_right[:, :], ALU.max))
            then(dve.tensor_tensor(is_right[:, :], height[:, :], is_left[:, :], ALU.subtract))
            then(dve.tensor_scalar(height[:, :], height[:, :], 2.0, None, ALU.mult))
            then(dve.tensor_tensor(left[:, :], left[:, :], is_left[:, :], ALU.mult))
            then(dve.tensor_tensor(right[:, :], right[:, :], is_right[:, :], ALU.mult))
            then(dve.tensor_tensor(value[:, :], left[:, :], right[:, :], ALU.add))
            then(dve.tensor_copy(value_i[:, :], value[:, :]))
            then(dve.tensor_scalar(low_i[:, :], value_i[:, :], W - 1, None, ALU.bitwise_and))
            then(dve.tensor_scalar(high_i[:, :], value_i[:, :], 4, None, ALU.logical_shift_right))
            then(dve.tensor_copy(nibble[:, 0, :], low_i[:, :]))
            then(dve.tensor_copy(nibble[:, 1, :], high_i[:, :]))
            for f in range(2):
                then(dve.tensor_tensor(spot[:, :, f, :], each(g.iota[:, 0:W], NT), over(nibble[:, f, :], W),
                                       ALU.is_equal))
                then(dve.tensor_tensor(spot[:, :, f, :], spot[:, :, f, :], over(height[:, :], W), ALU.mult))
            then(dve.tensor_tensor(g.x[:, :, :], g.x[:, :, :], y[:, :, :], ALU.add))
            field = g.x[:, :, OUT:OUT + 2 * W]
            then(dve.tensor_tensor(field, field, spot[:, :, :, :].rearrange("p n f w -> p n (f w)"), ALU.add))


def heads_stage(nc, g, d, name, qt, kt, v, d_wo):
    FV = HEADS * HD
    VC = FV // P
    SCALE = float(HD) ** -0.5
    with Stage(nc, name) as st:
        mask = [st.sb(f"mask{u}", [P, NP]) for u in range(2)]
        qs = [st.sb(f"qs{u}", [2 * HD, 2, VC, 2, P], F32R) for u in range(2)]
        wo = st.sb("wo", [P, VC, D])
        masked = st.sb("masked", [P, N])
        p = [st.sb(f"p{x}", [P, N]) for x in range(2)]
        att_t = [st.sb(f"att_t{x}", [P, NT, P]) for x in range(2)]
        o = [st.sb(f"o{u}", [P, FV]) for u in range(2)]
        o_t = st.sb("o_t", [P, VC, P])
        top, neg, total, inv = (st.sb(x, [P, 4]) for x in ("top", "neg", "total", "inv"))
        scores = st.banks("scores", 3)
        turned = [st.banks(f"turned{b}", 1) for b in range(3)]
        out, proj = st.banks("out", 1), st.banks("proj", 1)
        adj_in, mask_ready, mask_used, qs_ready = (st.sems(x) for x in ("adj_in", "mask_ready", "mask_used", "qs_ready"))
        eye_done, wo_in, split_step, scores_ready, masked_ready, neg_ready, exp_done, inv_ready, copied_act, \
            copied_dve, out_ready, out_used, o_turned, o_copied, proj_ready, proj_used = (st.sem(x) for x in (
                "eye_done", "wo_in", "split_step", "scores_ready", "masked_ready", "neg_ready", "exp_done",
                "inv_ready", "copied_act", "copied_dve", "out_ready", "out_used", "o_turned", "o_copied",
                "proj_ready", "proj_used"))
        turn_ready = [st.sem(f"turn_ready{b}") for b in range(3)]
        mask_begun, masked_begun, split_begun = (st.sem(x) for x in ("mask_begun", "masked_begun", "split_begun"))
        block = st.block()

        def lagged(body_head, body_tail):
            def body(t, prev):
                for h in range(HEADS):
                    one, two = ((t, h - n) if h >= n else (prev, h + HEADS - n) for n in (1, 2))
                    body_head((t, h), one if one[0] is not None else None, two if two[0] is not None else None)
                    if h in (2, 3) and prev is not None:
                        body_tail(prev, h)
            return body

        def finish(last, body_head, body_tail):
            body_head(None, (last, HEADS - 1), (last, HEADS - 2))
            body_head(None, None, (last, HEADS - 1))
            for h in (2, 3):
                body_tail(last, h)

        def number(t, h):
            return HEADS * t[0] + h

        @block.sync
        def _(sp):
            sp.dma_start(wo[:, :, :], d_wo).then_inc(wo_in, 16)

            def body(t, _):
                i, s, u = t
                sp.wait_ge(mask_used[u], s)
                sp.dma_start(mask[u][:, :], d["adj_rows"][bass.ds(i, 1), :, :].rearrange("a p n -> (a p) n")) \
                  .then_inc(adj_in[u], 16)

            tiles(sp, NT, body)

        @block.gpsimd
        def _(pool):
            def body(t, _):
                i, s, u = t
                if not (isinstance(i, int) and i < 2):
                    pool.wait_ge(scores_ready, HEADS * (i - 1))
                    pool.sem_inc(split_begun, 1)
                tile = bass.ts(i, P)
                for e in range(2):
                    own = slice(e * HD, (e + 1) * HD)
                    pool.tensor_copy(qs[u][own, 0, :, e, :], qt[own, :, tile]).then_inc(split_step, 1)
                pool.wait_ge(split_step, 8 * i + 2)
                pool.sem_inc(split_begun, 1)
                for e in range(2):
                    own = slice(e * HD, (e + 1) * HD)
                    pool.tensor_tensor(qs[u][own, 1, :, e, :], qt[own, :, tile], qs[u][own, 0, :, e, :].bitcast(F32),
                                       ALU.subtract).then_inc(split_step, 1)
                pool.wait_ge(split_step, 8 * i + 4)
                pool.sem_inc(split_begun, 1)
                for e in range(2):
                    own, other = slice(e * HD, (e + 1) * HD), slice((1 - e) * HD, (2 - e) * HD)
                    for part in range(2):
                        pool.tensor_copy(qs[u][other, part, :, e, :], qs[u][own, part, :, e, :].bitcast(F32)) \
                            .then_inc(split_step, 1)
                pool.wait_ge(split_step, 8 * i + 8)
                pool.sem_inc(qs_ready[u], 1)
                pool.wait_ge(eye_done, i + 1)
                pool.sem_inc(mask_begun, 1)
                pool.tensor_scalar(mask[u][:, :], mask[u][:, :], 1.0, MASK / SCALE, ALU.subtract, ALU.mult) \
                    .then_inc(mask_ready[u], 1)
                pool.wait_ge(mask_ready[u], s + 1)
                pool.sem_inc(split_begun, 1)

            tiles(pool, NT, body)

        @block.tensor
        def _(pe):
            pe.wait_ge(wo_in, 16)

            def score(t, h):
                i, s, u = t
                if h == 0:
                    pe.wait_ge(qs_ready[u], s + 1)
                pe.wait_ge(masked_ready, number(t, h))
                for part in range(2):
                    for a, size in COLS:
                        ins = pe.matmul(scores[:, a:a + size], qs[u][:, part, h // 2, h % 2, :], kt[:, h, a:a + size],
                                        start=(part == 0), stop=(part == 1))
                ins.then_inc(scores_ready, 1)

            def turn(t, h):
                n = number(t, h)
                pe.wait_ge(exp_done, n + 1)
                pe.wait_ge(copied_act, 2 * n)
                pe.wait_ge(copied_dve, n)
                for b, (k0, k1) in enumerate(GROUPS):
                    for k in range(k0, k1):
                        m = rows_of(k)
                        ins = pe.transpose(turned[b][0:m, (k - k0) * P:(k - k0 + 1) * P],
                                           p[h % 2][:, k * P:k * P + m], g.ident[:, :])
                    ins.then_inc(turn_ready[b], 1)

            def values(t, h):
                n = number(t, h)
                pe.wait_ge(out_used, n)
                pe.wait_ge(copied_dve, n + 1)
                pe.wait_ge(copied_act, 2 * n + 2)
                for k in range(NT):
                    m = rows_of(k)
                    ins = pe.matmul(out[:, 0:HD], att_t[h % 2][0:m, k, :], v[0:m, k, h * HD:(h + 1) * HD],
                                    start=(k == 0), stop=(k == NT - 1))
                ins.then_inc(out_ready, 1)

            def head(new, one, two):
                if new is not None:
                    score(*new)
                if one is not None:
                    turn(*one)
                if two is not None:
                    values(*two)

            def tail(t, h):
                i, s, u = t
                if h == 2:
                    pe.wait_ge(out_used, HEADS * i + HEADS)
                    pe.wait_ge(proj_used, i)
                    for c in range(VC):
                        ins = pe.transpose(proj[:, c * P:(c + 1) * P], o[u][:, c * P:(c + 1) * P], g.ident[:, :])
                    ins.then_inc(o_turned, 1)
                else:
                    pe.wait_ge(o_copied, i + 1)
                    for c in range(VC):
                        ins = pe.matmul(proj[:, 0:D], o_t[:, c, :], wo[:, c, :], start=(c == 0), stop=(c == VC - 1))
                    ins.then_inc(proj_ready, 1)

            last = tiles(pe, NT, lagged(head, tail))
            finish(last, head, tail)

        def copy_group(copy, x, b, sem):
            k0, k1 = GROUPS[b]
            full = k1 - (k1 == NT)
            ins = copy(att_t[x][:, k0:full, :], turned[b][:, 0:(full - k0) * P].rearrange("p (k n) -> p k n", n=P))
            if full < k1:
                ins = copy(att_t[x][0:TAIL, full, :], turned[b][0:TAIL, (full - k0) * P:(full - k0 + 1) * P])
            ins.then_inc(sem, 1)

        @block.scalar
        def _(act):
            def head(new, one, two):
                if one is not None:
                    n, h = number(*one), one[1]
                    for b in (0, 2):
                        act.wait_ge(turn_ready[b], n + 1)
                        copy_group(act.copy, h % 2, b, copied_act)
                if new is not None:
                    n, h = number(*new), new[1]
                    act.wait_ge(neg_ready, n + 1)
                    act.activation(p[h % 2][:, :], masked[:, :], ACT.Exp, bias=neg[:, h % 4:h % 4 + 1],
                                   accum_out=total[:, h % 4:h % 4 + 1]).then_inc(exp_done, 1)

            def tail(t, h):
                i, s, u = t
                if h == 2:
                    act.wait_ge(o_turned, i + 1)
                    act.copy(o_t[:, :, :], proj[:, :].rearrange("p (k n) -> p k n", n=P)).then_inc(o_copied, 1)

            last = tiles(act, NT, lagged(head, tail))
            finish(last, head, tail)

        @block.vector
        def _(dve):
            def set_diagonal(t):
                i, s, u = t
                dve.wait_ge(adj_in[u], 16 * (s + 1))
                own = mask[u][:, bass.ts(i, P)]
                dve.tensor_tensor(own, own, g.ident[:, :], ALU.max).then_inc(eye_done, 1)

            set_diagonal((0, 0, 0))

            def head(new, one, two):
                if new is not None:
                    t, h = new
                    i, s, u = t
                    m = number(t, h)
                    dve.wait_ge(scores_ready, m + 1)
                    if h == 0:
                        dve.wait_ge(mask_ready[u], s + 1)
                    dve.wait_ge(exp_done, m)
                    dve.sem_inc(masked_begun, 1)
                    dve.tensor_tensor_reduce(out=masked[:, :], in0=scores[:, 0:N], in1=mask[u][:, 0:N],
                                             scale=SCALE, scalar=-3.0e38, op0=ALU.add, op1=ALU.max,
                                             accum_out=top[:, h % 4:h % 4 + 1]).then_inc(masked_ready, 1)
                    dve.wait_ge(masked_ready, m + 1)
                    dve.tensor_scalar(neg[:, h % 4:h % 4 + 1], top[:, h % 4:h % 4 + 1], -1.0, None, ALU.mult) \
                       .then_inc(neg_ready, 1)
                    if h == HEADS - 1:
                        dve.sem_inc(mask_used[u], 1)
                    if h == HEADS - 3 and not (isinstance(i, int) and i == NT - 1):
                        set_diagonal((i + 1, s + u, 1 - u))
                if one is not None:
                    dve.wait_ge(turn_ready[1], number(*one) + 1)
                    copy_group(dve.tensor_copy, one[1] % 2, 1, copied_dve)
                if two is not None:
                    n, h = number(*two), two[1]
                    dve.reciprocal(inv[:, h % 4:h % 4 + 1], total[:, h % 4:h % 4 + 1]).then_inc(inv_ready, 1)
                    dve.wait_ge(inv_ready, n + 1)
                    dve.wait_ge(out_ready, n + 1)
                    dve.tensor_scalar(o[two[0][2]][:, h * HD:(h + 1) * HD], out[:, 0:HD], inv[:, h % 4:h % 4 + 1],
                                      None, ALU.mult).then_inc(out_used, 1)

            def tail(t, h):
                i, s, u = t
                if h == 3:
                    dve.wait_ge(proj_ready, i + 1)
                    dve.tensor_tensor(g.x[:, i, :], g.x[:, i, :], proj[:, 0:D], ALU.add).then_inc(proj_used, 1)

            last = tiles(dve, NT, lagged(head, tail))
            finish(last, head, tail)


def gate_stage(nc, g, d, name, hg, ex, ht):
    with Stage(nc, name) as st:
        adj = [st.sb(f"adj{u}", [P, NT, P]) for u in range(2)]
        e = [st.sb(f"e{u}", [P, NT, P]) for u in range(2)]
        z = st.sb("z", [P, NT, P])
        a_left = st.sb("a_left", [P, DC, P])
        a_right = st.sb("a_right", [P, D])
        bias = st.sb("bias", [1, D + 2])
        gate_bias = st.sb("gate_bias", [P, 2])
        left = st.sb("left", [P, NP])
        right = st.sb("right", [P, NT])
        junk = st.sb("junk", [P, D])
        xa = st.sb("xa", [P, NT, D])
        xb = st.sb("xb", [P, NT, D + 2])
        den = [st.sb(f"den{u}", [P, 1]) for u in range(2)]
        inv = [st.sb(f"inv{u}", [P, 1]) for u in range(2)]
        gate = st.sb("gate", [P, 2, NT])
        pleft = st.banks("pleft", 3)
        pa = [st.banks(f"pa{u}", 1) for u in range(2)]
        pb = [st.banks(f"pb{u}", 1) for u in range(2)]
        adj_in, e_ready, xa_ready, xb_ready, xa_used, xb_used = (st.sems(x) for x in (
            "adj_in", "e_ready", "xa_ready", "xb_ready", "xa_used", "xb_used"))
        loaded, left_ready, left_copied, right_ready, z_step, exp_done, den_step, gate_asked, gate_done, mixed, \
            sig_done = (st.sem(x) for x in (
                "loaded", "left_ready", "left_copied", "right_ready", "z_step", "exp_done", "den_step",
                "gate_asked", "gate_done", "mixed", "sig_done"))
        block = st.block()

        @block.sync
        def _(sp):
            sp.dma_start(a_left[:, :, :], d["a_left"]).then_inc(loaded, 16)
            sp.dma_start(a_right[:, :], d["a_right"].to_broadcast([P, D])).then_inc(loaded, 16)
            sp.dma_start(bias[:, :], d["b_gcnb"]).then_inc(loaded, 16)
            sp.dma_start(gate_bias[:, :], d["b_gates"].to_broadcast([P, 2])).then_inc(loaded, 16)

            def body(t, _):
                i, s, u = t
                sp.wait_ge(xb_ready[u], s)
                sp.wait_ge(e_ready[u], s)
                sp.dma_start(adj[u][:, :, :], d["adj_t"][bass.ds(i, 1), :, :, :].rearrange("a p k n -> (a p) k n")) \
                  .then_inc(adj_in[u], 16)

            tiles(sp, NT, body)

        @block.tensor
        def _(pe):
            pe.wait_ge(loaded, 64)
            for a in range(0, NP, BANK):
                size = min(BANK, NP - a)
                for c in range(DC):
                    ins = pe.matmul(pleft[:, a:a + size], a_left[:, c, :], ht[:, c, a:a + size],
                                    start=(c == 0), stop=(c == DC - 1))
            ins.then_inc(left_ready, 1)

            def body(t, _):
                i, s, u = t
                pe.wait_ge(adj_in[u], 16 * (s + 1))
                pe.wait_ge(xb_used[u], s)
                pe.matmul(pb[u][:, 0:D + 2], g.ones[0:1, :], bias[:, :], start=True, stop=False)
                for k in range(NT):
                    n = rows_of(k)
                    ins = pe.matmul(pb[u][:, 0:D + 2], adj[u][0:n, k, :], hg[0:n, k, 1 + D:2 * D + 3], start=False,
                                    stop=(k == NT - 1))
                ins.then_inc(xb_ready[u], 1)
                pe.wait_ge(e_ready[u], s + 1)
                pe.wait_ge(xa_used[u], s)
                for k in range(NT):
                    n = rows_of(k)
                    ins = pe.matmul(pa[u][:, 0:D + 1], e[u][0:n, k, :], hg[0:n, k, 0:D + 1],
                                    start=(k == 0), stop=(k == NT - 1))
                ins.then_inc(xa_ready[u], 1)

            tiles(pe, NT, body)

        @block.scalar
        def _(act):
            act.wait_ge(left_ready, 1)
            act.copy(left[:, :], pleft[:, 0:NP]).then_inc(left_copied, 1)

            def xb_out(t):
                i, s, u = t
                act.wait_ge(xb_ready[u], s + 1)
                act.copy(xb[:, i, :], pb[u][:, 0:D + 2]).then_inc(xb_used[u], 1)

            def body(t, prev):
                i, s, u = t
                act.wait_ge(z_step, 2 * i + 2)
                act.wait_ge(xa_ready[u], s)
                act.activation(e[u][:, :, :], z[:, :, :], ACT.Exp, scale=-1.0).then_inc(exp_done, 1)
                if prev is not None:
                    xb_out(prev)

            xb_out(tiles(act, NT, body))
            act.wait_ge(gate_asked, 2)
            act.activation(gate[:, :, :], gate[:, :, :], ACT.Sigmoid).then_inc(gate_done, 1)
            act.wait_ge(mixed, 2 * NT)
            act.activation(xa[:, :, :], xa[:, :, :], ACT.Sigmoid).then_inc(sig_done, 1)

        @block.vector
        def _(dve):
            dve.wait_ge(loaded, 64)
            for i in range(NT):
                if i:
                    dve.wait_ge(right_ready, i)
                dve.tensor_tensor_reduce(out=junk[:, :], in0=hg[:, i, 1:D + 1], in1=a_right[:, :], scale=1.0,
                                         scalar=0.0, op0=ALU.mult, op1=ALU.add, accum_out=right[:, i:i + 1]) \
                   .then_inc(right_ready, 1)
            dve.wait_ge(right_ready, NT)
            dve.wait_ge(left_copied, 1)

            def xa_out(t):
                i, s, u = t
                dve.wait_ge(xa_ready[u], s + 1)
                dve.tensor_scalar(den[u][:, :], pa[u][:, 0:1], 1e-5, None, ALU.add).then_inc(den_step, 1)
                dve.wait_ge(den_step, 2 * i + 1)
                dve.reciprocal(inv[u][:, :], den[u][:, :]).then_inc(den_step, 1)
                dve.wait_ge(den_step, 2 * i + 2)
                dve.tensor_scalar(xa[:, i, :], pa[u][:, 1:D + 1], inv[u][:, 0:1], None, ALU.mult) \
                   .then_inc(xa_used[u], 1)

            def body(t, prev):
                i, s, u = t
                dve.wait_ge(exp_done, i)
                dve.tensor_tensor(z[:, :, :], each(left[:, bass.ts(i, P)], NT), over(right[:, :], P), ALU.add) \
                   .then_inc(z_step, 1)
                dve.wait_ge(z_step, 2 * i + 1)
                dve.scalar_tensor_tensor(z[:, :, :], z[:, :, :], 0.01, z[:, :, :], ALU.mult, ALU.max) \
                   .then_inc(z_step, 1)
                if prev is not None:
                    xa_out(prev)
                dve.wait_ge(adj_in[u], 16 * (s + 1))
                dve.wait_ge(exp_done, i + 1)
                dve.scalar_tensor_tensor(e[u][:, :, :], adj[u][:, :, :], 0.0, e[u][:, :, :], ALU.not_equal, ALU.mult) \
                   .then_inc(e_ready[u], 1)

            xa_out(tiles(dve, NT, body))
            dve.wait_ge(xb_used[0], NT - NT // 2)
            dve.wait_ge(xb_used[1], NT // 2)
            dve.wait_ge(xa_used[0], NT - NT // 2)
            dve.wait_ge(xa_used[1], NT // 2)
            for k in range(2):
                dve.scalar_tensor_tensor(gate[:, k, :], xb[:, :, D + k], gate_bias[:, k:k + 1], ex[:, :, 2 + k],
                                         ALU.add, ALU.add).then_inc(gate_asked, 1)
            dve.wait_ge(gate_done, 1)
            for i in range(NT):
                dve.tensor_scalar(xa[:, i, :], xa[:, i, :], gate[:, 0, i:i + 1], None, ALU.mult).then_inc(mixed, 1)
            for i in range(NT):
                dve.wait_ge(mixed, NT + i)
                dve.scalar_tensor_tensor(xa[:, i, :], xb[:, i, 0:D], gate[:, 1, i:i + 1], xa[:, i, :],
                                         ALU.mult, ALU.add).then_inc(mixed, 1)
            dve.wait_ge(sig_done, 1)
            dve.tensor_tensor(g.x[:, :, :], g.x[:, :, :], xa[:, :, :], ALU.add).then_inc(mixed, 1)
            dve.wait_ge(mixed, 2 * NT + 1)


def build(nc, d, out):
    with ExitStack() as ctx:
        def sb(name, shape, dt=F32):
            return ctx.enter_context(nc.sbuf_tensor(name, shape, dt))

        g = Shared(x=sb("x", [P, NT, D]), ident=sb("ident", [P, P]), ones=sb("ones", [P, P]),
                  before=sb("before", [P, P]), iota=sb("iota", [P, IOTA]),
                  past_end=sb("past_end", [P, NT]))
        start_stage(nc, g, d)
        with ExitStack() as layer:
            def lsb(name, shape):
                return layer.enter_context(nc.sbuf_tensor(name, shape, F32))

            vr = lsb("vr", [P, NT, 2 * D])
            xt = lsb("xt", [P, DC, NP])
            qt, kt = lsb("qt", [P, DC, NP]), lsb("kt", [P, DC, N])
            v1 = lsb("v1", [P, NT, D])
            project_stage(nc, g, "proj0", g.x, True, d["w_vr0"], 2 * D, vr, d_bias=d["b_vr0"], xt=xt,
                          d_cols=(d["w_qk0"], d["b_qk0"]), cols=[(qt, NP, True, False), (kt, N, True, False)])
            hidden = vr[:, :, D:2 * D]
            attention_stage(nc, g, d, "att0", qt, kt, vr, hidden, 0)
            project_stage(nc, g, "proj1", hidden, False, d["w_v1"], D, v1, d_bias=d["b_v1"], xt=xt,
                          d_cols=(d["w_qk1"], d["b_qk1"]), cols=[(qt, NP, True, False), (kt, N, True, False)])
            attention_stage(nc, g, d, "att1", qt, kt, v1, hidden, 1)
        rest(nc, g, d)
        with Stage(nc, "end") as st:
            stored = st.sem("stored")
            block = st.block()

            @block.sync
            def _(sp):
                full = (NT - 1) * P
                sp.dma_start(out[0:full, :].rearrange("(n p) d -> p n d", p=P), g.x[:, 0:NT - 1, :]) \
                  .then_inc(stored, 16)
                sp.dma_start(out[full:N, :], g.x[0:TAIL, NT - 1, :]).then_inc(stored, 16)
                sp.wait_ge(stored, 32)


def mixture(nc, g, d, n, gated, over_all):
    E, H, S = EXPERTS[n], HIDDEN[n], SLOTS[n]
    with ExitStack() as part:
        def psb(name, shape, dt=F32):
            return part.enter_context(nc.sbuf_tensor(f"mix{n}_{name}", shape, dt))

        xn = psb("xn", [P, NT, D])
        logits = psb("logits", [P, NT, E])
        r = Routing(psb("slot", [P, 2, NT], U32), psb("weight", [P, 2, NT]), psb("expert", [1, S], I32))
        project_stage(nc, g, f"gate{n}", g.x, True, d[f"w_gate{n}"], E, logits,
                      d_bias=d.get(f"b_gate{n}"), xn=xn)
        route_stage(nc, g, f"route{n}", E, S, logits, xn, d["slot_rows"][n], r, over_all)
        expert_stage(nc, g, f"expert{n}", E, H, gated, S, d["slot_rows"][n], d["slot_out"][n], d[f"w_up{n}"],
                     d[f"w_down{n}"], d.get(f"b_up_down{n}"), r)
        if n == 0:
            combine_stage(nc, g, f"combine{n}", d["slot_out"][n], r, xn, d["gamma"], d["beta"])
        else:
            combine_stage(nc, g, f"combine{n}", d["slot_out"][n], r)


def rest(nc, g, d):
    mixture(nc, g, d, 0, False, 1)
    with ExitStack() as part:
        hidden = part.enter_context(nc.sbuf_tensor("hidden1", [P, NT, D], F32))
        project_stage(nc, g, "proj2", g.x, True, d["w_spread"], D, hidden)
        spread_stage(nc, g, d, "spread", hidden, d["b_spread"])
    shift_stage(nc, g, "shift")
    with ExitStack() as part:
        def psb(name, shape, dt=F32):
            return part.enter_context(nc.sbuf_tensor(f"heads_{name}", shape, dt))

        FV = HEADS * HD
        v = psb("v", [P, NT, FV])
        qt, kt = psb("qt", [P, FV // P, NP]), psb("kt", [2 * HD, HEADS, N], F32R)
        with ExitStack() as inner:
            xt = inner.enter_context(nc.sbuf_tensor("heads_xt", [P, DC, NP], F32))
            project_stage(nc, g, "proj3", g.x, True, d["w_v2"], FV, v, xt=xt, d_cols=(d["w_qk2"], None),
                          cols=[(qt, NP, None, False), (kt, N, None, True)])
        heads_stage(nc, g, d, "heads", qt, kt, v, d["w_o2"])
    mixture(nc, g, d, 1, True, 0)
    with ExitStack() as part:
        def psb(name, shape):
            return part.enter_context(nc.sbuf_tensor(f"gat_{name}", shape, F32))

        hg = psb("hg", [P, NT, 2 * D + 3])
        ex = psb("ex", [P, NT, 4])
        ht = psb("ht", [P, DC, NP])
        with ExitStack() as inner:
            xt = inner.enter_context(nc.sbuf_tensor("gat_xt", [P, DC, NP], F32))
            project_stage(nc, g, "proj4", g.x, True, d["w_hg"], 2 * D, hg[:, :, 1:2 * D + 1], xt=xt,
                          d_extra=d["w_gates"], extra=ex, d_cols=(d["w_sa"], None), cols=[(ht, NP, None, False)])
        with Stage(nc, "ends") as st:
            set_ = st.sem("set")
            block = st.block()

            @block.vector
            def _(dve):
                dve.memset(hg[:, :, 0:1], 1.0).then_inc(set_, 1)
                dve.tensor_copy(hg[:, :, 2 * D + 1:2 * D + 3], ex[:, :, 0:2]).then_inc(set_, 1)
        gate_stage(nc, g, d, "gat", hg, ex, ht)
    mixture(nc, g, d, 2, True, 0)




def layouts(np, a):
    def rows(w):
        return np.ascontiguousarray(w.reshape(-1, P, w.shape[1]).transpose(1, 0, 2))

    def cols(*bs):
        return np.ascontiguousarray(np.concatenate(bs).reshape(-1, P).T)

    f32 = np.float32
    x = np.zeros((NP, D), f32)
    x[:N] = a["x"]
    adj = np.zeros((NP, NP), f32)
    adj[:N, :N] = a["adj"]
    arrays = {
        "x": rows(x),
        "adj_rows": adj.reshape(NT, P, NP),
        "w_vr0": rows(np.concatenate([a["L0_gnn_wv0"].T, a["L0_gnn_wres"].T], 1)),
        "b_vr0": np.concatenate([a["L0_gnn_bv0"], a["L0_gnn_bres"]])[None],
        "w_qk0": rows(np.concatenate([a["L0_gnn_wq0"].T, a["L0_gnn_wk0"].T], 1)),
        "b_qk0": cols(a["L0_gnn_bq0"], a["L0_gnn_bk0"]),
        "w_v1": rows(a["L0_gnn_wv1"].T),
        "b_v1": a["L0_gnn_bv1"][None],
        "w_qk1": rows(np.concatenate([a["L0_gnn_wq1"].T, a["L0_gnn_wk1"].T], 1)),
        "b_qk1": cols(a["L0_gnn_bq1"], a["L0_gnn_bk1"]),
    }
    arrays["adj_t"] = adj.reshape(NT, P, NT, P).transpose(0, 3, 2, 1)

    def tiled(w):
        return w.reshape(w.shape[0], -1, P, w.shape[2]).transpose(0, 2, 1, 3)

    arrays.update(
        w_gate0=rows(a["L0_ffn_Wg"]), b_gate0=a["L0_ffn_bg"][None],
        w_up0=tiled(a["L0_ffn_W1"]), w_down0=tiled(a["L0_ffn_W2"]),
        b_up_down0=np.concatenate([a["L0_ffn_b1"], a["L0_ffn_b2"]], 1),
        gamma=a["L0_ffn_gamma"][None], beta=a["L0_ffn_beta"][None],
        w_spread=rows(a["L1_gnn_W"].transpose(1, 0, 2).reshape(D, D)), b_spread=a["L1_gnn_b"].reshape(1, D),
        w_v2=rows(a["L2_gnn_Wvs"].transpose(1, 0, 2).reshape(D, HEADS * HD)),
        w_qk2=rows(np.concatenate([a[f"L2_gnn_{w}"].transpose(1, 0, 2).reshape(D, HEADS * HD) for w in ("Wqs", "Wks")], 1)),
        w_o2=rows(a["L2_gnn_Wo"].reshape(HEADS * HD, D)),
        w_gate1=rows(a["L2_ffn_gate_w"]),
        w_up1=tiled(np.concatenate([a["L2_ffn_W1"], a["L2_ffn_W3"]], 2)), w_down1=tiled(a["L2_ffn_W2"]),
        w_hg=rows(np.concatenate([a["L3_gnn_W_sa"], a["L3_gnn_W_gcnb"]], 1)),
        w_sa=rows(a["L3_gnn_W_sa"]),
        w_gates=rows(np.concatenate([a["L3_gnn_Wa"].reshape(2, D), a["L3_gnn_Wb"].reshape(2, D)])[[0, 2, 1, 3]].T),
        a_left=rows(np.repeat(a["L3_gnn_a_sa"][0, :D, None], P, 1)),
        a_right=a["L3_gnn_a_sa"][:, D:],
        b_gcnb=np.concatenate([a["L3_gnn_b_gcnb"], np.zeros(2, f32)])[None],
        b_gates=np.concatenate([a["L3_gnn_ba"], a["L3_gnn_bb"]])[None],
        w_gate2=rows(a["L3_ffn_gate_w"].T),
        w_up2=tiled(np.concatenate([a["L3_ffn_w1"].transpose(0, 2, 1), a["L3_ffn_w3"].transpose(0, 2, 1)], 2)),
        w_down2=tiled(a["L3_ffn_w2"].transpose(0, 2, 1)),
    )
    return arrays


def kernel(**inputs):
    import numpy as np
    import concourse.bacc as bacc
    from concourse.bass_utils import run_bass_kernel_spmd

    nc = bacc.Bacc("TRN2", target_bir_lowering=False, num_devices=1)
    arrays = {k: np.ascontiguousarray(v) for k, v in
              layouts(np, {k: np.asarray(v) for k, v in inputs.items()}).items()}
    d = {k: nc.dram_tensor(f"in_{k}", v.shape, mybir.dt.from_np(v.dtype), kind="ExternalInput").ap()
         for k, v in arrays.items()}
    d["slot_rows"] = [nc.dram_tensor(f"slot_rows{n}", (s * P, D), F32, kind="Internal").ap() for n, s in enumerate(SLOTS)]
    d["slot_out"] = [nc.dram_tensor(f"slot_out{n}", (s * P, D), F32, kind="Internal").ap() for n, s in enumerate(SLOTS)]
    out = nc.dram_tensor("out", (N, D), F32, kind="ExternalOutput").ap()
    build(nc, d, out)
    return run_bass_kernel_spmd(nc, [{f"in_{k}": v for k, v in arrays.items()}], core_ids=[0]).results[0]["out"]
```

```python
from contextlib import ExitStack

import concourse.bass as bass
from concourse import mybir

F32 = mybir.dt.float32
F32R = mybir.dt.float32r
I32 = mybir.dt.int32
U32 = mybir.dt.uint32
ALU = mybir.AluOpType
ACT = mybir.ActivationFunctionType
AX = mybir.AxisListType.X

P = 128
N = 1354
NT = -(-N // P)
TAIL = N - (NT - 1) * P
NP = NT * P
D = 256
DC = D // P
BANK = 512
EPS = 1e-5
COLS = [(0, BANK), (BANK, BANK), (2 * BANK, N - 2 * BANK)]
GROUPS = [(0, 4), (4, 8), (8, NT)]
HEADS, HD = 8, 64
MASK = 1e16
IOTA = 48
EXPERTS = (16, 8, 8)
HIDDEN = (1024, 1024, 768)
SLOTS = [2 * N // P + e for e in EXPERTS]


def rows_of(k):
    return TAIL if k == NT - 1 else P


def tiles(eng, count, body):
    last = (count - 1) // 2
    body((0, 0, 0), None)
    body((1, 0, 1), (0, 0, 0))
    body((2, 1, 0), (1, 0, 1))
    with eng.Fori(1, last - 1) as s:
        body((2 * s + 1, s, 1), (2 * s, s, 0))
        body((2 * s + 2, s + 1, 0), (2 * s + 1, s, 1))
    body((2 * last - 1, last - 1, 1), (2 * last - 2, last - 1, 0))
    body((2 * last, last, 0), (2 * last - 1, last - 1, 1))
    return 2 * last, last, 0


def parts_product(pe, out, left, right, start, stop):
    (lh, ll), (rh, rl) = left, right
    pe.matmul(out, lh, rh, start=start, stop=False)
    pe.matmul(out, lh, rl, start=False, stop=False)
    return pe.matmul(out, ll, rh, start=False, stop=stop)


class Shared:

    def __init__(self, x, ident, ones, zeros, before, iota, past_end, cleared):
        self.x, self.ident, self.ones, self.zeros = x, ident, ones, zeros
        self.before, self.iota, self.past_end, self.cleared = before, iota, past_end, cleared


class Routing:

    def __init__(self, slot, weight, expert, side, upto):
        self.slot, self.weight, self.expert, self.side, self.upto = slot, weight, expert, side, upto


class Weights:

    def __init__(self, nc, part, name, hidden, d_up, d_down, d_bias):
        self.d_up, self.d_down, self.d_bias = d_up, d_down, d_bias
        self.down_cols = hidden // P * D
        self.parts = 1 if d_bias is None else 2
        self.up = part.enter_context(nc.sbuf_tensor(f"{name}_up", [P, 2, d_up.shape[2]], F32))
        self.down = part.enter_context(nc.sbuf_tensor(f"{name}_down", [P, 2, self.down_cols + D * (self.parts - 1)], F32))
        self.up_in, self.down_in = (nc.alloc_semaphore(f"{name}_{x}") for x in ("up_in", "down_in"))

    def load_up(self, sp, e, u):
        sp.dma_start(self.up[:, u, :], self.d_up[bass.ds(e, 1), :, :].rearrange("a p m -> (a p) m")) \
          .then_inc(self.up_in, 16)

    def load_down(self, sp, e, u):
        n = self.down_cols
        sp.dma_start(self.down[:, u, 0:n], self.d_down[bass.ds(e, 1), :, :].rearrange("a p m -> (a p) m")) \
          .then_inc(self.down_in, 16)
        if self.d_bias is not None:
            sp.dma_start(self.down[:, u, n:n + D], self.d_bias[bass.ds(e, 1), :].to_broadcast([P, D])) \
              .then_inc(self.down_in, 16)


class Stage:

    def __init__(self, nc, name):
        self.nc, self.name = nc, name

    def __enter__(self):
        self.ctx, self.taken = ExitStack(), []
        return self

    def __exit__(self, *a):
        self.ctx.close()
        self.nc.clear_and_free_semaphores(self.taken)
        self.nc.all_engine_barrier()

    def sb(self, name, shape, dt=F32):
        return self.ctx.enter_context(self.nc.sbuf_tensor(f"{self.name}_{name}", shape, dt))

    def banks(self, name, n):
        return self.ctx.enter_context(self.nc.psum_tensor(f"{self.name}_{name}", [P, n * BANK], F32))

    def sem(self, name):
        self.taken.append(self.nc.alloc_semaphore(f"{self.name}_{name}"))
        return self.taken[-1]

    def sems(self, name):
        return [self.sem(f"{name}{u}") for u in range(2)]

    def block(self):
        return self.ctx.enter_context(self.nc.Block())


def start_stage(nc, g, d):
    with Stage(nc, "start") as st:
        rows_i = st.sb("rows_i", [P, IOTA], I32)
        loaded, made, filled = (st.sem(x) for x in ("loaded", "made", "filled"))
        block = st.block()

        @block.sync
        def _(sp):
            sp.dma_start(g.x[:, :, :], d["x"]).then_inc(loaded, 16)
            sp.wait_ge(loaded, 16)

        @block.gpsimd
        def _(pool):
            pool.iota(rows_i[:, :], pattern=[[1, IOTA]], base=0, channel_multiplier=0).then_inc(filled, 1)
            pool.memset(g.ident[:, :], 0.0).then_inc(filled, 1)
            pool.memset(g.before[:, :], 1.0).then_inc(filled, 1)
            pool.memset(g.past_end[:, :], 0.0).then_inc(filled, 1)
            pool.wait_ge(filled, 4)
            pool.affine_select(out=g.past_end[:, NT - 1:NT], in_=g.past_end[:, NT - 1:NT], compare_op=ALU.is_gt,
                               fill=100.0, base=TAIL, pattern=[[0, 1]], channel_multiplier=-1).then_inc(filled, 1)
            pool.tensor_copy(g.iota[:, :], rows_i[:, :]).then_inc(filled, 1)
            pool.affine_select(out=g.ident[:, :], in_=g.ident[:, :], compare_op=ALU.not_equal, fill=1.0,
                               base=0, pattern=[[-1, P]], channel_multiplier=1).then_inc(filled, 1)
            pool.affine_select(out=g.before[:, :], in_=g.before[:, :], compare_op=ALU.is_gt, fill=0.0,
                               base=0, pattern=[[1, P]], channel_multiplier=-1).then_inc(filled, 1)
            pool.wait_ge(filled, 8)

        @block.vector
        def _(dve):
            dve.memset(g.zeros[:, :], 0.0).then_inc(made, 1)
            dve.memset(g.ones[:, :], 1.0).then_inc(made, 1)
            dve.wait_ge(made, 2)


def inverse_root(dve, rstd, variance, root, asked, ready, step):
    v, half, sq = root[:, 0, :], root[:, 1, :], root[:, 2, :]
    dve.tensor_scalar(v, variance, EPS, None, ALU.add).then_inc(asked, 1)
    dve.wait_ge(ready, 1)
    dve.reciprocal(half, half).then_inc(step, 1)
    dve.wait_ge(step, 1)
    dve.tensor_tensor(sq, half, half, ALU.mult).then_inc(step, 1)
    dve.wait_ge(step, 2)
    dve.tensor_tensor(sq, sq, v, ALU.mult).then_inc(step, 1)
    dve.wait_ge(step, 3)
    dve.tensor_scalar(sq, sq, -0.5, 1.5, ALU.mult, ALU.add).then_inc(step, 1)
    dve.wait_ge(step, 4)
    dve.tensor_tensor(rstd[:, :], half, sq, ALU.mult).then_inc(step, 1)
    dve.wait_ge(step, 5)


def project_stage(nc, g, name, src, normalise, d_w, width, dest, d_bias=None, xn=None, xt=None,
                  d_extra=None, extra=None, d_cols=None, cols=()):
    with Stage(nc, name) as st:
        w = st.sb("w", [P, DC, width])
        bias = st.sb("bias", [P, width]) if d_bias is not None else None
        wx = st.sb("wx", [P, DC, extra.shape[2]]) if extra is not None else None
        wc = st.sb("wc", [P, DC, d_cols[0].shape[2]]) if d_cols else None
        bc = st.sb("bc", [P, d_cols[1].shape[1]]) if d_cols and d_cols[1] is not None else None
        stats = st.sb("stats", [P, NT, 6])
        mv = st.sb("mv", [P, NT, 2])
        rstd = st.sb("rstd", [P, NT])
        xb = [st.sb(f"xb{u}", [P, D]) for u in range(2)]
        xtb = [st.sb(f"xtb{u}", [P, DC, P]) for u in range(2)]
        turned = [st.banks(f"turned{u}", 1) for u in range(2)]
        prod = [st.banks(f"prod{u}", 1) for u in range(2)]
        ring = [st.banks(f"ring{u}", 1) for u in range(4)]
        w_in = st.sem("w_in")
        stats_done, root_asked, root_ready, rstd_step = (
            st.sem(x) for x in ("stats_done", "root_asked", "root_ready", "rstd_step"))
        root = st.sb("root", [P, 3, NT])
        rows_ready, turn_ready, xt_ready, prod_ready, prod_taken, kept = (
            st.sems(x) for x in ("rows_ready", "turn_ready", "xt_ready", "prod_ready", "prod_taken", "kept"))
        kept_all, ring_ready, split_high = (st.sem(x) for x in ("kept_all", "ring_ready", "split_high"))
        ring_free = [st.sem(f"ring_free{n}") for n in range(4)]
        n_loads = 1 + (d_bias is not None) + (extra is not None) + (
            0 if not d_cols else 1 + (d_cols[1] is not None))
        keeps = xn is not None or xt is not None
        parted = len(dest.shape) == 5
        by_vector = parted or bias is not None
        part_high = st.sem("part_high")
        jobs = []
        m = 0
        for dst, tokens, biased, split in cols:
            for c in range(dst.shape[1] // (2 if split else 1)):
                for a in range(0, tokens, BANK):
                    jobs.append((m, dst, c, a, min(BANK, tokens - a), biased, split))
                m += 1
        split_at = [n for n, job in enumerate(jobs) if job[-1]]

        def halves(n):
            _, dst, c, a, size, _, _ = jobs[n]
            for e in range(2):
                yield (ring[n % 4][e * HD:(e + 1) * HD, 0:size], dst[0:HD, 2 * c + e, a:a + size],
                       dst[HD:2 * HD, 2 * c + e, a:a + size])

        block = st.block()

        @block.sync
        def _(sp):
            sp.dma_start(w[:, :, :], d_w).then_inc(w_in, 16)
            if bias is not None:
                sp.dma_start(bias[:, :], d_bias.to_broadcast([P, width])).then_inc(w_in, 16)
            if extra is not None:
                sp.dma_start(wx[:, :, :], d_extra).then_inc(w_in, 16)
            if d_cols:
                sp.dma_start(wc[:, :, :], d_cols[0]).then_inc(w_in, 16)
                if d_cols[1] is not None:
                    sp.dma_start(bc[:, :], d_cols[1]).then_inc(w_in, 16)
            sp.wait_ge(w_in, 16 * n_loads)

        @block.vector
        def _(dve):
            if normalise:
                for i in range(NT):
                    dve.bn_stats(stats[:, i, :], src[:, i, :]).then_inc(stats_done, 1)
                for i in range(NT):
                    dve.wait_ge(stats_done, i + 1)
                    dve.bn_aggr(mv[:, i, :], stats[:, i, :]).then_inc(stats_done, 1)
                dve.wait_ge(stats_done, 2 * NT)
                inverse_root(dve, rstd, mv[:, :, 1], root, root_asked, root_ready, rstd_step)

            def rows(t, _):
                i, s, u = t
                dve.wait_ge(turn_ready[u], s)
                if keeps:
                    dve.wait_ge(kept[u], s)
                if normalise:
                    dve.tensor_scalar(xb[u][:, :], src[:, i, :], mv[:, i, 0:1], rstd[:, bass.ds(i, 1)],
                                      ALU.subtract, ALU.mult).then_inc(rows_ready[u], 1)
                else:
                    dve.tensor_copy(xb[u][:, :], src[:, i, :]).then_inc(rows_ready[u], 1)

            def product_out(t):
                i, s, u = t
                if parted:
                    dve.wait_ge(part_high, i + 1)
                    high, low = dest[:, bass.ds(i, 1), :, 0, :], dest[:, bass.ds(i, 1), :, 1, :]
                    dve.tensor_tensor(low, prod[u][:, 0:width].rearrange("p (a h k) -> p a h k", a=1, k=dest.shape[4]),
                                      high.bitcast(F32), ALU.subtract).then_inc(prod_taken[u], 1)
                else:
                    dve.wait_ge(prod_ready[u], s + 1)
                    dve.tensor_tensor(dest[:, i, :], prod[u][:, 0:width], bias[:, :], ALU.add) \
                       .then_inc(prod_taken[u], 1)

            def body(t, prev):
                i, s, u = t
                if prev is None:
                    rows(t, None)
                if not (isinstance(i, int) and i == NT - 1):
                    rows((i + 1, s + u, 1 - u), None)
                if prev is not None:
                    product_out(prev)

            if by_vector:
                if bias is not None:
                    dve.wait_ge(w_in, 16 * n_loads)
                product_out(tiles(dve, NT, body))
            else:
                tiles(dve, NT, rows)
            for n, (m, dst, c, a, size, biased, split) in enumerate(jobs):
                if split:
                    dve.wait_ge(split_high, split_at.index(n) + 1)
                    for rows_, high, low in halves(n):
                        ins = dve.tensor_tensor(low, rows_, high.bitcast(F32), ALU.subtract)
                    ins.then_inc(ring_free[n % 4], 1)
                elif n % 2:
                    dve.wait_ge(ring_ready, n + 1)
                    into = dst[:, c, a:a + size]
                    if biased is None:
                        ins = dve.tensor_copy(into, ring[n % 4][:, 0:size])
                    else:
                        dve.wait_ge(w_in, 16 * n_loads)
                        ins = dve.tensor_scalar(into, ring[n % 4][:, 0:size], bc[:, m:m + 1], None, ALU.add)
                    ins.then_inc(ring_free[n % 4], 1)

        @block.gpsimd
        def _(pool):
            if keeps:
                def keep(t, _):
                    i, s, u = t
                    if xn is not None:
                        pool.wait_ge(rows_ready[u], s + 1)
                        ins = pool.tensor_copy(xn[:, i, :], xb[u][:, :])
                    if xt is not None:
                        pool.wait_ge(xt_ready[u], s + 1)
                        ins = pool.tensor_copy(xt[:, :, bass.ts(i, P)], xtb[u][:, :, :])
                    ins.then_inc(kept[u], 1)

                tiles(pool, NT, keep)
                pool.wait_ge(kept[0], NT - NT // 2)
                pool.wait_ge(kept[1], NT // 2)
                pool.sem_inc(kept_all, 1)

        @block.tensor
        def _(pe):
            pe.wait_ge(w_in, 16 * n_loads)

            def turn(t):
                i, s, u = t
                pe.wait_ge(rows_ready[u], s + 1)
                pe.wait_ge(xt_ready[u], s)
                for c in range(DC):
                    ins = pe.transpose(turned[u][:, c * P:(c + 1) * P], xb[u][:, c * P:(c + 1) * P], g.ident[:, :])
                ins.then_inc(turn_ready[u], 1)

            def product(t):
                i, s, u = t
                pe.wait_ge(xt_ready[u], s + 1)
                pe.wait_ge(prod_taken[u], s)
                for c in range(DC):
                    ins = pe.matmul(prod[u][:, 0:width], xtb[u][:, c, :], w[:, c, :],
                                    start=(c == 0), stop=(c == DC - 1))
                if extra is not None:
                    m = extra.shape[2]
                    for c in range(DC):
                        ins = pe.matmul(ring[u][:, 0:m], xtb[u][:, c, :], wx[:, c, :],
                                        start=(c == 0), stop=(c == DC - 1))
                ins.then_inc(prod_ready[u], 1)

            def body(t, prev):
                turn(t)
                if prev is not None:
                    product(prev)

            product(tiles(pe, NT, body))
            if jobs:
                pe.wait_ge(kept_all, 1)
                if extra is not None:
                    pe.wait_ge(prod_taken[0], NT - NT // 2)
                    pe.wait_ge(prod_taken[1], NT // 2)
            for n, (m, dst, col, a, size, biased, split) in enumerate(jobs):
                pe.wait_ge(ring_free[n % 4], n // 4)
                for c in range(DC):
                    ins = pe.matmul(ring[n % 4][:, 0:size], wc[:, c, m * P:(m + 1) * P], xt[:, c, a:a + size],
                                    start=(c == 0), stop=(c == DC - 1))
                ins.then_inc(ring_ready, 1)

        @block.scalar
        def _(act):
            if normalise:
                act.wait_ge(root_asked, 1)
                act.activation(root[:, 1, :], root[:, 0, :], ACT.Sqrt).then_inc(root_ready, 1)

            def turn_out(t):
                i, s, u = t
                act.wait_ge(turn_ready[u], s + 1)
                act.wait_ge(prod_ready[u], s)
                if xt is not None:
                    act.wait_ge(kept[u], s)
                act.copy(xtb[u][:, :, :], turned[u][:, 0:D].rearrange("p (c n) -> p c n", c=DC)) \
                   .then_inc(xt_ready[u], 1)

            def product_out(t):
                i, s, u = t
                if by_vector and not parted:
                    return
                act.wait_ge(prod_ready[u], s + 1)
                if parted:
                    act.copy(dest[:, bass.ds(i, 1), :, 0, :],
                             prod[u][:, 0:width].rearrange("p (a h k) -> p a h k", a=1, k=dest.shape[4])) \
                       .then_inc(part_high, 1)
                    return
                ins = act.copy(dest[:, i, :], prod[u][:, 0:width])
                if extra is not None:
                    ins = act.copy(extra[:, i, :], ring[u][:, 0:extra.shape[2]])
                ins.then_inc(prod_taken[u], 1)

            def body(t, prev):
                turn_out(t)
                if prev is not None:
                    product_out(prev)

            product_out(tiles(act, NT, body))
            for n, (m, dst, c, a, size, biased, split) in enumerate(jobs):
                if split:
                    act.wait_ge(ring_ready, n + 1)
                    for rows_, high, low in halves(n):
                        ins = act.copy(high, rows_)
                    ins.then_inc(split_high, 1)
                elif n % 2 == 0:
                    act.wait_ge(ring_ready, n + 1)
                    into = dst[:, c, a:a + size]
                    if biased is None:
                        ins = act.copy(into, ring[n % 4][:, 0:size])
                    else:
                        act.wait_ge(w_in, 16 * n_loads)
                        ins = act.activation(into, ring[n % 4][:, 0:size], ACT.Identity, bias=bc[:, m:m + 1])
                    ins.then_inc(ring_free[n % 4], 1)


CLEAR = 8


def clear_slots(sp, g, d, n):
    rows = d["slot_rows"][n].rearrange("(n p) d -> p n d", p=P)
    for a in range(0, SLOTS[n], CLEAR):
        b = min(a + CLEAR, SLOTS[n])
        sp.dma_start(rows[:, a:b, :], each(g.zeros[:, :], b - a)).then_inc(g.cleared[n], 16)


def attention_stage(nc, g, d, name, qt, kt, v, res, layer):
    scale = float(D) ** -0.5
    with Stage(nc, name) as st:
        adj = [st.sb(f"adj{u}", [P, NP]) for u in range(2)]
        qs = [st.sb(f"qs{u}", [P, DC, P]) for u in range(2)]
        att = st.sb("att", [P, N])
        att_t = st.sb("att_t", [P, NT, P])
        top, neg, total, inv = (st.sb(x, [P, 1]) for x in ("top", "neg", "total", "inv"))
        scores = st.banks("scores", 3)
        turned = [st.banks(f"turned{b}", 1) for b in range(3)]
        out = st.banks("out", 1)
        adj_in, adj_used, qs_ready = st.sems("adj_in"), st.sems("adj_used"), st.sems("qs_ready")
        (scores_ready, top_ready, neg_ready, exp_done, inv_ready, att_ready, out_ready, out_used, res_ready,
         copied_act, copied_dve) = (st.sem(x) for x in (
             "scores_ready", "top_ready", "neg_ready", "exp_done", "inv_ready", "att_ready", "out_ready",
             "out_used", "res_ready", "copied_act", "copied_dve"))
        turn_ready = [st.sem(f"turn_ready{b}") for b in range(3)]
        block = st.block()

        @block.sync
        def _(sp):
            def body(t, _):
                i, s, u = t
                sp.wait_ge(adj_used[u], s)
                sp.dma_start(adj[u][:, :], d["adj_rows"][bass.ds(i, 1), :, :].rearrange("a p n -> (a p) n")) \
                  .then_inc(adj_in[u], 16)

            tiles(sp, NT, body)
            for n in (0, 1) if layer == 0 else (2,):
                clear_slots(sp, g, d, n)

        @block.gpsimd
        def _(pool):
            if layer == 1:
                pool.tensor_tensor(g.x[:, :, :], g.x[:, :, :], res[:, :, :], ALU.add).then_inc(res_ready, 1)

            def body(t, _):
                i, s, u = t
                pool.wait_ge(scores_ready, 2 * s)
                pool.tensor_copy(qs[u][:, :, :], qt[:, :, bass.ts(i, P)]).then_inc(qs_ready[u], 1)

            tiles(pool, NT, body)

        @block.tensor
        def _(pe):
            def score(t):
                i, s, u = t
                pe.wait_ge(qs_ready[u], s + 1)
                pe.wait_ge(exp_done, i)
                for a, size in COLS:
                    for c in range(DC):
                        ins = pe.matmul(scores[:, a:a + size], qs[u][:, c, :], kt[:, c, a:a + size],
                                        start=(c == 0), stop=(c == DC - 1))
                ins.then_inc(scores_ready, 1)

            def turn(t):
                i, s, u = t
                pe.wait_ge(att_ready, i + 1)
                pe.wait_ge(copied_act, 2 * i)
                pe.wait_ge(copied_dve, i)
                for b, (k0, k1) in enumerate(GROUPS):
                    for k in range(k0, k1):
                        n = rows_of(k)
                        ins = pe.transpose(turned[b][0:n, (k - k0) * P:(k - k0 + 1) * P],
                                           att[:, k * P:k * P + n], g.ident[:, :])
                    ins.then_inc(turn_ready[b], 1)

            def values(t):
                i, s, u = t
                pe.wait_ge(out_used, i)
                for k in range(NT):
                    n = rows_of(k)
                    if k == GROUPS[0][0]:
                        pe.wait_ge(copied_act, 2 * i + 1)
                    if k == GROUPS[1][0]:
                        pe.wait_ge(copied_dve, i + 1)
                    if k == GROUPS[2][0]:
                        pe.wait_ge(copied_act, 2 * i + 2)
                    ins = pe.matmul(out[:, 0:D], att_t[0:n, k, :], v[0:n, k, 0:D],
                                    start=(k == 0), stop=(k == NT - 1))
                ins.then_inc(out_ready, 1)

            def body(t, prev):
                score(t)
                if prev is not None:
                    turn(prev)
                    values(prev)

            last = tiles(pe, NT, body)
            turn(last)
            values(last)

        def copy_group(copy, b, k0, k1, sem):
            full = k1 - (k1 == NT)
            src = turned[b][:, 0:(full - k0) * P].rearrange("p (k n) -> p k n", n=P)
            ins = copy(att_t[:, k0:full, :], src)
            if full < k1:
                ins = copy(att_t[0:TAIL, full, :], turned[b][0:TAIL, (full - k0) * P:(full - k0 + 1) * P])
            ins.then_inc(sem, 1)

        @block.scalar
        def _(act):
            def turned_out(t):
                for b in (0, 2):
                    act.wait_ge(turn_ready[b], t[0] + 1)
                    copy_group(act.copy, b, *GROUPS[b], copied_act)

            def body(t, prev):
                if prev is not None:
                    turned_out(prev)
                act.wait_ge(neg_ready, t[0] + 1)
                act.activation(att[:, :], scores[:, 0:N], ACT.Exp, bias=neg[:, :], scale=scale,
                               accum_out=total[:, :]).then_inc(exp_done, 1)

            turned_out(tiles(act, NT, body))

        @block.vector
        def _(dve):
            def result(t):
                i, s, u = t
                dve.wait_ge(out_ready, i + 1)
                into = res if layer == 0 else g.x
                dve.scalar_tensor_tensor(into[:, i, :], out[:, 0:D], 0.0, into[:, i, :],
                                         ALU.max, ALU.add).then_inc(out_used, 1)

            if layer == 1:
                dve.wait_ge(res_ready, 1)

            def turned_out(t):
                dve.wait_ge(turn_ready[1], t[0] + 1)
                copy_group(dve.tensor_copy, 1, *GROUPS[1], copied_dve)

            def body(t, prev):
                i, s, u = t
                dve.wait_ge(scores_ready, i + 1)
                dve.tensor_reduce(top[:, :], scores[:, 0:N], AX, ALU.max).then_inc(top_ready, 1)
                dve.wait_ge(top_ready, i + 1)
                dve.tensor_scalar(neg[:, :], top[:, :], -scale, None, ALU.mult).then_inc(neg_ready, 1)
                if prev is not None:
                    turned_out(prev)
                dve.wait_ge(exp_done, i + 1)
                dve.reciprocal(inv[:, :], total[:, :]).then_inc(inv_ready, 1)
                dve.wait_ge(inv_ready, i + 1)
                dve.wait_ge(adj_in[u], 16 * (s + 1))
                dve.scalar_tensor_tensor(att[:, :], att[:, :], inv[:, 0:1], adj[u][:, 0:N],
                                         ALU.mult, ALU.add).then_inc(att_ready, 1)
                dve.wait_ge(att_ready, i + 1)
                dve.sem_inc(adj_used[u], 1)
                if prev is not None:
                    result(prev)

            last = tiles(dve, NT, body)
            turned_out(last)
            result(last)


def norm_rows(dve, src, dst, stats, mv, rstd, root, sems):
    stats_done, root_asked, root_ready, rstd_step, rows_done = sems
    for i in range(NT):
        dve.bn_stats(stats[:, i, :], src[:, i, :]).then_inc(stats_done, 1)
    for i in range(NT):
        dve.wait_ge(stats_done, i + 1)
        dve.bn_aggr(mv[:, i, :], stats[:, i, :]).then_inc(stats_done, 1)
    dve.wait_ge(stats_done, 2 * NT)
    inverse_root(dve, rstd, mv[:, :, 1], root, root_asked, root_ready, rstd_step)
    for i in range(NT):
        dve.tensor_scalar(dst[:, i, :], src[:, i, :], mv[:, i, 0:1], rstd[:, i:i + 1],
                          ALU.subtract, ALU.mult).then_inc(rows_done, 1)
    dve.wait_ge(rows_done, NT)


def norm_memory(st):
    return (st.sb("stats", [P, NT, 6]), st.sb("mv", [P, NT, 2]), st.sb("rstd", [P, NT]), st.sb("root", [P, 3, NT]),
            [st.sem(x) for x in ("stats_done", "root_asked", "root_ready", "rstd_step", "rows_done")])


def over(ap, n):
    return ap.unsqueeze(2).to_broadcast([ap.shape[0], ap.shape[1], n])


def each(ap, n):
    return ap.unsqueeze(1).to_broadcast([ap.shape[0], n, ap.shape[1]])


def route_stage(nc, g, name, experts, slots, logits, xn, slot_rows, cleared, weights, r, over_all):
    E = experts
    with Stage(nc, name) as st:
        best = st.sb("best", [P, NT, 8])
        at = st.sb("at", [P, NT, 8], U32)
        atf = st.sb("atf", [P, NT, 2])
        hot = [st.sb(f"hot{k}", [P, NT, E]) for k in range(2)]
        either = st.sb("either", [P, NT, E])
        pos = st.sb("pos", [P, NT, E])
        pick = [st.sb(f"pick{k}", [P, NT, E]) for k in range(2)]
        part = st.sb("part", [P, NT, E])
        base = st.sb("base", [P, NT + 1, E])
        cnt_i = st.sb("cnt_i", [P, E], I32)
        cnt, upto, first = (st.sb(x, [P, E]) for x in ("cnt", "upto", "first"))
        slot_f = st.sb("slot_f", [P, 2, NT])
        below = st.sb("below", [1, slots, E])
        own = st.sb("own", [1, slots])
        shifted = st.sb("shifted", [P, NT, E])
        gap, den = st.sb("gap", [P, NT]), st.sb("den", [P, NT])
        rank, total = st.banks("rank", 1), st.banks("total", 1)
        step, picked, counted, exp_asked, exp_done, slots_ready, sent = (
            st.sem(x) for x in ("step", "picked", "counted", "exp_asked", "exp_done", "slots_ready", "sent"))
        block = st.block()

        @block.sync
        def _(sp):
            for e in range(2):
                if e:
                    sp.wait_ge(weights.up_in, 16)
                weights.load_up(sp, e, e)
                if e:
                    sp.wait_ge(weights.down_in, 16 * weights.parts)
                weights.load_down(sp, e, e)

        @block.vector
        def _(dve):
            done = [0]

            def then(ins):
                done[0] += 1
                ins.then_inc(step, 1)
                dve.wait_ge(step, done[0])

            for i in range(NT):
                done[0] += 1
                dve.max(best[:, i, :], logits[:, i, :]).then_inc(step, 1)
            for i in range(NT):
                dve.wait_ge(step, i + 1)
                done[0] += 1
                dve.max_index(at[:, i, :], best[:, i, :], logits[:, i, :]).then_inc(step, 1)
            dve.wait_ge(step, done[0])
            then(dve.tensor_copy(atf[:, :, :], at[:, :, 0:2]))
            then(dve.tensor_tensor(atf[:, :, :], atf[:, :, :], over(g.past_end[:, :], 2), ALU.add))
            for k in range(2):
                then(dve.tensor_tensor(hot[k][:, :, :], each(g.iota[:, 0:E], NT), over(atf[:, :, k], E),
                                       ALU.is_equal))
            dve.tensor_tensor(either[:, :, :], hot[0][:, :, :], hot[1][:, :, :], ALU.add).then_inc(picked, 1)
            dve.tensor_tensor(gap[:, :], best[:, :, 1], best[:, :, 0], ALU.subtract).then_inc(exp_asked, 1)
            if over_all:
                dve.tensor_tensor(shifted[:, :, :], logits[:, :, :], over(best[:, :, 0], E), ALU.subtract) \
                   .then_inc(exp_asked, 1)
            then(dve.memset(base[:, 0, :], 0.0))
            dve.wait_ge(counted, 1)
            for i in range(NT):
                then(dve.tensor_tensor(base[:, i + 1, :], base[:, i, :], total[:, i * E:(i + 1) * E], ALU.add))
            then(dve.tensor_scalar(cnt_i[:, :], base[:, NT, :], float(P - 1), None, ALU.add))
            then(dve.tensor_scalar(cnt_i[:, :], cnt_i[:, :], P.bit_length() - 1, None, ALU.arith_shift_right))
            then(dve.tensor_copy(cnt[:, :], cnt_i[:, :]))
            then(dve.tensor_tensor_scan(upto[:, :], g.ones[:, 0:E], cnt[:, :], 0.0, ALU.mult, ALU.add))
            then(dve.tensor_tensor(first[:, :], upto[:, :], cnt[:, :], ALU.subtract))
            then(dve.scalar_tensor_tensor(pos[:, :, :], each(first[:, :], NT), float(P), base[:, 0:NT, :],
                                          ALU.mult, ALU.add))
            then(dve.tensor_tensor(pos[:, :, :], pos[:, :, :],
                                   rank[:, 0:NT * E].rearrange("p (n e) -> p n e", e=E), ALU.add))
            for k in range(2):
                then(dve.tensor_tensor(pick[k][:, :, :], hot[k][:, :, :], pos[:, :, :], ALU.mult))
                then(dve.tensor_reduce(slot_f[:, k, :], pick[k][:, :, :], AX, ALU.add))
            dve.tensor_copy(r.slot[:, :, :], slot_f[:, :, :]).then_inc(slots_ready, 1)
            then(dve.tensor_tensor(below[:, :, :], each(upto[0:1, :], slots), over(g.iota[0:1, 0:slots], E), ALU.is_le))
            then(dve.tensor_reduce(own[:, :], below[:, :, :], AX, ALU.add))
            then(dve.tensor_scalar(r.expert[:, :], own[:, :], float(E - 1), None, ALU.min))
            then(dve.tensor_scalar(r.side[:, :], r.expert[:, :], 1, None, ALU.bitwise_and))
            then(dve.tensor_copy(r.upto[:, :], upto[0:1, :]))
            dve.wait_ge(exp_done, 1 + over_all)
            if over_all:
                then(dve.tensor_reduce(den[:, :], shifted[:, :, :], AX, ALU.add))
            else:
                then(dve.tensor_scalar(den[:, :], gap[:, :], 1.0, None, ALU.add))
            then(dve.reciprocal(r.weight[:, 0, :], den[:, :]))
            then(dve.tensor_tensor(r.weight[:, 1, :], r.weight[:, 0, :], gap[:, :], ALU.mult))

        @block.scalar
        def _(act):
            act.wait_ge(exp_asked, 1 + over_all)
            act.activation(gap[:, :], gap[:, :], ACT.Exp).then_inc(exp_done, 1)
            if over_all:
                act.activation(shifted[:, :, :], shifted[:, :, :], ACT.Exp).then_inc(exp_done, 1)

        @block.tensor
        def _(pe):
            pe.wait_ge(picked, 1)
            flat = either[:, :, :].rearrange("p n e -> p (n e)")
            pe.matmul(rank[:, 0:NT * E], g.before[:, :], flat, start=True, stop=True)
            pe.matmul(total[:, 0:NT * E], g.ones[:, :], flat, start=True, stop=True).then_inc(counted, 1)

        @block.gpsimd
        def _(pool):
            pool.wait_ge(slots_ready, 1)
            pool.wait_ge(cleared, 16 * -(-slots // CLEAR))
            for i in range(NT):
                n = rows_of(i)
                for k in range(2):
                    pool.indirect_dma_start(
                        out=slot_rows[:, :], out_offset=bass.IndirectOffsetOnAxis(ap=r.slot[0:n, k, i:i + 1], axis=0),
                        in_=xn[0:n, i, :], in_offset=None).then_inc(sent, 16)
            pool.wait_ge(sent, 32 * NT)


def expert_stage(nc, g, name, experts, hidden, gated, slots, slot_rows, slot_out, weights, r):
    H = hidden
    U = 2 * H if gated else H
    KH = H // P
    biased = weights.d_bias is not None
    UW, DW = weights.up.shape[2], weights.down.shape[2]
    UP_CUT = U
    HALVES = [(0, 4), (4, KH)]
    with Stage(nc, name) as st:
        up = [st.sb(f"up{u}", [P, UW]) for u in range(2)]
        down = [[st.sb(f"down{u}{part}", [P, KH * D], F32R) for part in range(2)] for u in range(2)]
        down_bias = [st.sb(f"down_bias{u}", [P, D]) for u in range(2)] if biased else None
        rows = [st.sb(f"rows{u}", [P, D]) for u in range(2)]
        rows_t = [st.sb(f"rows_t{u}", [P, DC, P]) for u in range(2)]
        half = st.sb("half", [P, KH, P]) if gated else None
        h = st.sb("h", [P, KH, P])
        h_t = [[st.sb(f"h_t{u}{part}", [P, KH, P], F32R) for part in range(2)] for u in range(2)]
        y = [st.sb(f"y{u}", [P, D]) for u in range(2)]
        pup = [[st.banks(f"pup{b}{k}", 1) for k in range(1 + gated)] for b in range(2)]
        prow, pout = st.banks("prow", 1), st.banks("pout", 1)
        rows_in, up_used, down_used, rows_used, y_stored = (st.sems(x) for x in (
            "rows_in", "up_used", "down_used", "rows_used", "y_stored"))
        hidden_ready, half_ready, h_taken, h_high, h_ready = (st.sems(x) for x in (
            "hidden_ready", "half_ready", "h_taken", "h_high", "h_ready"))
        rows_t_ready, y_ready = st.sem("rows_t_ready"), st.sem("y_ready")
        up_act, up_dve, down_act, down_dve = (st.sem(x) for x in ("up_act", "up_dve", "down_act", "down_dve"))
        load_begun = st.sem("load_begun")
        block = st.block()

        def is_last(t):
            return isinstance(t[0], int) and t[0] == slots - 1

        def following(t):
            j, s, u = t
            return j + 1, s + u, 1 - u

        @block.sync
        def _(sp):
            def wait(sem, value):
                sp.wait_ge(sem, value)
                sp.sem_inc(load_begun, 1)

            def load(e, u):
                before = sp.value_load(r.upto[0:1, bass.ds(e - 2, 1)], min_val=0, max_val=slots)
                wait(up_act, before + 1)
                wait(up_dve, before + 1)
                wait(weights.up_in, 16 * e)
                weights.load_up(sp, e, u)
                wait(down_act, before + 1)
                wait(down_dve, before + 1)
                wait(weights.down_in, 16 * weights.parts * e)
                weights.load_down(sp, e, u)

            with sp.Fori(1, experts // 2) as pair:
                load(2 * pair, 0)
                load(2 * pair + 1, 1)

        def copy_up(eng, copy, a, b, done, t, e, side):
            j, s, u = t
            eng.wait_ge(weights.up_in, 16 * (e + 1))
            eng.wait_ge(up_used[u], s)
            if biased:
                if not (isinstance(j, int) and j < 2):
                    for bank in range(2):
                        eng.wait_ge(h_taken[bank], j - 1)
            copy(up[u][:, a:b].unsqueeze(1), weights.up[:, bass.ds(side, 1), a:b]).then_inc(done, 1)

        def down_free(eng, t, e):
            j, s, u = t
            eng.wait_ge(weights.down_in, 16 * weights.parts * (e + 1))
            eng.wait_ge(down_used[u], s)

        def expert_of(eng, t):
            at = bass.ds(t[0], 1)
            return (eng.value_load(r.expert[0:1, at], min_val=0, max_val=experts - 1),
                    eng.value_load(r.side[0:1, at], min_val=0, max_val=1))

        @block.tensor
        def _(pe):
            def turn_rows(t):
                j, s, u = t
                pe.wait_ge(rows_in[u], 16 * (s + 1))
                pe.wait_ge(rows_t_ready, j)
                for c in range(DC):
                    ins = pe.transpose(prow[:, c * P:(c + 1) * P], rows[u][:, c * P:(c + 1) * P], g.ident[:, :])
                ins.then_inc(rows_used[u], 1)

            def go_up(t):
                j, s, u = t
                pe.wait_ge(rows_t_ready, j + 1)
                pe.wait_ge(up_act, j + 2)
                pe.wait_ge(up_dve, j + 2)
                for b, (m0, m1) in enumerate(HALVES):
                    pe.wait_ge(h_taken[b], j)
                    for k in range(1 + gated):
                        for m in range(m0, m1):
                            for c in range(DC):
                                w = c * U + k * H + m * P
                                ins = pe.matmul(pup[b][k][:, (m - m0) * P:(m - m0 + 1) * P], up[u][:, w:w + P],
                                                rows_t[u][:, c, :], start=(c == 0), stop=(c == DC - 1))
                    ins.then_inc(hidden_ready[b], 1)
                pe.sem_inc(up_used[u], 1)

            def go_down(t):
                j, s, u = t
                pe.wait_ge(down_act, j + 2)
                pe.wait_ge(down_dve, j + 2)
                pe.wait_ge(y_ready, j)
                for b, (k0, k1) in enumerate(HALVES):
                    pe.wait_ge(h_ready[b], j + 1)
                    for k in range(k0, k1):
                        ins = parts_product(pe, pout[:, 0:D], [x[:, k, :] for x in h_t[u]],
                                            [x[:, k * D:(k + 1) * D] for x in down[u]], k == 0, k == KH - 1)
                ins.then_inc(down_used[u], 1)

            def body(t, prev):
                if prev is None:
                    turn_rows(t)
                go_up(t)
                if not is_last(t):
                    turn_rows(following(t))
                if prev is not None:
                    go_down(prev)

            go_down(tiles(pe, slots, body))

        @block.scalar
        def _(act):
            act.sem_inc(up_act, 1)
            act.sem_inc(down_act, 1)

            def rows_out(t):
                j, s, u = t
                act.wait_ge(rows_used[u], s + 1)
                act.wait_ge(up_used[u], s)
                act.copy(rows_t[u][:, :, :], prow[:, 0:D].rearrange("p (c n) -> p c n", c=DC)) \
                   .then_inc(rows_t_ready, 1)

            def result_out(t):
                j, s, u = t
                act.wait_ge(down_used[u], s + 1)
                act.wait_ge(y_stored[u], 16 * s)
                act.copy(y[u][:, :], pout[:, 0:D]).then_inc(y_ready, 1)

            def hidden_out(t, b):
                j, s, u = t
                m0, m1 = HALVES[b]
                act.wait_ge(hidden_ready[b], j + 1)
                if gated:
                    act.activation(half[:, m0:m1, :], pup[b][0][:, 0:(m1 - m0) * P].rearrange("p (k n) -> p k n", n=P),
                                   ACT.Silu).then_inc(half_ready[b], 1)
                elif b == 0:
                    act.wait_ge(h_ready[b], j)
                    for m in range(m0, m1):
                        ins = act.activation(h[:, m, :], pup[b][0][:, (m - m0) * P:(m - m0 + 1) * P], ACT.Relu,
                                             bias=up[u][:, DC * U + m:DC * U + m + 1])
                    ins.then_inc(h_taken[b], 1)

            def hidden_high(t, b):
                j, s, u = t
                m0, m1 = HALVES[b]
                act.wait_ge(h_taken[b], j + 1)
                act.copy(h_t[u][0][:, m0:m1, :], h[:, m0:m1, :]).then_inc(h_high[b], 1)

            def copy_down(t, e, side):
                down_free(act, t, e)
                act.copy(down[t[2]][0][:, :].unsqueeze(1), weights.down[:, bass.ds(side, 1), 0:KH * D]) \
                   .then_inc(down_act, 1)

            def body(t, prev):
                if prev is None:
                    e, side = expert_of(act, t)
                    rows_out(t)
                    copy_up(act, act.copy, UP_CUT, UW, up_act, t, e, side)
                    copy_down(t, e, side)
                if not is_last(t):
                    e, side = expert_of(act, following(t))
                    copy_up(act, act.copy, UP_CUT, UW, up_act, following(t), e, side)
                hidden_out(t, 0)
                if gated:
                    hidden_out(t, 1)
                if not is_last(t):
                    rows_out(following(t))
                for b in range(2):
                    hidden_high(t, b)
                if gated and prev is not None:
                    result_out(prev)
                if not is_last(t):
                    copy_down(following(t), e, side)

            last = tiles(act, slots, body)
            if gated:
                result_out(last)

        @block.vector
        def _(dve):
            dve.sem_inc(up_dve, 1)
            dve.sem_inc(down_dve, 1)

            def result_out(t):
                j, s, u = t
                dve.wait_ge(down_used[u], s + 1)
                dve.wait_ge(y_stored[u], 16 * s)
                dve.tensor_tensor(y[u][:, :], pout[:, 0:D], down_bias[u][:, :], ALU.add).then_inc(y_ready, 1)

            def hidden_out(t, b):
                j, s, u = t
                m0, m1 = HALVES[b]
                if gated:
                    dve.wait_ge(half_ready[b], j + 1)
                    dve.wait_ge(h_ready[b], j)
                    dve.tensor_tensor(h[:, m0:m1, :], half[:, m0:m1, :],
                                      pup[b][1][:, 0:(m1 - m0) * P].rearrange("p (k n) -> p k n", n=P), ALU.mult) \
                       .then_inc(h_taken[b], 1)
                elif b == 1:
                    dve.wait_ge(hidden_ready[b], j + 1)
                    dve.wait_ge(h_ready[b], j)
                    for m in range(m0, m1):
                        ins = dve.tensor_scalar(h[:, m, :], pup[b][0][:, (m - m0) * P:(m - m0 + 1) * P],
                                                up[u][:, DC * U + m:DC * U + m + 1], 0.0, ALU.add, ALU.max)
                    ins.then_inc(h_taken[b], 1)

            def hidden_low(t, b):
                j, s, u = t
                m0, m1 = HALVES[b]
                dve.wait_ge(h_high[b], j + 1)
                dve.tensor_tensor(h_t[u][1][:, m0:m1, :], h[:, m0:m1, :], h_t[u][0][:, m0:m1, :].bitcast(F32),
                                  ALU.subtract).then_inc(h_ready[b], 1)

            def copy_down(t, e, side):
                j, s, u = t
                down_free(dve, t, e)
                if biased:
                    if not (isinstance(j, int) and j < 2):
                        dve.wait_ge(y_ready, j - 1)
                    dve.tensor_copy(down_bias[u][:, :].unsqueeze(1), weights.down[:, bass.ds(side, 1), KH * D:DW])
                dve.wait_ge(down_act, j + 2)
                high, low = down[u]
                dve.tensor_tensor(low[:, :].unsqueeze(1), weights.down[:, bass.ds(side, 1), 0:KH * D],
                                  high[:, :].bitcast(F32).unsqueeze(1), ALU.subtract).then_inc(down_dve, 1)

            def body(t, prev):
                if prev is None:
                    e, side = expert_of(dve, t)
                    copy_up(dve, dve.tensor_copy, 0, UP_CUT, up_dve, t, e, side)
                    copy_down(t, e, side)
                if not is_last(t):
                    e, side = expert_of(dve, following(t))
                    copy_up(dve, dve.tensor_copy, 0, UP_CUT, up_dve, following(t), e, side)
                hidden_out(t, 0)
                hidden_out(t, 1)
                hidden_low(t, 0)
                hidden_low(t, 1)
                if prev is not None and biased:
                    result_out(prev)
                if not is_last(t):
                    copy_down(following(t), e, side)

            last = tiles(dve, slots, body)
            if biased:
                result_out(last)

        @block.gpsimd
        def _(pool):
            def load(j, u):
                pool.dma_start(rows[u][:, :], slot_rows.rearrange("(n p) d -> n p d", p=P)[bass.ds(j, 1), :, :]
                               .rearrange("a p d -> (a p) d")).then_inc(rows_in[u], 16)

            def store(t):
                j, s, u = t
                pool.wait_ge(y_ready, j + 1)
                pool.dma_start(slot_out.rearrange("(n p) d -> n p d", p=P)[bass.ds(j, 1), :, :]
                               .rearrange("a p d -> (a p) d"), y[u][:, :]).then_inc(y_stored[u], 16)

            def body(t, prev):
                j, s, u = t
                if not (isinstance(j, int) and j >= slots - 2):
                    pool.wait_ge(rows_used[u], s + 1)
                    load(j + 2, u)
                if prev is not None:
                    store(prev)

            load(0, 0)
            load(1, 1)
            store(tiles(pool, slots, body))
            pool.wait_ge(y_stored[0], 16 * (slots - slots // 2))
            pool.wait_ge(y_stored[1], 16 * (slots // 2))


def combine_stage(nc, g, name, slot_out, r, xn=None, d_gain=None, d_offset=None):
    with Stage(nc, name) as st:
        got = st.sb("got", [P, 2, NT, D])
        stats, mv, rstd, root, sems = norm_memory(st)
        gain, offset = (st.sb("gain", [P, D]), st.sb("offset", [P, D])) if xn is not None else (None, None)
        fetched = [st.sem(f"fetched{i}") for i in range(NT)]
        step, loaded = st.sem("step"), st.sem("loaded")
        block = st.block()
        into = xn if xn is not None else g.x

        @block.gpsimd
        def _(pool):
            for i in range(NT):
                for k in range(2):
                    pool.indirect_dma_start(
                        out=got[:, k, i, :], out_offset=None, in_=slot_out[:, :],
                        in_offset=bass.IndirectOffsetOnAxis(ap=r.slot[:, k, i:i + 1], axis=0)) \
                        .then_inc(fetched[i], 16)
            for i in range(NT):
                pool.wait_ge(fetched[i], 32)

        @block.sync
        def _(sp):
            if xn is not None:
                sp.dma_start(gain[:, :], d_gain.to_broadcast([P, D])).then_inc(loaded, 16)
                sp.dma_start(offset[:, :], d_offset.to_broadcast([P, D])).then_inc(loaded, 16)

        @block.scalar
        def _(act):
            if xn is not None:
                act.wait_ge(sems[1], 1)
                act.activation(root[:, 1, :], root[:, 0, :], ACT.Sqrt).then_inc(sems[2], 1)

        @block.vector
        def _(dve):
            for i in range(NT):
                dve.wait_ge(fetched[i], 32)
                for k in range(2):
                    dve.scalar_tensor_tensor(into[:, i, :], got[:, k, i, :], r.weight[:, k, i:i + 1], into[:, i, :],
                                             ALU.mult, ALU.add).then_inc(step, 1)
                    dve.wait_ge(step, 2 * i + k + 1)
            if xn is not None:
                out = got[:, 0, :, :]
                norm_rows(dve, xn, out, stats, mv, rstd, root, sems)
                dve.wait_ge(loaded, 32)
                n = 2 * NT
                for other, op in ((each(gain[:, :], NT), ALU.mult), (each(offset[:, :], NT), ALU.add)):
                    dve.tensor_tensor(out, out, other, op).then_inc(step, 1)
                    n += 1
                    dve.wait_ge(step, n)
                dve.tensor_tensor(g.x[:, :, :], g.x[:, :, :], out, ALU.add).then_inc(step, 1)
                dve.wait_ge(step, n + 1)


def spread_stage(nc, g, d, name, hidden, d_bias):
    with Stage(nc, name) as st:
        adj = [st.sb(f"adj{u}", [P, NT, P]) for u in range(2)]
        bias = st.sb("bias", [P, D])
        sum_ = st.sb("sum", [P, D])
        out = [st.banks(f"out{u}", 1) for u in range(2)]
        adj_in, out_ready, out_used = st.sems("adj_in"), st.sems("out_ready"), st.sems("out_used")
        bias_in, added = st.sem("bias_in"), st.sem("added")
        block = st.block()

        @block.sync
        def _(sp):
            sp.dma_start(bias[:, :], d_bias.to_broadcast([P, D])).then_inc(bias_in, 16)

            def body(t, _):
                i, s, u = t
                sp.wait_ge(out_ready[u], s)
                sp.dma_start(adj[u][:, :, :], d["adj_t"][bass.ds(i, 1), :, :, :].rearrange("a p k n -> (a p) k n")) \
                  .then_inc(adj_in[u], 16)

            tiles(sp, NT, body)

        @block.tensor
        def _(pe):
            def body(t, _):
                i, s, u = t
                pe.wait_ge(adj_in[u], 16 * (s + 1))
                pe.wait_ge(out_used[u], s)
                for k in range(NT):
                    n = rows_of(k)
                    ins = pe.matmul(out[u][:, 0:D], adj[u][0:n, k, :], hidden[0:n, k, :], start=(k == 0),
                                    stop=(k == NT - 1))
                ins.then_inc(out_ready[u], 1)

            tiles(pe, NT, body)

        @block.vector
        def _(dve):
            def body(t, _):
                i, s, u = t
                dve.wait_ge(out_ready[u], s + 1)
                dve.tensor_tensor(sum_[:, :], out[u][:, 0:D], bias[:, :], ALU.add).then_inc(out_used[u], 1)
                dve.wait_ge(out_used[u], s + 1)
                dve.tensor_tensor(g.x[:, i, :], g.x[:, i, :], sum_[:, :], ALU.add).then_inc(added, 1)
                dve.wait_ge(added, i + 1)

            dve.wait_ge(bias_in, 16)
            tiles(dve, NT, body)


def shift_stage(nc, g, name):
    MARK, SHL, SHR, FIELDS, OUT = 0, 39, 40, 64, 128
    W = 16
    with Stage(nc, name) as st:
        y = st.sb("y", [P, NT, D])
        stats, mv, rstd, root, sems = norm_memory(st)
        fall = st.sb("fall", [P, 3, W])
        hot = st.sb("hot", [P, NT, 3, W])
        top = st.sb("top", [P, NT, 3])
        none = st.sb("none", [P, NT, 3])
        value = st.sb("value", [P, NT])
        value_i, by_i, left_i, right_i, low_i, high_i = (
            st.sb(x, [P, NT], I32) for x in ("value_i", "by_i", "left_i", "right_i", "low_i", "high_i"))
        left, right, mark, is_left, is_right, height = (
            st.sb(x, [P, NT]) for x in ("left", "right", "mark", "is_left", "is_right", "height"))
        nibble = st.sb("nibble", [P, 2, NT])
        spot = st.sb("spot", [P, NT, 2, W])
        step = st.sem("step")
        block = st.block()

        @block.scalar
        def _(act):
            act.wait_ge(sems[1], 1)
            act.activation(root[:, 1, :], root[:, 0, :], ACT.Sqrt).then_inc(sems[2], 1)

        @block.vector
        def _(dve):
            norm_rows(dve, g.x, y, stats, mv, rstd, root, sems)
            done = [0]

            def then(ins):
                done[0] += 1
                ins.then_inc(step, 1)
                dve.wait_ge(step, done[0])

            for f in range(3):
                then(dve.tensor_scalar(fall[:, f, :], g.iota[:, 0:W], -1.0, float(W), ALU.mult, ALU.add))
            then(dve.scalar_tensor_tensor(hot[:, :, :, :].rearrange("p n f w -> p n (f w)"),
                                          y[:, :, FIELDS:FIELDS + 3 * W], 0.5,
                                          each(fall[:, :, :].rearrange("p f w -> p (f w)"), NT), ALU.is_gt, ALU.mult))
            then(dve.tensor_reduce(top[:, :, :].rearrange("p n f -> p (n f)"),
                                   hot[:, :, :, :].rearrange("p n f w -> p (n f) w"), AX, ALU.max))
            then(dve.tensor_scalar(none[:, :, :], top[:, :, :], 0.0, float(W), ALU.is_equal, ALU.mult))
            then(dve.tensor_tensor(top[:, :, :], top[:, :, :], none[:, :, :], ALU.add))
            then(dve.tensor_scalar(top[:, :, :], top[:, :, :], -1.0, float(W), ALU.mult, ALU.add))
            then(dve.scalar_tensor_tensor(value[:, :], top[:, :, 1], float(W), top[:, :, 0], ALU.mult, ALU.add))
            then(dve.tensor_copy(value_i[:, :], value[:, :]))
            then(dve.tensor_copy(by_i[:, :], top[:, :, 2]))
            then(dve.tensor_tensor(left_i[:, :], value_i[:, :], by_i[:, :], ALU.logical_shift_left))
            then(dve.tensor_scalar(left_i[:, :], left_i[:, :], W * W - 1, None, ALU.bitwise_and))
            then(dve.tensor_tensor(right_i[:, :], value_i[:, :], by_i[:, :], ALU.logical_shift_right))
            then(dve.tensor_copy(left[:, :], left_i[:, :]))
            then(dve.tensor_copy(right[:, :], right_i[:, :]))
            then(dve.tensor_scalar(mark[:, :], y[:, :, MARK], 0.5, None, ALU.is_gt))
            then(dve.scalar_tensor_tensor(is_left[:, :], y[:, :, SHL], 0.5, mark[:, :], ALU.is_gt, ALU.mult))
            then(dve.scalar_tensor_tensor(is_right[:, :], y[:, :, SHR], 0.5, mark[:, :], ALU.is_gt, ALU.mult))
            then(dve.tensor_tensor(height[:, :], is_left[:, :], is_right[:, :], ALU.max))
            then(dve.tensor_tensor(is_right[:, :], height[:, :], is_left[:, :], ALU.subtract))
            then(dve.tensor_scalar(height[:, :], height[:, :], 2.0, None, ALU.mult))
            then(dve.tensor_tensor(left[:, :], left[:, :], is_left[:, :], ALU.mult))
            then(dve.tensor_tensor(right[:, :], right[:, :], is_right[:, :], ALU.mult))
            then(dve.tensor_tensor(value[:, :], left[:, :], right[:, :], ALU.add))
            then(dve.tensor_copy(value_i[:, :], value[:, :]))
            then(dve.tensor_scalar(low_i[:, :], value_i[:, :], W - 1, None, ALU.bitwise_and))
            then(dve.tensor_scalar(high_i[:, :], value_i[:, :], 4, None, ALU.logical_shift_right))
            then(dve.tensor_copy(nibble[:, 0, :], low_i[:, :]))
            then(dve.tensor_copy(nibble[:, 1, :], high_i[:, :]))
            for f in range(2):
                then(dve.tensor_tensor(spot[:, :, f, :], each(g.iota[:, 0:W], NT), over(nibble[:, f, :], W),
                                       ALU.is_equal))
                then(dve.tensor_tensor(spot[:, :, f, :], spot[:, :, f, :], over(height[:, :], W), ALU.mult))
            then(dve.tensor_tensor(g.x[:, :, :], g.x[:, :, :], y[:, :, :], ALU.add))
            field = g.x[:, :, OUT:OUT + 2 * W]
            then(dve.tensor_tensor(field, field, spot[:, :, :, :].rearrange("p n f w -> p n (f w)"), ALU.add))


def heads_stage(nc, g, d, name, qt, kt, v, d_wo):
    FV = HEADS * HD
    VC = FV // P
    SCALE = float(HD) ** -0.5
    with Stage(nc, name) as st:
        mask = [st.sb(f"mask{u}", [P, NP]) for u in range(2)]
        qs = [st.sb(f"qs{u}", [2 * HD, 2, VC, 2, P], F32R) for u in range(2)]
        wo = st.sb("wo", [2 * HD, HEADS, D])
        p = [st.sb(f"p{x}", [P, N]) for x in range(2)]
        att_t = [st.sb(f"att_t{x}", [P, 2, NT, P], F32R) for x in range(2)]
        o_t = [st.sb(f"o_t{x}", [2 * HD, P]) for x in range(2)]
        top, neg, total, inv = (st.sb(x, [P, 4]) for x in ("top", "neg", "total", "inv"))
        scores = st.banks("scores", 3)
        turned = [st.banks(f"turned{b}", 1) for b in range(3)]
        out, proj = st.banks("out", 1), st.banks("proj", 1)
        adj_in, mask_ready, mask_used, qs_ready = (st.sems(x) for x in ("adj_in", "mask_ready", "mask_used", "qs_ready"))
        eye_done, wo_in, split_step, scores_ready, masked_ready, neg_ready, exp_done, inv_ready, copied_high, \
            copied_low, out_ready, out_used, proj_ready, proj_used = (st.sem(x) for x in (
                "eye_done", "wo_in", "split_step", "scores_ready", "masked_ready", "neg_ready", "exp_done",
                "inv_ready", "copied_high", "copied_low", "out_ready", "out_used", "proj_ready", "proj_used"))
        turn_ready = [st.sem(f"turn_ready{b}") for b in range(3)]
        mask_begun, masked_begun, split_begun = (st.sem(x) for x in ("mask_begun", "masked_begun", "split_begun"))
        first_split = st.sem("first_split")
        block = st.block()

        def lagged(body_head):
            def body(t, prev):
                for h in range(HEADS):
                    old = ((t, h - n) if h >= n else (prev, h + HEADS - n) for n in (1, 2, 3))
                    body_head((t, h), *(x if x[0] is not None else None for x in old))
            return body

        def finish(last, body_head):
            for steps in range(1, 4):
                body_head(None, *((last, HEADS - 1 + steps - n) if n >= steps else None for n in (1, 2, 3)))

        def number(t, h):
            return HEADS * t[0] + h

        @block.sync
        def _(sp):
            sp.dma_start(wo[:, :, :], d_wo).then_inc(wo_in, 16)

            def body(t, _):
                i, s, u = t
                sp.wait_ge(mask_used[u], s)
                sp.dma_start(mask[u][:, :], d["adj_rows"][bass.ds(i, 1), :, :].rearrange("a p n -> (a p) n")) \
                  .then_inc(adj_in[u], 16)

            tiles(sp, NT, body)

        @block.gpsimd
        def _(pool):
            def body(t, _):
                i, s, u = t
                if isinstance(i, int) and i == 0:
                    return
                if not (isinstance(i, int) and i < 2):
                    pool.wait_ge(scores_ready, HEADS * (i - 1))
                    pool.sem_inc(split_begun, 1)
                tile = bass.ts(i, P)
                for e in range(2):
                    own = slice(e * HD, (e + 1) * HD)
                    pool.tensor_copy(qs[u][own, 0, :, e, :], qt[own, :, tile]).then_inc(split_step, 1)
                pool.wait_ge(split_step, 8 * i - 6)
                pool.sem_inc(split_begun, 1)
                for e in range(2):
                    own = slice(e * HD, (e + 1) * HD)
                    pool.tensor_tensor(qs[u][own, 1, :, e, :], qt[own, :, tile], qs[u][own, 0, :, e, :].bitcast(F32),
                                       ALU.subtract).then_inc(split_step, 1)
                pool.wait_ge(split_step, 8 * i - 4)
                pool.sem_inc(split_begun, 1)
                for e in range(2):
                    own, other = slice(e * HD, (e + 1) * HD), slice((1 - e) * HD, (2 - e) * HD)
                    for part in range(2):
                        pool.tensor_copy(qs[u][other, part, :, e, :], qs[u][own, part, :, e, :].bitcast(F32)) \
                            .then_inc(split_step, 1)
                pool.wait_ge(split_step, 8 * i)
                pool.sem_inc(qs_ready[u], 1)
                pool.wait_ge(eye_done, i + 1)
                pool.sem_inc(mask_begun, 1)
                pool.tensor_scalar(mask[u][:, :], mask[u][:, :], 1.0, MASK / SCALE, ALU.subtract, ALU.mult) \
                    .then_inc(mask_ready[u], 1)
                pool.wait_ge(mask_ready[u], s + 1)
                pool.sem_inc(split_begun, 1)

            tiles(pool, NT, body)

        @block.tensor
        def _(pe):
            pe.wait_ge(wo_in, 16)

            def score(t, h):
                i, s, u = t
                if h == 0:
                    pe.wait_ge(qs_ready[u], s + 1)
                pe.wait_ge(masked_ready, number(t, h))
                for part in range(2):
                    for a, size in COLS:
                        ins = pe.matmul(scores[:, a:a + size], qs[u][:, part, h // 2, h % 2, :], kt[:, h, a:a + size],
                                        start=(part == 0), stop=(part == 1))
                ins.then_inc(scores_ready, 1)

            def turn(t, h):
                n = number(t, h)
                pe.wait_ge(exp_done, n + 1)
                pe.wait_ge(copied_low, 3 * n)
                for b, (k0, k1) in enumerate(GROUPS):
                    for k in range(k0, k1):
                        m = rows_of(k)
                        ins = pe.transpose(turned[b][0:m, (k - k0) * P:(k - k0 + 1) * P],
                                           p[h % 2][:, k * P:k * P + m], g.ident[:, :])
                    ins.then_inc(turn_ready[b], 1)

            def values(t, h):
                n = number(t, h)
                pe.wait_ge(out_used, n)
                pe.wait_ge(copied_low, 3 * n + 3)
                for k in range(NT):
                    m = rows_of(k)
                    ins = pe.matmul(out[:, 0:2 * P], v[0:m, k, h, :, :].rearrange("p a k -> p (a k)"),
                                    att_t[h % 2][0:m, :, k, :], start=(k == 0), stop=(k == NT - 1))
                ins.then_inc(out_ready, 1)

            def project(t, h):
                n = number(t, h)
                pe.wait_ge(out_used, n + 1)
                pe.wait_ge(proj_used, n)
                pe.matmul(proj[:, 0:D], o_t[h % 2][:, :], wo[:, h, :], start=True, stop=True).then_inc(proj_ready, 1)

            def head(new, one, two, three):
                if new is not None:
                    score(*new)
                if one is not None:
                    turn(*one)
                if three is not None:
                    project(*three)
                if two is not None:
                    values(*two)

            finish(tiles(pe, NT, lagged(head)), head)

        def pieces(x, b):
            k0, k1 = GROUPS[b]
            full = k1 - (k1 == NT)
            high, low = att_t[x][:, 0, :, :], att_t[x][:, 1, :, :]
            yield (turned[b][:, 0:(full - k0) * P].rearrange("p (k n) -> p k n", n=P), high[:, k0:full, :],
                   low[:, k0:full, :])
            if full < k1:
                yield (turned[b][0:TAIL, (full - k0) * P:(full - k0 + 1) * P], high[0:TAIL, full, :],
                       low[0:TAIL, full, :])

        @block.scalar
        def _(act):
            def head(new, one, two, three):
                if one is not None:
                    n, h = number(*one), one[1]
                    for b in range(3):
                        act.wait_ge(turn_ready[b], n + 1)
                        for bank, high, _ in pieces(h % 2, b):
                            ins = act.copy(high, bank)
                        ins.then_inc(copied_high, 1)
                if new is not None:
                    n, h = number(*new), new[1]
                    act.wait_ge(neg_ready, n + 1)
                    act.activation(p[h % 2][:, :], p[h % 2][:, :], ACT.Exp, bias=neg[:, h % 4:h % 4 + 1],
                                   accum_out=total[:, h % 4:h % 4 + 1]).then_inc(exp_done, 1)

            finish(tiles(act, NT, lagged(head)), head)

        @block.vector
        def _(dve):
            def set_diagonal(t):
                i, s, u = t
                dve.wait_ge(adj_in[u], 16 * (s + 1))
                own = mask[u][:, bass.ts(i, P)]
                dve.tensor_tensor(own, own, g.ident[:, :], ALU.max).then_inc(eye_done, 1)

            for e in range(2):
                for to in range(2):
                    own, into = slice(e * HD, (e + 1) * HD), slice(to * HD, (to + 1) * HD)
                    dve.tensor_copy(qs[0][into, 0, :, e, :], qt[own, :, 0:P]).then_inc(first_split, 1)
            dve.wait_ge(first_split, 4)
            for e in range(2):
                for to in range(2):
                    own, into = slice(e * HD, (e + 1) * HD), slice(to * HD, (to + 1) * HD)
                    dve.tensor_tensor(qs[0][into, 1, :, e, :], qt[own, :, 0:P], qs[0][own, 0, :, e, :].bitcast(F32),
                                      ALU.subtract).then_inc(first_split, 1)
            dve.wait_ge(first_split, 8)
            dve.sem_inc(qs_ready[0], 1)
            set_diagonal((0, 0, 0))
            dve.wait_ge(eye_done, 1)
            dve.tensor_scalar(mask[0][:, :], mask[0][:, :], 1.0, MASK / SCALE, ALU.subtract, ALU.mult) \
               .then_inc(mask_ready[0], 1)

            def head(new, one, two, three):
                if three is not None:
                    n, h = number(*three), three[1]
                    dve.wait_ge(out_ready, n + 1)
                    dve.tensor_reduce(o_t[h % 2][:, :], out[:, 0:2 * P].rearrange("p (a n) -> p n a", a=2), AX, ALU.add) \
                       .then_inc(out_used, 1)
                if new is not None:
                    t, h = new
                    i, s, u = t
                    m = number(t, h)
                    dve.wait_ge(scores_ready, m + 1)
                    if h == 0:
                        dve.wait_ge(mask_ready[u], s + 1)
                    dve.sem_inc(masked_begun, 1)
                    dve.tensor_tensor_reduce(out=p[h % 2][:, :], in0=scores[:, 0:N], in1=mask[u][:, 0:N],
                                             scale=SCALE, scalar=-3.0e38, op0=ALU.add, op1=ALU.max,
                                             accum_out=top[:, h % 4:h % 4 + 1]).then_inc(masked_ready, 1)
                    dve.wait_ge(masked_ready, m + 1)
                    dve.tensor_scalar(neg[:, h % 4:h % 4 + 1], top[:, h % 4:h % 4 + 1], -1.0, None, ALU.mult) \
                       .then_inc(neg_ready, 1)
                    if h == HEADS - 1:
                        dve.sem_inc(mask_used[u], 1)
                    if h == HEADS - 3 and not (isinstance(i, int) and i == NT - 1):
                        set_diagonal((i + 1, s + u, 1 - u))
                if three is not None:
                    n, h = number(*three), three[1]
                    x = g.x[:, three[0][0], :]
                    dve.wait_ge(inv_ready, n + 1)
                    dve.wait_ge(proj_ready, n + 1)
                    dve.scalar_tensor_tensor(x, proj[:, 0:D], inv[:, h % 4:h % 4 + 1], x, ALU.mult, ALU.add) \
                       .then_inc(proj_used, 1)
                if one is not None:
                    for b in range(3):
                        dve.wait_ge(copied_high, 3 * number(*one) + b + 1)
                        for bank, high, low in pieces(one[1] % 2, b):
                            ins = dve.tensor_tensor(low, bank, high.bitcast(F32), ALU.subtract)
                        ins.then_inc(copied_low, 1)
                if two is not None:
                    n, h = number(*two), two[1]
                    dve.reciprocal(inv[:, h % 4:h % 4 + 1], total[:, h % 4:h % 4 + 1]).then_inc(inv_ready, 1)

            finish(tiles(dve, NT, lagged(head)), head)


def gate_stage(nc, g, d, name, hg, ex, ht):
    with Stage(nc, name) as st:
        adj = [st.sb(f"adj{u}", [P, NT, P]) for u in range(2)]
        e = [st.sb(f"e{u}", [P, NT, P]) for u in range(2)]
        z = st.sb("z", [P, NT, P])
        a_left = st.sb("a_left", [P, DC, P])
        a_right = st.sb("a_right", [P, D])
        bias = st.sb("bias", [1, D + 2])
        gate_bias = st.sb("gate_bias", [P, 2])
        left = st.sb("left", [P, NP])
        right = st.sb("right", [P, NT])
        junk = st.sb("junk", [P, D])
        xa = st.sb("xa", [P, NT, D])
        xb = st.sb("xb", [P, NT, D + 2])
        den = [st.sb(f"den{u}", [P, 1]) for u in range(2)]
        inv = [st.sb(f"inv{u}", [P, 1]) for u in range(2)]
        gate = st.sb("gate", [P, 2, NT])
        pleft = st.banks("pleft", 3)
        pa = [st.banks(f"pa{u}", 1) for u in range(2)]
        pb = [st.banks(f"pb{u}", 1) for u in range(2)]
        adj_in, e_ready, xa_ready, xb_ready, xa_used, xb_used = (st.sems(x) for x in (
            "adj_in", "e_ready", "xa_ready", "xb_ready", "xa_used", "xb_used"))
        loaded, left_ready, left_copied, right_ready, z_step, exp_done, den_step, gate_asked, gate_done, mixed, \
            sig_done = (st.sem(x) for x in (
                "loaded", "left_ready", "left_copied", "right_ready", "z_step", "exp_done", "den_step",
                "gate_asked", "gate_done", "mixed", "sig_done"))
        block = st.block()

        @block.sync
        def _(sp):
            sp.dma_start(a_left[:, :, :], d["a_left"]).then_inc(loaded, 16)
            sp.dma_start(a_right[:, :], d["a_right"].to_broadcast([P, D])).then_inc(loaded, 16)
            sp.dma_start(bias[:, :], d["b_gcnb"]).then_inc(loaded, 16)
            sp.dma_start(gate_bias[:, :], d["b_gates"].to_broadcast([P, 2])).then_inc(loaded, 16)

            def body(t, _):
                i, s, u = t
                sp.wait_ge(xb_ready[u], s)
                sp.wait_ge(e_ready[u], s)
                sp.dma_start(adj[u][:, :, :], d["adj_t"][bass.ds(i, 1), :, :, :].rearrange("a p k n -> (a p) k n")) \
                  .then_inc(adj_in[u], 16)

            tiles(sp, NT, body)

        @block.tensor
        def _(pe):
            pe.wait_ge(loaded, 64)
            for a in range(0, NP, BANK):
                size = min(BANK, NP - a)
                for c in range(DC):
                    ins = pe.matmul(pleft[:, a:a + size], a_left[:, c, :], ht[:, c, a:a + size],
                                    start=(c == 0), stop=(c == DC - 1))
            ins.then_inc(left_ready, 1)

            def body(t, _):
                i, s, u = t
                pe.wait_ge(adj_in[u], 16 * (s + 1))
                pe.wait_ge(xb_used[u], s)
                pe.matmul(pb[u][:, 0:D + 2], g.ones[0:1, :], bias[:, :], start=True, stop=False)
                for k in range(NT):
                    n = rows_of(k)
                    ins = pe.matmul(pb[u][:, 0:D + 2], adj[u][0:n, k, :], hg[0:n, k, 1 + D:2 * D + 3], start=False,
                                    stop=(k == NT - 1))
                ins.then_inc(xb_ready[u], 1)
                pe.wait_ge(e_ready[u], s + 1)
                pe.wait_ge(xa_used[u], s)
                for k in range(NT):
                    n = rows_of(k)
                    ins = pe.matmul(pa[u][:, 0:D + 1], e[u][0:n, k, :], hg[0:n, k, 0:D + 1],
                                    start=(k == 0), stop=(k == NT - 1))
                ins.then_inc(xa_ready[u], 1)

            tiles(pe, NT, body)

        @block.scalar
        def _(act):
            act.wait_ge(left_ready, 1)
            act.copy(left[:, :], pleft[:, 0:NP]).then_inc(left_copied, 1)

            def xb_out(t):
                i, s, u = t
                act.wait_ge(xb_ready[u], s + 1)
                act.copy(xb[:, i, :], pb[u][:, 0:D + 2]).then_inc(xb_used[u], 1)

            def body(t, prev):
                i, s, u = t
                act.wait_ge(z_step, 2 * i + 2)
                act.wait_ge(xa_ready[u], s)
                act.activation(e[u][:, :, :], z[:, :, :], ACT.Exp, scale=-1.0).then_inc(exp_done, 1)
                if prev is not None:
                    xb_out(prev)

            xb_out(tiles(act, NT, body))
            act.wait_ge(gate_asked, 2)
            act.activation(gate[:, :, :], gate[:, :, :], ACT.Sigmoid).then_inc(gate_done, 1)
            act.wait_ge(mixed, 2 * NT)
            act.activation(xa[:, :, :], xa[:, :, :], ACT.Sigmoid).then_inc(sig_done, 1)

        @block.vector
        def _(dve):
            dve.wait_ge(loaded, 64)
            for i in range(NT):
                if i:
                    dve.wait_ge(right_ready, i)
                dve.tensor_tensor_reduce(out=junk[:, :], in0=hg[:, i, 1:D + 1], in1=a_right[:, :], scale=1.0,
                                         scalar=0.0, op0=ALU.mult, op1=ALU.add, accum_out=right[:, i:i + 1]) \
                   .then_inc(right_ready, 1)
            dve.wait_ge(right_ready, NT)
            dve.wait_ge(left_copied, 1)

            def xa_out(t):
                i, s, u = t
                dve.wait_ge(xa_ready[u], s + 1)
                dve.tensor_scalar(den[u][:, :], pa[u][:, 0:1], 1e-5, None, ALU.add).then_inc(den_step, 1)
                dve.wait_ge(den_step, 2 * i + 1)
                dve.reciprocal(inv[u][:, :], den[u][:, :]).then_inc(den_step, 1)
                dve.wait_ge(den_step, 2 * i + 2)
                dve.tensor_scalar(xa[:, i, :], pa[u][:, 1:D + 1], inv[u][:, 0:1], None, ALU.mult) \
                   .then_inc(xa_used[u], 1)

            def body(t, prev):
                i, s, u = t
                dve.wait_ge(exp_done, i)
                dve.tensor_tensor(z[:, :, :], each(left[:, bass.ts(i, P)], NT), over(right[:, :], P), ALU.add) \
                   .then_inc(z_step, 1)
                dve.wait_ge(z_step, 2 * i + 1)
                dve.scalar_tensor_tensor(z[:, :, :], z[:, :, :], 0.01, z[:, :, :], ALU.mult, ALU.max) \
                   .then_inc(z_step, 1)
                if prev is not None:
                    xa_out(prev)
                dve.wait_ge(adj_in[u], 16 * (s + 1))
                dve.wait_ge(exp_done, i + 1)
                dve.scalar_tensor_tensor(e[u][:, :, :], adj[u][:, :, :], 0.0, e[u][:, :, :], ALU.not_equal, ALU.mult) \
                   .then_inc(e_ready[u], 1)

            xa_out(tiles(dve, NT, body))
            dve.wait_ge(xb_used[0], NT - NT // 2)
            dve.wait_ge(xb_used[1], NT // 2)
            dve.wait_ge(xa_used[0], NT - NT // 2)
            dve.wait_ge(xa_used[1], NT // 2)
            for k in range(2):
                dve.scalar_tensor_tensor(gate[:, k, :], xb[:, :, D + k], gate_bias[:, k:k + 1], ex[:, :, 2 + k],
                                         ALU.add, ALU.add).then_inc(gate_asked, 1)
            dve.wait_ge(gate_done, 1)
            for i in range(NT):
                dve.tensor_scalar(xa[:, i, :], xa[:, i, :], gate[:, 0, i:i + 1], None, ALU.mult).then_inc(mixed, 1)
            for i in range(NT):
                dve.wait_ge(mixed, NT + i)
                dve.scalar_tensor_tensor(xa[:, i, :], xb[:, i, 0:D], gate[:, 1, i:i + 1], xa[:, i, :],
                                         ALU.mult, ALU.add).then_inc(mixed, 1)
            dve.wait_ge(sig_done, 1)
            dve.tensor_tensor(g.x[:, :, :], g.x[:, :, :], xa[:, :, :], ALU.add).then_inc(mixed, 1)
            dve.wait_ge(mixed, 2 * NT + 1)


def build(nc, d, out):
    with ExitStack() as ctx:
        def sb(name, shape, dt=F32):
            return ctx.enter_context(nc.sbuf_tensor(name, shape, dt))

        g = Shared(x=sb("x", [P, NT, D]), ident=sb("ident", [P, P]), ones=sb("ones", [P, P]),
                  zeros=sb("zeros", [P, D]), before=sb("before", [P, P]), iota=sb("iota", [P, IOTA]),
                  past_end=sb("past_end", [P, NT]),
                  cleared=[nc.alloc_semaphore(f"cleared{n}") for n in range(len(SLOTS))])
        start_stage(nc, g, d)
        with ExitStack() as layer:
            def lsb(name, shape):
                return layer.enter_context(nc.sbuf_tensor(name, shape, F32))

            vr = lsb("vr", [P, NT, 2 * D])
            xt = lsb("xt", [P, DC, NP])
            qt, kt = lsb("qt", [P, DC, NP]), lsb("kt", [P, DC, N])
            v1 = lsb("v1", [P, NT, D])
            project_stage(nc, g, "proj0", g.x, True, d["w_vr0"], 2 * D, vr, d_bias=d["b_vr0"], xt=xt,
                          d_cols=(d["w_qk0"], d["b_qk0"]), cols=[(qt, NP, True, False), (kt, N, True, False)])
            hidden = vr[:, :, D:2 * D]
            attention_stage(nc, g, d, "att0", qt, kt, vr, hidden, 0)
            project_stage(nc, g, "proj1", hidden, False, d["w_v1"], D, v1, d_bias=d["b_v1"], xt=xt,
                          d_cols=(d["w_qk1"], d["b_qk1"]), cols=[(qt, NP, True, False), (kt, N, True, False)])
            attention_stage(nc, g, d, "att1", qt, kt, v1, hidden, 1)
        rest(nc, g, d)
        with Stage(nc, "end") as st:
            stored = st.sem("stored")
            block = st.block()

            @block.sync
            def _(sp):
                full = (NT - 1) * P
                sp.dma_start(out[0:full, :].rearrange("(n p) d -> p n d", p=P), g.x[:, 0:NT - 1, :]) \
                  .then_inc(stored, 16)
                sp.dma_start(out[full:N, :], g.x[0:TAIL, NT - 1, :]).then_inc(stored, 16)
                sp.wait_ge(stored, 32)


def mixture(nc, g, d, n, gated, over_all):
    E, H, S = EXPERTS[n], HIDDEN[n], SLOTS[n]
    with ExitStack() as part:
        def psb(name, shape, dt=F32):
            return part.enter_context(nc.sbuf_tensor(f"mix{n}_{name}", shape, dt))

        xn = psb("xn", [P, NT, D])
        logits = psb("logits", [P, NT, E])
        r = Routing(psb("slot", [P, 2, NT], U32), psb("weight", [P, 2, NT]), psb("expert", [1, S], I32),
                    psb("side", [1, S], I32), psb("upto", [1, E], I32))
        project_stage(nc, g, f"gate{n}", g.x, True, d[f"w_gate{n}"], E, logits,
                      d_bias=d.get(f"b_gate{n}"), xn=xn)
        with ExitStack() as loaded:
            weights = Weights(nc, loaded, f"weights{n}", H, d[f"w_up{n}"], d[f"w_down{n}"], d.get(f"b_down{n}"))
            route_stage(nc, g, f"route{n}", E, S, logits, xn, d["slot_rows"][n], g.cleared[n], weights, r, over_all)
            expert_stage(nc, g, f"expert{n}", E, H, gated, S, d["slot_rows"][n], d["slot_out"][n], weights, r)
        if n == 0:
            combine_stage(nc, g, f"combine{n}", d["slot_out"][n], r, xn, d["gamma"], d["beta"])
        else:
            combine_stage(nc, g, f"combine{n}", d["slot_out"][n], r)


def rest(nc, g, d):
    mixture(nc, g, d, 0, False, 1)
    with ExitStack() as part:
        hidden = part.enter_context(nc.sbuf_tensor("hidden1", [P, NT, D], F32))
        project_stage(nc, g, "proj2", g.x, True, d["w_spread"], D, hidden)
        spread_stage(nc, g, d, "spread", hidden, d["b_spread"])
    shift_stage(nc, g, "shift")
    with ExitStack() as part:
        def psb(name, shape, dt=F32):
            return part.enter_context(nc.sbuf_tensor(f"heads_{name}", shape, dt))

        FV = HEADS * HD
        v = psb("v", [P, NT, HEADS, 2, HD], F32R)
        qt, kt = psb("qt", [P, FV // P, NP]), psb("kt", [2 * HD, HEADS, N], F32R)
        with ExitStack() as inner:
            xt = inner.enter_context(nc.sbuf_tensor("heads_xt", [P, DC, NP], F32))
            project_stage(nc, g, "proj3", g.x, True, d["w_v2"], FV, v, xt=xt, d_cols=(d["w_qk2"], None),
                          cols=[(qt, NP, None, False), (kt, N, None, True)])
        heads_stage(nc, g, d, "heads", qt, kt, v, d["w_o2"])
    mixture(nc, g, d, 1, True, 0)
    with ExitStack() as part:
        def psb(name, shape):
            return part.enter_context(nc.sbuf_tensor(f"gat_{name}", shape, F32))

        hg = psb("hg", [P, NT, 2 * D + 3])
        ex = psb("ex", [P, NT, 4])
        ht = psb("ht", [P, DC, NP])
        with ExitStack() as inner:
            xt = inner.enter_context(nc.sbuf_tensor("gat_xt", [P, DC, NP], F32))
            project_stage(nc, g, "proj4", g.x, True, d["w_hg"], 2 * D, hg[:, :, 1:2 * D + 1], xt=xt,
                          d_extra=d["w_gates"], extra=ex, d_cols=(d["w_sa"], None), cols=[(ht, NP, None, False)])
        with Stage(nc, "ends") as st:
            set_ = st.sem("set")
            block = st.block()

            @block.vector
            def _(dve):
                dve.memset(hg[:, :, 0:1], 1.0).then_inc(set_, 1)
                dve.tensor_copy(hg[:, :, 2 * D + 1:2 * D + 3], ex[:, :, 0:2]).then_inc(set_, 1)
        gate_stage(nc, g, d, "gat", hg, ex, ht)
    mixture(nc, g, d, 2, True, 0)




def layouts(np, a):
    def rows(w):
        return np.ascontiguousarray(w.reshape(-1, P, w.shape[1]).transpose(1, 0, 2))

    def cols(*bs):
        return np.ascontiguousarray(np.concatenate(bs).reshape(-1, P).T)

    f32 = np.float32
    x = np.zeros((NP, D), f32)
    x[:N] = a["x"]
    adj = np.zeros((NP, NP), f32)
    adj[:N, :N] = a["adj"]
    arrays = {
        "x": rows(x),
        "adj_rows": adj.reshape(NT, P, NP),
        "w_vr0": rows(np.concatenate([a["L0_gnn_wv0"].T, a["L0_gnn_wres"].T], 1)),
        "b_vr0": np.concatenate([a["L0_gnn_bv0"], a["L0_gnn_bres"]])[None],
        "w_qk0": rows(np.concatenate([a["L0_gnn_wq0"].T, a["L0_gnn_wk0"].T], 1)),
        "b_qk0": cols(a["L0_gnn_bq0"], a["L0_gnn_bk0"]),
        "w_v1": rows(a["L0_gnn_wv1"].T),
        "b_v1": a["L0_gnn_bv1"][None],
        "w_qk1": rows(np.concatenate([a["L0_gnn_wq1"].T, a["L0_gnn_wk1"].T], 1)),
        "b_qk1": cols(a["L0_gnn_bq1"], a["L0_gnn_bk1"]),
    }
    arrays["adj_t"] = adj.reshape(NT, P, NT, P).transpose(0, 3, 2, 1)

    def tiled(w):
        return w.reshape(w.shape[0], -1, P, w.shape[2]).transpose(0, 2, 1, 3).reshape(w.shape[0], P, -1)

    arrays.update(
        w_gate0=rows(a["L0_ffn_Wg"]), b_gate0=a["L0_ffn_bg"][None],
        w_up0=np.concatenate([tiled(a["L0_ffn_W1"]), tiled(a["L0_ffn_b1"][:, :, None])], 2), w_down0=tiled(a["L0_ffn_W2"]),
        b_down0=a["L0_ffn_b2"],
        gamma=a["L0_ffn_gamma"][None], beta=a["L0_ffn_beta"][None],
        w_spread=rows(a["L1_gnn_W"].transpose(1, 0, 2).reshape(D, D)), b_spread=a["L1_gnn_b"].reshape(1, D),
        w_v2=rows(a["L2_gnn_Wvs"].transpose(1, 0, 2).reshape(D, HEADS * HD)),
        w_qk2=rows(np.concatenate([a[f"L2_gnn_{w}"].transpose(1, 0, 2).reshape(D, HEADS * HD) for w in ("Wqs", "Wks")], 1)),
        w_o2=np.concatenate([a["L2_gnn_Wo"].transpose(1, 0, 2)] * 2, 0),
        w_gate1=rows(a["L2_ffn_gate_w"]),
        w_up1=tiled(np.concatenate([a["L2_ffn_W1"], a["L2_ffn_W3"]], 2)), w_down1=tiled(a["L2_ffn_W2"]),
        w_hg=rows(np.concatenate([a["L3_gnn_W_sa"], a["L3_gnn_W_gcnb"]], 1)),
        w_sa=rows(a["L3_gnn_W_sa"]),
        w_gates=rows(np.concatenate([a["L3_gnn_Wa"].reshape(2, D), a["L3_gnn_Wb"].reshape(2, D)])[[0, 2, 1, 3]].T),
        a_left=rows(np.repeat(a["L3_gnn_a_sa"][0, :D, None], P, 1)),
        a_right=a["L3_gnn_a_sa"][:, D:],
        b_gcnb=np.concatenate([a["L3_gnn_b_gcnb"], np.zeros(2, f32)])[None],
        b_gates=np.concatenate([a["L3_gnn_ba"], a["L3_gnn_bb"]])[None],
        w_gate2=rows(a["L3_ffn_gate_w"].T),
        w_up2=tiled(np.concatenate([a["L3_ffn_w1"].transpose(0, 2, 1), a["L3_ffn_w3"].transpose(0, 2, 1)], 2)),
        w_down2=tiled(a["L3_ffn_w2"].transpose(0, 2, 1)),
    )
    return arrays


def kernel(**inputs):
    import numpy as np
    import concourse.bacc as bacc
    from concourse.bass_utils import run_bass_kernel_spmd

    nc = bacc.Bacc("TRN2", target_bir_lowering=False, num_devices=1)
    arrays = {k: np.ascontiguousarray(v) for k, v in
              layouts(np, {k: np.asarray(v) for k, v in inputs.items()}).items()}
    d = {k: nc.dram_tensor(f"in_{k}", v.shape, mybir.dt.from_np(v.dtype), kind="ExternalInput").ap()
         for k, v in arrays.items()}
    d["slot_rows"] = [nc.dram_tensor(f"slot_rows{n}", (s * P, D), F32, kind="Internal").ap() for n, s in enumerate(SLOTS)]
    d["slot_out"] = [nc.dram_tensor(f"slot_out{n}", (s * P, D), F32, kind="Internal").ap() for n, s in enumerate(SLOTS)]
    out = nc.dram_tensor("out", (N, D), F32, kind="ExternalOutput").ap()
    build(nc, d, out)
    return run_bass_kernel_spmd(nc, [{f"in_{k}": v for k, v in arrays.items()}], core_ids=[0]).results[0]["out"]
```

```python
from contextlib import ExitStack

import concourse.bass as bass
from concourse import mybir

F32 = mybir.dt.float32
F32R = mybir.dt.float32r
I32 = mybir.dt.int32
U32 = mybir.dt.uint32
ALU = mybir.AluOpType
ACT = mybir.ActivationFunctionType
AX = mybir.AxisListType.X

P = 128
N = 1354
NT = -(-N // P)
TAIL = N - (NT - 1) * P
NP = NT * P
D = 256
DC = D // P
BANK = 512
EPS = 1e-5
COLS = [(0, BANK), (BANK, BANK), (2 * BANK, N - 2 * BANK)]
GROUPS = [(0, 4), (4, 8), (8, NT)]
HEADS, HD = 8, 64
MASK = 1e16
IOTA = 48
EXPERTS = (16, 8, 8)
HIDDEN = (1024, 1024, 768)
SLOTS = [2 * N // P + e for e in EXPERTS]


def rows_of(k):
    return TAIL if k == NT - 1 else P


def tiles(eng, count, body):
    last = (count - 1) // 2
    body((0, 0, 0), None)
    body((1, 0, 1), (0, 0, 0))
    body((2, 1, 0), (1, 0, 1))
    with eng.Fori(1, last - 1) as s:
        body((2 * s + 1, s, 1), (2 * s, s, 0))
        body((2 * s + 2, s + 1, 0), (2 * s + 1, s, 1))
    body((2 * last - 1, last - 1, 1), (2 * last - 2, last - 1, 0))
    body((2 * last, last, 0), (2 * last - 1, last - 1, 1))
    return 2 * last, last, 0


def parts_product(pe, out, left, right, start, stop):
    (lh, ll), (rh, rl) = left, right
    pe.matmul(out, lh, rh, start=start, stop=False)
    pe.matmul(out, lh, rl, start=False, stop=False)
    return pe.matmul(out, ll, rh, start=False, stop=stop)


class Shared:

    def __init__(self, x, stats, ident, ones, zeros, before, iota, past_end, cleared):
        self.x, self.stats, self.ident, self.ones, self.zeros = x, stats, ident, ones, zeros
        self.before, self.iota, self.past_end, self.cleared = before, iota, past_end, cleared


class Routing:

    def __init__(self, slot, weight, expert, side, upto):
        self.slot, self.weight, self.expert, self.side, self.upto = slot, weight, expert, side, upto


class Weights:

    def __init__(self, nc, part, name, hidden, d_up, d_down, d_bias):
        self.d_up, self.d_down, self.d_bias = d_up, d_down, d_bias
        self.down_cols = hidden // P * D
        self.parts = 1 if d_bias is None else 2
        self.up = part.enter_context(nc.sbuf_tensor(f"{name}_up", [P, 2, d_up.shape[2]], F32))
        self.down = part.enter_context(nc.sbuf_tensor(f"{name}_down", [P, 2, self.down_cols + D * (self.parts - 1)], F32))
        self.up_in, self.down_in = (nc.alloc_semaphore(f"{name}_{x}") for x in ("up_in", "down_in"))

    def load_up(self, sp, e, u):
        sp.dma_start(self.up[:, u, :], self.d_up[bass.ds(e, 1), :, :].rearrange("a p m -> (a p) m")) \
          .then_inc(self.up_in, 16)

    def load_down(self, sp, e, u):
        n = self.down_cols
        sp.dma_start(self.down[:, u, 0:n], self.d_down[bass.ds(e, 1), :, :].rearrange("a p m -> (a p) m")) \
          .then_inc(self.down_in, 16)
        if self.d_bias is not None:
            sp.dma_start(self.down[:, u, n:n + D], self.d_bias[bass.ds(e, 1), :].to_broadcast([P, D])) \
              .then_inc(self.down_in, 16)


class Stage:

    def __init__(self, nc, name):
        self.nc, self.name = nc, name

    def __enter__(self):
        self.ctx, self.taken = ExitStack(), []
        return self

    def __exit__(self, *a):
        self.ctx.close()
        self.nc.clear_and_free_semaphores(self.taken)
        self.nc.all_engine_barrier()

    def sb(self, name, shape, dt=F32):
        return self.ctx.enter_context(self.nc.sbuf_tensor(f"{self.name}_{name}", shape, dt))

    def banks(self, name, n):
        return self.ctx.enter_context(self.nc.psum_tensor(f"{self.name}_{name}", [P, n * BANK], F32))

    def sem(self, name):
        self.taken.append(self.nc.alloc_semaphore(f"{self.name}_{name}"))
        return self.taken[-1]

    def sems(self, name):
        return [self.sem(f"{name}{u}") for u in range(2)]

    def block(self):
        return self.ctx.enter_context(self.nc.Block())


def start_stage(nc, g, d):
    with Stage(nc, "start") as st:
        rows_i = st.sb("rows_i", [P, IOTA], I32)
        loaded, made, filled = (st.sem(x) for x in ("loaded", "made", "filled"))
        block = st.block()

        @block.sync
        def _(sp):
            sp.dma_start(g.x[:, :, :], d["x"]).then_inc(loaded, 16)
            sp.wait_ge(loaded, 16)

        @block.gpsimd
        def _(pool):
            pool.iota(rows_i[:, :], pattern=[[1, IOTA]], base=0, channel_multiplier=0).then_inc(filled, 1)
            pool.memset(g.ident[:, :], 0.0).then_inc(filled, 1)
            pool.memset(g.before[:, :], 1.0).then_inc(filled, 1)
            pool.memset(g.past_end[:, :], 0.0).then_inc(filled, 1)
            pool.wait_ge(filled, 4)
            pool.affine_select(out=g.past_end[:, NT - 1:NT], in_=g.past_end[:, NT - 1:NT], compare_op=ALU.is_gt,
                               fill=100.0, base=TAIL, pattern=[[0, 1]], channel_multiplier=-1).then_inc(filled, 1)
            pool.tensor_copy(g.iota[:, :], rows_i[:, :]).then_inc(filled, 1)
            pool.affine_select(out=g.ident[:, :], in_=g.ident[:, :], compare_op=ALU.not_equal, fill=1.0,
                               base=0, pattern=[[-1, P]], channel_multiplier=1).then_inc(filled, 1)
            pool.affine_select(out=g.before[:, :], in_=g.before[:, :], compare_op=ALU.is_gt, fill=0.0,
                               base=0, pattern=[[1, P]], channel_multiplier=-1).then_inc(filled, 1)
            pool.wait_ge(filled, 8)

        @block.vector
        def _(dve):
            dve.memset(g.zeros[:, :], 0.0).then_inc(made, 1)
            dve.memset(g.ones[:, :], 1.0).then_inc(made, 1)
            dve.wait_ge(made, 2)


def inverse_root(dve, rstd, variance, root, asked, ready, step):
    v, half, sq = root[:, 0, :], root[:, 1, :], root[:, 2, :]
    dve.tensor_scalar(v, variance, EPS, None, ALU.add).then_inc(asked, 1)
    dve.wait_ge(ready, 1)
    dve.reciprocal(half, half).then_inc(step, 1)
    dve.wait_ge(step, 1)
    dve.tensor_tensor(sq, half, half, ALU.mult).then_inc(step, 1)
    dve.wait_ge(step, 2)
    dve.tensor_tensor(sq, sq, v, ALU.mult).then_inc(step, 1)
    dve.wait_ge(step, 3)
    dve.tensor_scalar(sq, sq, -0.5, 1.5, ALU.mult, ALU.add).then_inc(step, 1)
    dve.wait_ge(step, 4)
    dve.tensor_tensor(rstd[:, :], half, sq, ALU.mult).then_inc(step, 1)
    dve.wait_ge(step, 5)


def take_stats(dve, stats, src, mv, stats_done, known):
    if not known:
        for i in range(NT):
            dve.bn_stats(stats[:, i, :], src[:, i, :]).then_inc(stats_done, 1)
    for i in range(NT):
        if not known:
            dve.wait_ge(stats_done, i + 1)
        dve.bn_aggr(mv[:, i, :], stats[:, i, :]).then_inc(stats_done, 1)
    dve.wait_ge(stats_done, NT if known else 2 * NT)


def project_stage(nc, g, name, src, normalise, d_w, width, dest, d_bias=None, xn=None, xt=None,
                  d_extra=None, extra=None, d_cols=None, cols=(), known=False):
    with Stage(nc, name) as st:
        w = st.sb("w", [P, DC, width])
        bias = st.sb("bias", [P, width]) if d_bias is not None else None
        wx = st.sb("wx", [P, DC, extra.shape[2]]) if extra is not None else None
        wc = st.sb("wc", [P, DC, d_cols[0].shape[2]]) if d_cols else None
        wcs = [st.sb(f"wcs{part}", wc.shape, F32R) for part in range(2)] if d_cols else None
        bc = st.sb("bc", [P, d_cols[1].shape[1]]) if d_cols and d_cols[1] is not None else None
        stats = g.stats if known else st.sb("stats", [P, NT, 6])
        mv = st.sb("mv", [P, NT, 2])
        rstd = st.sb("rstd", [P, NT])
        xb = [st.sb(f"xb{u}", [P, D]) for u in range(2)]
        xtb = [st.sb(f"xtb{u}", [P, DC, P]) for u in range(2)]
        turned = [st.banks(f"turned{u}", 1) for u in range(2)]
        prod = [st.banks(f"prod{u}", 1) for u in range(2)]
        ring = [st.banks(f"ring{u}", 1) for u in range(4)]
        w_in = st.sem("w_in")
        stats_done, root_asked, root_ready, rstd_step = (
            st.sem(x) for x in ("stats_done", "root_asked", "root_ready", "rstd_step"))
        root = st.sb("root", [P, 3, NT])
        rows_ready, turn_ready, xt_ready, prod_ready, prod_taken, kept = (
            st.sems(x) for x in ("rows_ready", "turn_ready", "xt_ready", "prod_ready", "prod_taken", "kept"))
        kept_high, kept_low, wc_high, wc_low, ring_ready, split_high = (st.sem(x) for x in (
            "kept_high", "kept_low", "wc_high", "wc_low", "ring_ready", "split_high"))
        ring_free = [st.sem(f"ring_free{n}") for n in range(4)]
        n_loads = 1 + (d_bias is not None) + (extra is not None) + (
            0 if not d_cols else 1 + (d_cols[1] is not None))
        parted = len(dest.shape) == 5
        by_vector = parted or bias is not None
        part_high = st.sem("part_high")
        jobs = []
        m = 0
        for dst, tokens, biased, split in cols:
            for c in range(dst.shape[1] // (2 if split else 1)):
                for a in range(0, tokens, BANK):
                    jobs.append((m, dst, c, a, min(BANK, tokens - a), biased, split))
                m += 1
        split_at = [n for n, job in enumerate(jobs) if job[-1]]

        def halves(n):
            _, dst, c, a, size, _, _ = jobs[n]
            for e in range(2):
                yield (ring[n % 4][e * HD:(e + 1) * HD, 0:size], dst[0:HD, 2 * c + e, a:a + size],
                       dst[HD:2 * HD, 2 * c + e, a:a + size])

        block = st.block()

        @block.sync
        def _(sp):
            sp.dma_start(w[:, :, :], d_w).then_inc(w_in, 16)
            if bias is not None:
                sp.dma_start(bias[:, :], d_bias.to_broadcast([P, width])).then_inc(w_in, 16)
            if extra is not None:
                sp.dma_start(wx[:, :, :], d_extra).then_inc(w_in, 16)
            if d_cols:
                sp.dma_start(wc[:, :, :], d_cols[0]).then_inc(w_in, 16)
                if d_cols[1] is not None:
                    sp.dma_start(bc[:, :], d_cols[1]).then_inc(w_in, 16)
            sp.wait_ge(w_in, 16 * n_loads)

        @block.vector
        def _(dve):
            if normalise:
                take_stats(dve, stats, src, mv, stats_done, known)
                inverse_root(dve, rstd, mv[:, :, 1], root, root_asked, root_ready, rstd_step)

            def rows(t, _):
                i, s, u = t
                dve.wait_ge(turn_ready[u], s)
                if xn is not None:
                    dve.wait_ge(kept[u], s)
                if normalise:
                    dve.tensor_scalar(xb[u][:, :], src[:, i, :], mv[:, i, 0:1], rstd[:, bass.ds(i, 1)],
                                      ALU.subtract, ALU.mult).then_inc(rows_ready[u], 1)
                else:
                    dve.tensor_copy(xb[u][:, :], src[:, i, :]).then_inc(rows_ready[u], 1)

            def product_out(t):
                i, s, u = t
                if parted:
                    dve.wait_ge(part_high, i + 1)
                    high, low = dest[:, bass.ds(i, 1), :, 0, :], dest[:, bass.ds(i, 1), :, 1, :]
                    dve.tensor_tensor(low, prod[u][:, 0:width].rearrange("p (a h k) -> p a h k", a=1, k=dest.shape[4]),
                                      high.bitcast(F32), ALU.subtract).then_inc(prod_taken[u], 1)
                else:
                    dve.wait_ge(prod_ready[u], s + 1)
                    dve.tensor_tensor(dest[:, i, :], prod[u][:, 0:width], bias[:, :], ALU.add) \
                       .then_inc(prod_taken[u], 1)

            def keep_low(t):
                i, s, u = t
                dve.wait_ge(kept_high, i + 1)
                high, low = (x[:, :, bass.ts(i, P)] for x in xt)
                dve.tensor_tensor(low, turned[u][:, 0:D].rearrange("p (c n) -> p c n", c=DC), high.bitcast(F32),
                                  ALU.subtract).then_inc(kept_low, 1)

            def body(t, prev):
                i, s, u = t
                if prev is None:
                    rows(t, None)
                if not (isinstance(i, int) and i == NT - 1):
                    rows((i + 1, s + u, 1 - u), None)
                if xt is not None:
                    keep_low(t)
                if by_vector and prev is not None:
                    product_out(prev)

            if bias is not None:
                dve.wait_ge(w_in, 16 * n_loads)
            last = tiles(dve, NT, body)
            if by_vector:
                product_out(last)
            for n in range(0 if wc is None else wc.shape[2] // P):
                own = slice(n * P, (n + 1) * P)
                dve.wait_ge(wc_high, 1)
                dve.tensor_tensor(wcs[1][:, :, own], wc[:, :, own], wcs[0][:, :, own].bitcast(F32), ALU.subtract) \
                   .then_inc(wc_low, 1)
            for n, (m, dst, c, a, size, biased, split) in enumerate(jobs):
                if split:
                    dve.wait_ge(split_high, split_at.index(n) + 1)
                    for rows_, high, low in halves(n):
                        ins = dve.tensor_tensor(low, rows_, high.bitcast(F32), ALU.subtract)
                    ins.then_inc(ring_free[n % 4], 1)
                elif n % 2:
                    dve.wait_ge(ring_ready, n + 1)
                    into = dst[:, c, a:a + size]
                    if biased is None:
                        ins = dve.tensor_copy(into, ring[n % 4][:, 0:size])
                    else:
                        dve.wait_ge(w_in, 16 * n_loads)
                        ins = dve.tensor_scalar(into, ring[n % 4][:, 0:size], bc[:, m:m + 1], None, ALU.add)
                    ins.then_inc(ring_free[n % 4], 1)

        @block.gpsimd
        def _(pool):
            if xn is not None:
                def keep(t, _):
                    i, s, u = t
                    pool.wait_ge(rows_ready[u], s + 1)
                    pool.tensor_copy(xn[:, i, :], xb[u][:, :]).then_inc(kept[u], 1)

                tiles(pool, NT, keep)
                pool.wait_ge(kept[0], NT - NT // 2)
                pool.wait_ge(kept[1], NT // 2)

        @block.tensor
        def _(pe):
            pe.wait_ge(w_in, 16 * n_loads)

            def turn(t):
                i, s, u = t
                pe.wait_ge(rows_ready[u], s + 1)
                pe.wait_ge(xt_ready[u], s)
                if xt is not None and not (isinstance(i, int) and i < 2):
                    pe.wait_ge(kept_low, i - 1)
                for c in range(DC):
                    ins = pe.transpose(turned[u][:, c * P:(c + 1) * P], xb[u][:, c * P:(c + 1) * P], g.ident[:, :])
                ins.then_inc(turn_ready[u], 1)

            def product(t):
                i, s, u = t
                pe.wait_ge(xt_ready[u], s + 1)
                pe.wait_ge(prod_taken[u], s)
                for c in range(DC):
                    ins = pe.matmul(prod[u][:, 0:width], xtb[u][:, c, :], w[:, c, :],
                                    start=(c == 0), stop=(c == DC - 1))
                if extra is not None:
                    m = extra.shape[2]
                    for c in range(DC):
                        ins = pe.matmul(ring[u][:, 0:m], xtb[u][:, c, :], wx[:, c, :],
                                        start=(c == 0), stop=(c == DC - 1))
                ins.then_inc(prod_ready[u], 1)

            def body(t, prev):
                turn(t)
                if prev is not None:
                    product(prev)

            product(tiles(pe, NT, body))
            if jobs:
                pe.wait_ge(kept_low, NT)
                if extra is not None:
                    pe.wait_ge(prod_taken[0], NT - NT // 2)
                    pe.wait_ge(prod_taken[1], NT // 2)
            for n, (m, _, _, a, size, _, _) in enumerate(jobs):
                pe.wait_ge(ring_free[n % 4], n // 4)
                pe.wait_ge(wc_low, m + 1)
                for c in range(DC):
                    ins = parts_product(pe, ring[n % 4][:, 0:size], [x[:, c, m * P:(m + 1) * P] for x in wcs],
                                        [x[:, c, a:a + size] for x in xt], c == 0, c == DC - 1)
                ins.then_inc(ring_ready, 1)

        @block.scalar
        def _(act):
            if normalise:
                act.wait_ge(root_asked, 1)
                act.activation(root[:, 1, :], root[:, 0, :], ACT.Sqrt).then_inc(root_ready, 1)
            if wc is not None:
                act.wait_ge(w_in, 16 * n_loads)
                act.copy(wcs[0][:, :, :], wc[:, :, :]).then_inc(wc_high, 1)

            def turn_out(t):
                i, s, u = t
                act.wait_ge(turn_ready[u], s + 1)
                act.wait_ge(prod_ready[u], s)
                bank = turned[u][:, 0:D].rearrange("p (c n) -> p c n", c=DC)
                act.copy(xtb[u][:, :, :], bank).then_inc(xt_ready[u], 1)
                if xt is not None:
                    act.copy(xt[0][:, :, bass.ts(i, P)], bank).then_inc(kept_high, 1)

            def product_out(t):
                i, s, u = t
                if by_vector and not parted:
                    return
                act.wait_ge(prod_ready[u], s + 1)
                if parted:
                    if extra is not None:
                        act.copy(extra[:, i, :], ring[u][:, 0:extra.shape[2]])
                    act.copy(dest[:, bass.ds(i, 1), :, 0, :],
                             prod[u][:, 0:width].rearrange("p (a h k) -> p a h k", a=1, k=dest.shape[4])) \
                       .then_inc(part_high, 1)
                    return
                ins = act.copy(dest[:, i, :], prod[u][:, 0:width])
                if extra is not None:
                    ins = act.copy(extra[:, i, :], ring[u][:, 0:extra.shape[2]])
                ins.then_inc(prod_taken[u], 1)

            def body(t, prev):
                turn_out(t)
                if prev is not None:
                    product_out(prev)

            product_out(tiles(act, NT, body))
            for n, (m, dst, c, a, size, biased, split) in enumerate(jobs):
                if split:
                    act.wait_ge(ring_ready, n + 1)
                    for rows_, high, low in halves(n):
                        ins = act.copy(high, rows_)
                    ins.then_inc(split_high, 1)
                elif n % 2 == 0:
                    act.wait_ge(ring_ready, n + 1)
                    into = dst[:, c, a:a + size]
                    if biased is None:
                        ins = act.copy(into, ring[n % 4][:, 0:size])
                    else:
                        act.wait_ge(w_in, 16 * n_loads)
                        ins = act.activation(into, ring[n % 4][:, 0:size], ACT.Identity, bias=bc[:, m:m + 1])
                    ins.then_inc(ring_free[n % 4], 1)


CLEAR = 8


def clear_slots(sp, g, d, n):
    rows = d["slot_rows"][n].rearrange("(n p) d -> p n d", p=P)
    for a in range(0, SLOTS[n], CLEAR):
        b = min(a + CLEAR, SLOTS[n])
        sp.dma_start(rows[:, a:b, :], each(g.zeros[:, :], b - a)).then_inc(g.cleared[n], 16)


def attention_stage(nc, g, d, name, qt, kt, v, res, layer):
    scale = float(D) ** -0.5
    with Stage(nc, name) as st:
        adj = [st.sb(f"adj{u}", [P, NP]) for u in range(2)]
        qs = [[st.sb(f"qs{u}{part}", [P, DC, P], F32R) for part in range(2)] for u in range(2)]
        ks = [st.sb(f"ks{part}", [P, DC, N], F32R) for part in range(2)]
        vs = [st.sb(f"vs{part}", [P, NT, D], F32R) for part in range(2)]
        att = st.sb("att", [P, N])
        att_t = [[st.sb(f"att_t{u}{part}", [P, NT, P], F32R) for part in range(2)] for u in range(2)]
        top, neg, total, inv = (st.sb(x, [P, 1]) for x in ("top", "neg", "total", "inv"))
        scores = st.banks("scores", 3)
        turned = [st.banks(f"turned{b}", 1) for b in range(3)]
        out = st.banks("out", 1)
        adj_in, adj_used, qs_ready = st.sems("adj_in"), st.sems("adj_used"), st.sems("qs_ready")
        (scores_ready, top_ready, neg_ready, exp_done, inv_ready, att_ready, out_ready, out_used, res_ready,
         copied_high, copied_low, split_begun, q_high, kv_high, kv_ready) = (st.sem(x) for x in (
             "scores_ready", "top_ready", "neg_ready", "exp_done", "inv_ready", "att_ready", "out_ready",
             "out_used", "res_ready", "copied_high", "copied_low", "split_begun", "q_high", "kv_high", "kv_ready"))
        turn_ready = [st.sem(f"turn_ready{b}") for b in range(3)]
        stats_taken = st.sem("stats_taken")
        block = st.block()
        chunks = [[x[:, :, a:a + size] for x in (kt, *ks)] for a, size in COLS] + [
            [x[:, k0:k1, 0:D] for x in (v, *vs)] for k0, k1 in GROUPS]

        def two_before(t):
            i, s, u = t
            return None if isinstance(i, int) and i < 2 else (i - 2, s - 1, u)

        @block.sync
        def _(sp):
            def body(t, _):
                i, s, u = t
                sp.wait_ge(adj_used[u], s)
                sp.dma_start(adj[u][:, :], d["adj_rows"][bass.ds(i, 1), :, :].rearrange("a p n -> (a p) n")) \
                  .then_inc(adj_in[u], 16)

            tiles(sp, NT, body)
            for n in (0, 1) if layer == 0 else (2,):
                clear_slots(sp, g, d, n)

        @block.gpsimd
        def _(pool):
            def body(t, _):
                i, s, u = t
                pool.wait_ge(scores_ready, 2 * s)
                pool.sem_inc(split_begun, 1)
                high, low = qs[u]
                pool.tensor_copy(high[:, :, :], qt[:, :, bass.ts(i, P)]).then_inc(q_high, 1)
                pool.wait_ge(q_high, i + 1)
                pool.sem_inc(split_begun, 1)
                pool.tensor_tensor(low[:, :, :], qt[:, :, bass.ts(i, P)], high[:, :, :].bitcast(F32), ALU.subtract) \
                    .then_inc(qs_ready[u], 1)
                if layer == 1 and isinstance(i, int) and i == 1:
                    pool.tensor_tensor(g.x[:, :, :], g.x[:, :, :], res[:, :, :], ALU.add).then_inc(res_ready, 1)

            tiles(pool, NT, body)

        @block.tensor
        def _(pe):
            def score(t):
                i, s, u = t
                pe.wait_ge(qs_ready[u], s + 1)
                pe.wait_ge(exp_done, i)
                for b, (a, size) in enumerate(COLS):
                    if isinstance(i, int) and i == 0:
                        pe.wait_ge(kv_ready, b + 1)
                    for c in range(DC):
                        ins = parts_product(pe, scores[:, a:a + size], [x[:, c, :] for x in qs[u]],
                                            [x[:, c, a:a + size] for x in ks], c == 0, c == DC - 1)
                ins.then_inc(scores_ready, 1)

            def turn(t):
                i, s, u = t
                pe.wait_ge(att_ready, i + 1)
                pe.wait_ge(copied_low, 3 * i)
                for b, (k0, k1) in enumerate(GROUPS):
                    for k in range(k0, k1):
                        n = rows_of(k)
                        ins = pe.transpose(turned[b][0:n, (k - k0) * P:(k - k0 + 1) * P],
                                           att[:, k * P:k * P + n], g.ident[:, :])
                    ins.then_inc(turn_ready[b], 1)

            def values(t):
                i, s, u = t
                pe.wait_ge(out_used, i)
                if isinstance(i, int) and i == 0:
                    pe.wait_ge(kv_ready, len(chunks))
                pe.wait_ge(copied_low, 3 * i + 3)
                for k in range(NT):
                    n = rows_of(k)
                    ins = parts_product(pe, out[:, 0:D], [x[0:n, k, :] for x in att_t[u]],
                                        [x[0:n, k, :] for x in vs], k == 0, k == NT - 1)
                ins.then_inc(out_ready, 1)

            def body(t, prev):
                score(t)
                if prev is not None:
                    turn(prev)
                if two_before(t) is not None:
                    values(two_before(t))

            last = tiles(pe, NT, body)
            turn(last)
            values((NT - 2, (NT - 2) // 2, 1))
            values(last)

        def pieces(t, b):
            k0, k1 = GROUPS[b]
            full = k1 - (k1 == NT)
            high, low = att_t[t[2]]
            yield (turned[b][:, 0:(full - k0) * P].rearrange("p (k n) -> p k n", n=P), high[:, k0:full, :],
                   low[:, k0:full, :])
            if full < k1:
                yield (turned[b][0:TAIL, (full - k0) * P:(full - k0 + 1) * P], high[0:TAIL, full, :],
                       low[0:TAIL, full, :])

        @block.scalar
        def _(act):
            for whole, high, _ in chunks:
                act.copy(high, whole).then_inc(kv_high, 1)

            def turned_out(t):
                for b in range(3):
                    act.wait_ge(turn_ready[b], t[0] + 1)
                    for bank, high, _ in pieces(t, b):
                        ins = act.copy(high, bank)
                    ins.then_inc(copied_high, 1)

            def body(t, prev):
                if prev is not None:
                    turned_out(prev)
                act.wait_ge(neg_ready, t[0] + 1)
                act.activation(att[:, :], scores[:, 0:N], ACT.Exp, bias=neg[:, :], scale=scale,
                               accum_out=total[:, :]).then_inc(exp_done, 1)

            turned_out(tiles(act, NT, body))

        @block.vector
        def _(dve):
            def result(t):
                i, s, u = t
                if layer == 1 and isinstance(i, int) and i == 0:
                    dve.wait_ge(res_ready, 1)
                dve.wait_ge(out_ready, i + 1)
                into = res if layer == 0 else g.x
                dve.scalar_tensor_tensor(into[:, i, :], out[:, 0:D], 0.0, into[:, i, :],
                                         ALU.max, ALU.add).then_inc(out_used, 1)
                if layer == 1:
                    dve.wait_ge(out_used, i + 1)
                    dve.sem_inc(split_begun, 1)
                    dve.bn_stats(g.stats[:, i, :], g.x[:, i, :]).then_inc(stats_taken, 1)

            for n, (whole, high, low) in enumerate(chunks):
                dve.wait_ge(kv_high, n + 1)
                dve.tensor_tensor(low, whole, high.bitcast(F32), ALU.subtract).then_inc(kv_ready, 1)

            def turned_out(t):
                for b in range(3):
                    dve.wait_ge(copied_high, 3 * t[0] + b + 1)
                    for bank, high, low in pieces(t, b):
                        ins = dve.tensor_tensor(low, bank, high.bitcast(F32), ALU.subtract)
                    ins.then_inc(copied_low, 1)

            def body(t, prev):
                i, s, u = t
                dve.wait_ge(scores_ready, i + 1)
                dve.tensor_reduce(top[:, :], scores[:, 0:N], AX, ALU.max).then_inc(top_ready, 1)
                dve.wait_ge(top_ready, i + 1)
                dve.tensor_scalar(neg[:, :], top[:, :], -scale, None, ALU.mult).then_inc(neg_ready, 1)
                if prev is not None:
                    turned_out(prev)
                dve.wait_ge(exp_done, i + 1)
                dve.reciprocal(inv[:, :], total[:, :]).then_inc(inv_ready, 1)
                dve.wait_ge(inv_ready, i + 1)
                dve.wait_ge(adj_in[u], 16 * (s + 1))
                dve.scalar_tensor_tensor(att[:, :], att[:, :], inv[:, 0:1], adj[u][:, 0:N],
                                         ALU.mult, ALU.add).then_inc(att_ready, 1)
                dve.wait_ge(att_ready, i + 1)
                dve.sem_inc(adj_used[u], 1)
                if two_before(t) is not None:
                    result(two_before(t))

            last = tiles(dve, NT, body)
            turned_out(last)
            result((NT - 2, (NT - 2) // 2, 1))
            result(last)


def norm_rows(dve, src, dst, stats, mv, rstd, root, sems, known):
    stats_done, root_asked, root_ready, rstd_step, rows_done = sems
    take_stats(dve, stats, src, mv, stats_done, known)
    inverse_root(dve, rstd, mv[:, :, 1], root, root_asked, root_ready, rstd_step)
    for i in range(NT):
        dve.tensor_scalar(dst[:, i, :], src[:, i, :], mv[:, i, 0:1], rstd[:, i:i + 1],
                          ALU.subtract, ALU.mult).then_inc(rows_done, 1)
    dve.wait_ge(rows_done, NT)


def norm_memory(st):
    return (st.sb("mv", [P, NT, 2]), st.sb("rstd", [P, NT]), st.sb("root", [P, 3, NT]),
            [st.sem(x) for x in ("stats_done", "root_asked", "root_ready", "rstd_step", "rows_done")])


def over(ap, n):
    return ap.unsqueeze(2).to_broadcast([ap.shape[0], ap.shape[1], n])


def each(ap, n):
    return ap.unsqueeze(1).to_broadcast([ap.shape[0], n, ap.shape[1]])


def route_stage(nc, g, name, experts, slots, logits, xn, slot_rows, cleared, weights, r, over_all):
    E = experts
    with Stage(nc, name) as st:
        best = st.sb("best", [P, NT, 8])
        at = st.sb("at", [P, NT, 8], U32)
        atf = st.sb("atf", [P, NT, 2])
        hot = [st.sb(f"hot{k}", [P, NT, E]) for k in range(2)]
        either = st.sb("either", [P, NT, E])
        pos = st.sb("pos", [P, NT, E])
        pick = [st.sb(f"pick{k}", [P, NT, E]) for k in range(2)]
        base = st.sb("base", [P, NT + 1, E])
        cnt_i = st.sb("cnt_i", [P, E], I32)
        cnt, upto, first = (st.sb(x, [P, E]) for x in ("cnt", "upto", "first"))
        slot_f = st.sb("slot_f", [P, 2, NT])
        below = st.sb("below", [1, slots, E])
        own = st.sb("own", [1, slots])
        shifted = st.sb("shifted", [P, NT, E])
        gap, den = st.sb("gap", [P, NT]), st.sb("den", [P, NT])
        rank, total = st.banks("rank", 1), st.banks("total", 1)
        step, picked, counted, exp_asked, exp_done, slots_ready, sent = (
            st.sem(x) for x in ("step", "picked", "counted", "exp_asked", "exp_done", "slots_ready", "sent"))
        block = st.block()

        @block.sync
        def _(sp):
            for e in range(2):
                if e:
                    sp.wait_ge(weights.up_in, 16)
                weights.load_up(sp, e, e)
                if e:
                    sp.wait_ge(weights.down_in, 16 * weights.parts)
                weights.load_down(sp, e, e)

        @block.vector
        def _(dve):
            done = [0]

            def then(ins):
                done[0] += 1
                ins.then_inc(step, 1)
                dve.wait_ge(step, done[0])

            for i in range(NT):
                done[0] += 1
                dve.max(best[:, i, :], logits[:, i, :]).then_inc(step, 1)
            for i in range(NT):
                dve.wait_ge(step, i + 1)
                done[0] += 1
                dve.max_index(at[:, i, :], best[:, i, :], logits[:, i, :]).then_inc(step, 1)
            dve.wait_ge(step, done[0])
            then(dve.tensor_copy(atf[:, :, :], at[:, :, 0:2]))
            then(dve.tensor_tensor(atf[:, :, :], atf[:, :, :], over(g.past_end[:, :], 2), ALU.add))
            for k in range(2):
                then(dve.tensor_tensor(hot[k][:, :, :], each(g.iota[:, 0:E], NT), over(atf[:, :, k], E),
                                       ALU.is_equal))
            dve.tensor_tensor(either[:, :, :], hot[0][:, :, :], hot[1][:, :, :], ALU.add).then_inc(picked, 1)
            dve.tensor_tensor(gap[:, :], best[:, :, 1], best[:, :, 0], ALU.subtract).then_inc(exp_asked, 1)
            if over_all:
                dve.tensor_tensor(shifted[:, :, :], logits[:, :, :], over(best[:, :, 0], E), ALU.subtract) \
                   .then_inc(exp_asked, 1)
            then(dve.memset(base[:, 0, :], 0.0))
            dve.wait_ge(counted, 1)
            for i in range(NT):
                then(dve.tensor_tensor(base[:, i + 1, :], base[:, i, :], total[:, i * E:(i + 1) * E], ALU.add))
            then(dve.tensor_scalar(cnt_i[:, :], base[:, NT, :], float(P - 1), None, ALU.add))
            then(dve.tensor_scalar(cnt_i[:, :], cnt_i[:, :], P.bit_length() - 1, None, ALU.arith_shift_right))
            then(dve.tensor_copy(cnt[:, :], cnt_i[:, :]))
            then(dve.tensor_tensor_scan(upto[:, :], g.ones[:, 0:E], cnt[:, :], 0.0, ALU.mult, ALU.add))
            then(dve.tensor_tensor(first[:, :], upto[:, :], cnt[:, :], ALU.subtract))
            then(dve.scalar_tensor_tensor(pos[:, :, :], each(first[:, :], NT), float(P), base[:, 0:NT, :],
                                          ALU.mult, ALU.add))
            then(dve.tensor_tensor(pos[:, :, :], pos[:, :, :],
                                   rank[:, 0:NT * E].rearrange("p (n e) -> p n e", e=E), ALU.add))
            for k in range(2):
                then(dve.tensor_tensor(pick[k][:, :, :], hot[k][:, :, :], pos[:, :, :], ALU.mult))
                then(dve.tensor_reduce(slot_f[:, k, :], pick[k][:, :, :], AX, ALU.add))
            dve.tensor_copy(r.slot[:, :, :], slot_f[:, :, :]).then_inc(slots_ready, 1)
            then(dve.tensor_tensor(below[:, :, :], each(upto[0:1, :], slots), over(g.iota[0:1, 0:slots], E), ALU.is_le))
            then(dve.tensor_reduce(own[:, :], below[:, :, :], AX, ALU.add))
            then(dve.tensor_scalar(r.expert[:, :], own[:, :], float(E - 1), None, ALU.min))
            then(dve.tensor_scalar(r.side[:, :], r.expert[:, :], 1, None, ALU.bitwise_and))
            then(dve.tensor_copy(r.upto[:, :], upto[0:1, :]))
            dve.wait_ge(exp_done, 1 + over_all)
            if over_all:
                then(dve.tensor_reduce(den[:, :], shifted[:, :, :], AX, ALU.add))
            else:
                then(dve.tensor_scalar(den[:, :], gap[:, :], 1.0, None, ALU.add))
            then(dve.reciprocal(r.weight[:, 0, :], den[:, :]))
            then(dve.tensor_tensor(r.weight[:, 1, :], r.weight[:, 0, :], gap[:, :], ALU.mult))

        @block.scalar
        def _(act):
            act.wait_ge(exp_asked, 1 + over_all)
            act.activation(gap[:, :], gap[:, :], ACT.Exp).then_inc(exp_done, 1)
            if over_all:
                act.activation(shifted[:, :, :], shifted[:, :, :], ACT.Exp).then_inc(exp_done, 1)

        @block.tensor
        def _(pe):
            pe.wait_ge(picked, 1)
            flat = either[:, :, :].rearrange("p n e -> p (n e)")
            pe.matmul(rank[:, 0:NT * E], g.before[:, :], flat, start=True, stop=True)
            pe.matmul(total[:, 0:NT * E], g.ones[:, :], flat, start=True, stop=True).then_inc(counted, 1)

        @block.gpsimd
        def _(pool):
            pool.wait_ge(slots_ready, 1)
            pool.wait_ge(cleared, 16 * -(-slots // CLEAR))
            for i in range(NT):
                n = rows_of(i)
                for k in range(2):
                    pool.indirect_dma_start(
                        out=slot_rows[:, :], out_offset=bass.IndirectOffsetOnAxis(ap=r.slot[0:n, k, i:i + 1], axis=0),
                        in_=xn[0:n, i, :], in_offset=None).then_inc(sent, 16)
            pool.wait_ge(sent, 32 * NT)


def expert_stage(nc, g, name, experts, hidden, gated, slots, slot_rows, slot_out, weights, r):
    H = hidden
    U = 2 * H if gated else H
    KH = H // P
    biased = weights.d_bias is not None
    UW, DW = weights.up.shape[2], weights.down.shape[2]
    UP_CUT = U if gated else U // 4
    HALVES = [(0, 4), (4, KH)]
    with Stage(nc, name) as st:
        up = [st.sb(f"up{u}", [P, UW]) for u in range(2)]
        down = [[st.sb(f"down{u}{part}", [P, KH * D], F32R) for part in range(2)] for u in range(2)]
        down_bias = [st.sb(f"down_bias{u}", [P, D]) for u in range(2)] if biased else None
        rows = [st.sb(f"rows{u}", [P, D]) for u in range(2)]
        rows_t = [st.sb(f"rows_t{u}", [P, DC, P]) for u in range(2)]
        half = st.sb("half", [P, KH, P]) if gated else None
        h = st.sb("h", [P, KH, P])
        h_t = [[st.sb(f"h_t{u}{part}", [P, KH, P], F32R) for part in range(2)] for u in range(2)]
        y = [st.sb(f"y{u}", [P, D]) for u in range(2)]
        pup = [[st.banks(f"pup{b}{k}", 1) for k in range(1 + gated)] for b in range(2)]
        prow, pout = st.banks("prow", 1), st.banks("pout", 1)
        rows_in, up_used, down_used, rows_used, y_stored = (st.sems(x) for x in (
            "rows_in", "up_used", "down_used", "rows_used", "y_stored"))
        hidden_ready, half_ready, h_taken, h_high, h_ready = (st.sems(x) for x in (
            "hidden_ready", "half_ready", "h_taken", "h_high", "h_ready"))
        rows_t_ready, y_ready = st.sem("rows_t_ready"), st.sem("y_ready")
        up_act, up_dve, down_act, down_dve = (st.sem(x) for x in ("up_act", "up_dve", "down_act", "down_dve"))
        load_begun = st.sem("load_begun")
        block = st.block()

        def is_last(t):
            return isinstance(t[0], int) and t[0] == slots - 1

        def following(t):
            j, s, u = t
            return j + 1, s + u, 1 - u

        @block.sync
        def _(sp):
            def wait(sem, value):
                sp.wait_ge(sem, value)
                sp.sem_inc(load_begun, 1)

            def load(e, u):
                before = sp.value_load(r.upto[0:1, bass.ds(e - 2, 1)], min_val=0, max_val=slots)
                wait(up_act, before + 1)
                wait(up_dve, before + 1)
                wait(weights.up_in, 16 * e)
                weights.load_up(sp, e, u)
                wait(down_act, before + 1)
                wait(down_dve, before + 1)
                wait(weights.down_in, 16 * weights.parts * e)
                weights.load_down(sp, e, u)

            with sp.Fori(1, experts // 2) as pair:
                load(2 * pair, 0)
                load(2 * pair + 1, 1)

        def copy_up(eng, copy, a, b, done, t, e, side):
            j, s, u = t
            eng.wait_ge(weights.up_in, 16 * (e + 1))
            eng.wait_ge(up_used[u], s)
            if biased:
                if not (isinstance(j, int) and j < 2):
                    for bank in range(2):
                        eng.wait_ge(h_taken[bank], j - 1)
            copy(up[u][:, a:b].unsqueeze(1), weights.up[:, bass.ds(side, 1), a:b]).then_inc(done, 1)

        def down_free(eng, t, e):
            j, s, u = t
            eng.wait_ge(weights.down_in, 16 * weights.parts * (e + 1))
            eng.wait_ge(down_used[u], s)

        def expert_of(eng, t):
            at = bass.ds(t[0], 1)
            return (eng.value_load(r.expert[0:1, at], min_val=0, max_val=experts - 1),
                    eng.value_load(r.side[0:1, at], min_val=0, max_val=1))

        @block.tensor
        def _(pe):
            def turn_rows(t):
                j, s, u = t
                pe.wait_ge(rows_in[u], 16 * (s + 1))
                pe.wait_ge(rows_t_ready, j)
                for c in range(DC):
                    ins = pe.transpose(prow[:, c * P:(c + 1) * P], rows[u][:, c * P:(c + 1) * P], g.ident[:, :])
                ins.then_inc(rows_used[u], 1)

            def go_up(t):
                j, s, u = t
                pe.wait_ge(rows_t_ready, j + 1)
                pe.wait_ge(up_act, j + 2)
                pe.wait_ge(up_dve, j + 2)
                for b, (m0, m1) in enumerate(HALVES):
                    pe.wait_ge(h_taken[b], j)
                    for k in range(1 + gated):
                        for m in range(m0, m1):
                            for c in range(DC):
                                w = c * U + k * H + m * P
                                ins = pe.matmul(pup[b][k][:, (m - m0) * P:(m - m0 + 1) * P], up[u][:, w:w + P],
                                                rows_t[u][:, c, :], start=(c == 0), stop=(c == DC - 1))
                    ins.then_inc(hidden_ready[b], 1)
                pe.sem_inc(up_used[u], 1)

            def go_down(t):
                j, s, u = t
                pe.wait_ge(down_act, j + 2)
                pe.wait_ge(down_dve, j + 2)
                pe.wait_ge(y_ready, j)
                for b, (k0, k1) in enumerate(HALVES):
                    pe.wait_ge(h_ready[b], j + 1)
                    for k in range(k0, k1):
                        ins = parts_product(pe, pout[:, 0:D], [x[:, k, :] for x in h_t[u]],
                                            [x[:, k * D:(k + 1) * D] for x in down[u]], k == 0, k == KH - 1)
                ins.then_inc(down_used[u], 1)

            def body(t, prev):
                if prev is None:
                    turn_rows(t)
                go_up(t)
                if not is_last(t):
                    turn_rows(following(t))
                if prev is not None:
                    go_down(prev)

            go_down(tiles(pe, slots, body))

        @block.scalar
        def _(act):
            act.sem_inc(up_act, 1)
            act.sem_inc(down_act, 1)

            def rows_out(t):
                j, s, u = t
                act.wait_ge(rows_used[u], s + 1)
                act.wait_ge(up_used[u], s)
                act.copy(rows_t[u][:, :, :], prow[:, 0:D].rearrange("p (c n) -> p c n", c=DC)) \
                   .then_inc(rows_t_ready, 1)

            def result_out(t):
                j, s, u = t
                act.wait_ge(down_used[u], s + 1)
                act.wait_ge(y_stored[u], 16 * s)
                act.copy(y[u][:, :], pout[:, 0:D]).then_inc(y_ready, 1)

            def hidden_out(t, b):
                j, s, u = t
                m0, m1 = HALVES[b]
                act.wait_ge(hidden_ready[b], j + 1)
                if gated:
                    act.activation(half[:, m0:m1, :], pup[b][0][:, 0:(m1 - m0) * P].rearrange("p (k n) -> p k n", n=P),
                                   ACT.Silu).then_inc(half_ready[b], 1)
                elif b == 0:
                    act.wait_ge(h_ready[b], j)
                    for m in range(m0, m1):
                        ins = act.activation(h[:, m, :], pup[b][0][:, (m - m0) * P:(m - m0 + 1) * P], ACT.Relu,
                                             bias=up[u][:, DC * U + m:DC * U + m + 1])
                    ins.then_inc(h_taken[b], 1)

            def hidden_high(t, b):
                j, s, u = t
                m0, m1 = HALVES[b]
                act.wait_ge(h_taken[b], j + 1)
                act.copy(h_t[u][0][:, m0:m1, :], h[:, m0:m1, :]).then_inc(h_high[b], 1)

            def copy_down(t, e, side):
                down_free(act, t, e)
                act.copy(down[t[2]][0][:, :].unsqueeze(1), weights.down[:, bass.ds(side, 1), 0:KH * D]) \
                   .then_inc(down_act, 1)

            def body(t, prev):
                if prev is None:
                    e, side = expert_of(act, t)
                    rows_out(t)
                    copy_up(act, act.copy, UP_CUT, UW, up_act, t, e, side)
                    copy_down(t, e, side)
                if not is_last(t):
                    e, side = expert_of(act, following(t))
                    copy_up(act, act.copy, UP_CUT, UW, up_act, following(t), e, side)
                hidden_out(t, 0)
                if gated:
                    hidden_out(t, 1)
                if not is_last(t):
                    rows_out(following(t))
                for b in range(2):
                    hidden_high(t, b)
                if gated and prev is not None:
                    result_out(prev)
                if not is_last(t):
                    copy_down(following(t), e, side)

            last = tiles(act, slots, body)
            if gated:
                result_out(last)

        @block.vector
        def _(dve):
            dve.sem_inc(up_dve, 1)
            dve.sem_inc(down_dve, 1)

            def result_out(t):
                j, s, u = t
                dve.wait_ge(down_used[u], s + 1)
                dve.wait_ge(y_stored[u], 16 * s)
                dve.tensor_tensor(y[u][:, :], pout[:, 0:D], down_bias[u][:, :], ALU.add).then_inc(y_ready, 1)

            def hidden_out(t, b):
                j, s, u = t
                m0, m1 = HALVES[b]
                if gated:
                    dve.wait_ge(half_ready[b], j + 1)
                    dve.wait_ge(h_ready[b], j)
                    dve.tensor_tensor(h[:, m0:m1, :], half[:, m0:m1, :],
                                      pup[b][1][:, 0:(m1 - m0) * P].rearrange("p (k n) -> p k n", n=P), ALU.mult) \
                       .then_inc(h_taken[b], 1)
                elif b == 1:
                    dve.wait_ge(hidden_ready[b], j + 1)
                    dve.wait_ge(h_ready[b], j)
                    for m in range(m0, m1):
                        ins = dve.tensor_scalar(h[:, m, :], pup[b][0][:, (m - m0) * P:(m - m0 + 1) * P],
                                                up[u][:, DC * U + m:DC * U + m + 1], 0.0, ALU.add, ALU.max)
                    ins.then_inc(h_taken[b], 1)

            def hidden_low(t, b):
                j, s, u = t
                m0, m1 = HALVES[b]
                dve.wait_ge(h_high[b], j + 1)
                dve.tensor_tensor(h_t[u][1][:, m0:m1, :], h[:, m0:m1, :], h_t[u][0][:, m0:m1, :].bitcast(F32),
                                  ALU.subtract).then_inc(h_ready[b], 1)

            def copy_down(t, e, side):
                j, s, u = t
                down_free(dve, t, e)
                if biased:
                    if not (isinstance(j, int) and j < 2):
                        dve.wait_ge(y_ready, j - 1)
                    dve.tensor_copy(down_bias[u][:, :].unsqueeze(1), weights.down[:, bass.ds(side, 1), KH * D:DW])
                dve.wait_ge(down_act, j + 2)
                high, low = down[u]
                dve.tensor_tensor(low[:, :].unsqueeze(1), weights.down[:, bass.ds(side, 1), 0:KH * D],
                                  high[:, :].bitcast(F32).unsqueeze(1), ALU.subtract).then_inc(down_dve, 1)

            def body(t, prev):
                if prev is None:
                    e, side = expert_of(dve, t)
                    copy_up(dve, dve.tensor_copy, 0, UP_CUT, up_dve, t, e, side)
                    copy_down(t, e, side)
                if not is_last(t):
                    e, side = expert_of(dve, following(t))
                    copy_up(dve, dve.tensor_copy, 0, UP_CUT, up_dve, following(t), e, side)
                hidden_out(t, 0)
                hidden_out(t, 1)
                hidden_low(t, 0)
                hidden_low(t, 1)
                if prev is not None and biased:
                    result_out(prev)
                if not is_last(t):
                    copy_down(following(t), e, side)

            last = tiles(dve, slots, body)
            if biased:
                result_out(last)

        @block.gpsimd
        def _(pool):
            def load(j, u):
                pool.dma_start(rows[u][:, :], slot_rows.rearrange("(n p) d -> n p d", p=P)[bass.ds(j, 1), :, :]
                               .rearrange("a p d -> (a p) d")).then_inc(rows_in[u], 16)

            def store(t):
                j, s, u = t
                pool.wait_ge(y_ready, j + 1)
                pool.dma_start(slot_out.rearrange("(n p) d -> n p d", p=P)[bass.ds(j, 1), :, :]
                               .rearrange("a p d -> (a p) d"), y[u][:, :]).then_inc(y_stored[u], 16)

            def body(t, prev):
                j, s, u = t
                if not (isinstance(j, int) and j >= slots - 2):
                    pool.wait_ge(rows_used[u], s + 1)
                    load(j + 2, u)
                if prev is not None:
                    store(prev)

            load(0, 0)
            load(1, 1)
            store(tiles(pool, slots, body))
            pool.wait_ge(y_stored[0], 16 * (slots - slots // 2))
            pool.wait_ge(y_stored[1], 16 * (slots // 2))


def combine_stage(nc, g, name, slot_out, r, xn=None, d_gain=None, d_offset=None, result=None):
    with Stage(nc, name) as st:
        got = st.sb("got", [P, 2, NT, D])
        mv, rstd, root, sems = norm_memory(st)
        gain, offset = (st.sb("gain", [P, D]), st.sb("offset", [P, D])) if xn is not None else (None, None)
        fetched = [st.sem(f"fetched{i}") for i in range(NT)]
        step, loaded, stored = st.sem("step"), st.sem("loaded"), st.sem("stored")
        block = st.block()
        into = xn if xn is not None else g.x

        @block.gpsimd
        def _(pool):
            for i in range(NT):
                for k in range(2):
                    pool.indirect_dma_start(
                        out=got[:, k, i, :], out_offset=None, in_=slot_out[:, :],
                        in_offset=bass.IndirectOffsetOnAxis(ap=r.slot[:, k, i:i + 1], axis=0)) \
                        .then_inc(fetched[i], 16)
            for i in range(NT):
                pool.wait_ge(fetched[i], 32)

        @block.sync
        def _(sp):
            if xn is not None:
                sp.dma_start(gain[:, :], d_gain.to_broadcast([P, D])).then_inc(loaded, 16)
                sp.dma_start(offset[:, :], d_offset.to_broadcast([P, D])).then_inc(loaded, 16)
            if result is not None:
                for k0, k1 in GROUPS:
                    full = k1 - (k1 == NT)
                    sp.wait_ge(step, 3 * k1)
                    sp.dma_start(result[k0 * P:full * P, :].rearrange("(n p) d -> p n d", p=P), g.x[:, k0:full, :]) \
                      .then_inc(stored, 16)
                sp.dma_start(result[(NT - 1) * P:N, :], g.x[0:TAIL, NT - 1, :]).then_inc(stored, 16)
                sp.wait_ge(stored, 16 * (len(GROUPS) + 1))

        @block.scalar
        def _(act):
            if xn is not None:
                act.wait_ge(sems[1], 1)
                act.activation(root[:, 1, :], root[:, 0, :], ACT.Sqrt).then_inc(sems[2], 1)

        @block.vector
        def _(dve):
            for i in range(NT):
                dve.wait_ge(fetched[i], 32)
                for k in range(2):
                    dve.scalar_tensor_tensor(into[:, i, :], got[:, k, i, :], r.weight[:, k, i:i + 1], into[:, i, :],
                                             ALU.mult, ALU.add).then_inc(step, 1)
                    dve.wait_ge(step, 3 * i + k + 1)
                dve.bn_stats(g.stats[:, i, :], into[:, i, :]).then_inc(step, 1)
            dve.wait_ge(step, 3 * NT)
            if xn is not None:
                out = got[:, 0, :, :]
                norm_rows(dve, xn, out, g.stats, mv, rstd, root, sems, known=True)
                dve.wait_ge(loaded, 32)
                n = 3 * NT
                for other, op in ((each(gain[:, :], NT), ALU.mult), (each(offset[:, :], NT), ALU.add)):
                    dve.tensor_tensor(out, out, other, op).then_inc(step, 1)
                    n += 1
                    dve.wait_ge(step, n)
                dve.tensor_tensor(g.x[:, :, :], g.x[:, :, :], out, ALU.add).then_inc(step, 1)
                dve.wait_ge(step, n + 1)


def spread_stage(nc, g, d, name, hidden, d_bias):
    with Stage(nc, name) as st:
        adj = [st.sb(f"adj{u}", [P, NT, P]) for u in range(2)]
        parts = [[st.sb(f"parts{u}{part}", [P, NT, P], F32R) for part in range(2)] for u in range(2)]
        bias = st.sb("bias", [P, D])
        sum_ = st.sb("sum", [P, D])
        out = [st.banks(f"out{u}", 1) for u in range(2)]
        adj_in, out_ready, out_used, low_ready = (st.sems(x) for x in ("adj_in", "out_ready", "out_used", "low_ready"))
        high_ready = st.sem("high_ready")
        bias_in, added, begun = st.sem("bias_in"), st.sem("added"), st.sem("begun")
        block = st.block()

        @block.sync
        def _(sp):
            sp.dma_start(bias[:, :], d_bias.to_broadcast([P, D])).then_inc(bias_in, 16)

            def body(t, _):
                i, s, u = t
                sp.wait_ge(low_ready[u], s)
                sp.dma_start(adj[u][:, :, :], d["adj_t"][bass.ds(i, 1), :, :, :].rearrange("a p k n -> (a p) k n")) \
                  .then_inc(adj_in[u], 16)

            tiles(sp, NT, body)

        @block.tensor
        def _(pe):
            def body(t, _):
                i, s, u = t
                pe.wait_ge(low_ready[u], s + 1)
                pe.wait_ge(out_used[u], s)
                for k in range(NT):
                    n = rows_of(k)
                    ins = parts_product(pe, out[u][:, 0:D], [x[0:n, k, :] for x in parts[u]],
                                        [hidden[0:n, k, 0, part, :] for part in range(2)], k == 0, k == NT - 1)
                ins.then_inc(out_ready[u], 1)

            tiles(pe, NT, body)

        @block.scalar
        def _(act):
            def body(t, _):
                i, s, u = t
                act.wait_ge(adj_in[u], 16 * (s + 1))
                act.wait_ge(out_ready[u], s)
                act.copy(parts[u][0][:, :, :], adj[u][:, :, :]).then_inc(high_ready, 1)

            tiles(act, NT, body)

        @block.vector
        def _(dve):
            def split_low(t):
                i, s, u = t
                dve.wait_ge(high_ready, i + 1)
                high, low = parts[u]
                dve.tensor_tensor(low[:, :, :], adj[u][:, :, :], high[:, :, :].bitcast(F32), ALU.subtract) \
                   .then_inc(low_ready[u], 1)

            def body(t, prev):
                split_low(t)
                if prev is not None:
                    result(prev)

            def result(t):
                i, s, u = t
                dve.wait_ge(out_ready[u], s + 1)
                dve.tensor_tensor(sum_[:, :], out[u][:, 0:D], bias[:, :], ALU.add).then_inc(out_used[u], 1)
                dve.wait_ge(out_used[u], s + 1)
                dve.tensor_tensor(g.x[:, i, :], g.x[:, i, :], sum_[:, :], ALU.add).then_inc(added, 1)
                dve.wait_ge(added, 2 * i + 1)
                dve.sem_inc(begun, 1)
                dve.bn_stats(g.stats[:, i, :], g.x[:, i, :]).then_inc(added, 1)

            dve.wait_ge(bias_in, 16)
            result(tiles(dve, NT, body))


def shift_stage(nc, g, name):
    MARK, SHL, SHR, FIELDS, OUT = 0, 39, 40, 64, 128
    W = 16
    with Stage(nc, name) as st:
        y = st.sb("y", [P, NT, D])
        mv, rstd, root, sems = norm_memory(st)
        fall = st.sb("fall", [P, 3, W])
        hot = st.sb("hot", [P, NT, 3, W])
        top = st.sb("top", [P, NT, 3])
        none = st.sb("none", [P, NT, 3])
        value = st.sb("value", [P, NT])
        value_i, by_i, left_i, right_i, low_i, high_i = (
            st.sb(x, [P, NT], I32) for x in ("value_i", "by_i", "left_i", "right_i", "low_i", "high_i"))
        left, right, mark, is_left, is_right, height = (
            st.sb(x, [P, NT]) for x in ("left", "right", "mark", "is_left", "is_right", "height"))
        nibble = st.sb("nibble", [P, 2, NT])
        spot = st.sb("spot", [P, NT, 2, W])
        step = st.sem("step")
        block = st.block()

        @block.scalar
        def _(act):
            act.wait_ge(sems[1], 1)
            act.activation(root[:, 1, :], root[:, 0, :], ACT.Sqrt).then_inc(sems[2], 1)

        @block.vector
        def _(dve):
            norm_rows(dve, g.x, y, g.stats, mv, rstd, root, sems, known=True)
            done = [0]

            def then(ins):
                done[0] += 1
                ins.then_inc(step, 1)
                dve.wait_ge(step, done[0])

            for f in range(3):
                then(dve.tensor_scalar(fall[:, f, :], g.iota[:, 0:W], -1.0, float(W), ALU.mult, ALU.add))
            then(dve.scalar_tensor_tensor(hot[:, :, :, :].rearrange("p n f w -> p n (f w)"),
                                          y[:, :, FIELDS:FIELDS + 3 * W], 0.5,
                                          each(fall[:, :, :].rearrange("p f w -> p (f w)"), NT), ALU.is_gt, ALU.mult))
            then(dve.tensor_reduce(top[:, :, :].rearrange("p n f -> p (n f)"),
                                   hot[:, :, :, :].rearrange("p n f w -> p (n f) w"), AX, ALU.max))
            then(dve.tensor_scalar(none[:, :, :], top[:, :, :], 0.0, float(W), ALU.is_equal, ALU.mult))
            then(dve.tensor_tensor(top[:, :, :], top[:, :, :], none[:, :, :], ALU.add))
            then(dve.tensor_scalar(top[:, :, :], top[:, :, :], -1.0, float(W), ALU.mult, ALU.add))
            then(dve.scalar_tensor_tensor(value[:, :], top[:, :, 1], float(W), top[:, :, 0], ALU.mult, ALU.add))
            then(dve.tensor_copy(value_i[:, :], value[:, :]))
            then(dve.tensor_copy(by_i[:, :], top[:, :, 2]))
            then(dve.tensor_tensor(left_i[:, :], value_i[:, :], by_i[:, :], ALU.logical_shift_left))
            then(dve.tensor_scalar(left_i[:, :], left_i[:, :], W * W - 1, None, ALU.bitwise_and))
            then(dve.tensor_tensor(right_i[:, :], value_i[:, :], by_i[:, :], ALU.logical_shift_right))
            then(dve.tensor_copy(left[:, :], left_i[:, :]))
            then(dve.tensor_copy(right[:, :], right_i[:, :]))
            then(dve.tensor_scalar(mark[:, :], y[:, :, MARK], 0.5, None, ALU.is_gt))
            then(dve.scalar_tensor_tensor(is_left[:, :], y[:, :, SHL], 0.5, mark[:, :], ALU.is_gt, ALU.mult))
            then(dve.scalar_tensor_tensor(is_right[:, :], y[:, :, SHR], 0.5, mark[:, :], ALU.is_gt, ALU.mult))
            then(dve.tensor_tensor(height[:, :], is_left[:, :], is_right[:, :], ALU.max))
            then(dve.tensor_tensor(is_right[:, :], height[:, :], is_left[:, :], ALU.subtract))
            then(dve.tensor_scalar(height[:, :], height[:, :], 2.0, None, ALU.mult))
            then(dve.tensor_tensor(left[:, :], left[:, :], is_left[:, :], ALU.mult))
            then(dve.tensor_tensor(right[:, :], right[:, :], is_right[:, :], ALU.mult))
            then(dve.tensor_tensor(value[:, :], left[:, :], right[:, :], ALU.add))
            then(dve.tensor_copy(value_i[:, :], value[:, :]))
            then(dve.tensor_scalar(low_i[:, :], value_i[:, :], W - 1, None, ALU.bitwise_and))
            then(dve.tensor_scalar(high_i[:, :], value_i[:, :], 4, None, ALU.logical_shift_right))
            then(dve.tensor_copy(nibble[:, 0, :], low_i[:, :]))
            then(dve.tensor_copy(nibble[:, 1, :], high_i[:, :]))
            for f in range(2):
                then(dve.tensor_tensor(spot[:, :, f, :], each(g.iota[:, 0:W], NT), over(nibble[:, f, :], W),
                                       ALU.is_equal))
                then(dve.tensor_tensor(spot[:, :, f, :], spot[:, :, f, :], over(height[:, :], W), ALU.mult))
            then(dve.tensor_tensor(g.x[:, :, :], g.x[:, :, :], y[:, :, :], ALU.add))
            field = g.x[:, :, OUT:OUT + 2 * W]
            then(dve.tensor_tensor(field, field, spot[:, :, :, :].rearrange("p n f w -> p n (f w)"), ALU.add))


def heads_stage(nc, g, d, name, qt, kt, v, d_wo):
    FV = HEADS * HD
    VC = FV // P
    SCALE = float(HD) ** -0.5
    with Stage(nc, name) as st:
        mask = [st.sb(f"mask{u}", [P, NP]) for u in range(2)]
        qs = [st.sb(f"qs{u}", [2 * HD, 2, VC, 2, P], F32R) for u in range(2)]
        wo = st.sb("wo", [2 * HD, HEADS, D])
        p = [st.sb(f"p{x}", [P, N]) for x in range(2)]
        att_t = [st.sb(f"att_t{x}", [P, 2, NT, P], F32R) for x in range(2)]
        o_t = [st.sb(f"o_t{x}", [2 * HD, P]) for x in range(2)]
        neg, total, inv = (st.sb(x, [P, 4]) for x in ("neg", "total", "inv"))
        scores = st.banks("scores", 3)
        turned = [st.banks(f"turned{b}", 1) for b in range(3)]
        out, proj = st.banks("out", 1), st.banks("proj", 1)
        adj_in, mask_ready, mask_used, qs_ready = (st.sems(x) for x in ("adj_in", "mask_ready", "mask_used", "qs_ready"))
        eye_done, wo_in, split_step, scores_ready, masked_ready, exp_done, inv_ready, copied_high, \
            copied_low, out_ready, out_used, proj_ready, proj_used = (st.sem(x) for x in (
                "eye_done", "wo_in", "split_step", "scores_ready", "masked_ready", "exp_done",
                "inv_ready", "copied_high", "copied_low", "out_ready", "out_used", "proj_ready", "proj_used"))
        turn_ready = [st.sem(f"turn_ready{b}") for b in range(3)]
        mask_begun, masked_begun, split_begun = (st.sem(x) for x in ("mask_begun", "masked_begun", "split_begun"))
        first_split = st.sem("first_split")
        block = st.block()

        def lagged(body_head):
            def body(t, prev):
                for h in range(HEADS):
                    old = ((t, h - n) if h >= n else (prev, h + HEADS - n) for n in (1, 2, 3))
                    body_head((t, h), *(x if x[0] is not None else None for x in old))
            return body

        def finish(last, body_head):
            for steps in range(1, 4):
                body_head(None, *((last, HEADS - 1 + steps - n) if n >= steps else None for n in (1, 2, 3)))

        def number(t, h):
            return HEADS * t[0] + h

        @block.sync
        def _(sp):
            sp.dma_start(wo[:, :, :], d_wo).then_inc(wo_in, 16)

            def body(t, _):
                i, s, u = t
                sp.wait_ge(mask_used[u], s)
                sp.dma_start(mask[u][:, :], d["adj_rows"][bass.ds(i, 1), :, :].rearrange("a p n -> (a p) n")) \
                  .then_inc(adj_in[u], 16)

            tiles(sp, NT, body)

        @block.gpsimd
        def _(pool):
            def body(t, _):
                i, s, u = t
                if isinstance(i, int) and i == 0:
                    return
                if not (isinstance(i, int) and i < 2):
                    pool.wait_ge(scores_ready, HEADS * (i - 1))
                    pool.sem_inc(split_begun, 1)
                tile = bass.ts(i, P)
                for e in range(2):
                    own = slice(e * HD, (e + 1) * HD)
                    pool.tensor_copy(qs[u][own, 0, :, e, :], qt[own, :, tile]).then_inc(split_step, 1)
                pool.wait_ge(split_step, 8 * i - 6)
                pool.sem_inc(split_begun, 1)
                for e in range(2):
                    own = slice(e * HD, (e + 1) * HD)
                    pool.tensor_tensor(qs[u][own, 1, :, e, :], qt[own, :, tile], qs[u][own, 0, :, e, :].bitcast(F32),
                                       ALU.subtract).then_inc(split_step, 1)
                pool.wait_ge(split_step, 8 * i - 4)
                pool.sem_inc(split_begun, 1)
                for e in range(2):
                    own, other = slice(e * HD, (e + 1) * HD), slice((1 - e) * HD, (2 - e) * HD)
                    for part in range(2):
                        pool.tensor_copy(qs[u][other, part, :, e, :], qs[u][own, part, :, e, :].bitcast(F32)) \
                            .then_inc(split_step, 1)
                pool.wait_ge(split_step, 8 * i)
                pool.sem_inc(qs_ready[u], 1)
                pool.wait_ge(eye_done, i + 1)
                pool.sem_inc(mask_begun, 1)
                pool.tensor_scalar(mask[u][:, :], mask[u][:, :], 1.0, MASK / SCALE, ALU.subtract, ALU.mult) \
                    .then_inc(mask_ready[u], 1)
                pool.wait_ge(mask_ready[u], s + 1)
                pool.sem_inc(split_begun, 1)

            tiles(pool, NT, body)

        @block.tensor
        def _(pe):
            pe.wait_ge(wo_in, 16)

            def score(t, h):
                i, s, u = t
                if h == 0:
                    pe.wait_ge(qs_ready[u], s + 1)
                pe.wait_ge(masked_ready, number(t, h))
                for part in range(2):
                    for a, size in COLS:
                        ins = pe.matmul(scores[:, a:a + size], qs[u][:, part, h // 2, h % 2, :], kt[:, h, a:a + size],
                                        start=(part == 0), stop=(part == 1))
                ins.then_inc(scores_ready, 1)

            def turn(t, h):
                n = number(t, h)
                pe.wait_ge(exp_done, n + 1)
                for b, (k0, k1) in enumerate(GROUPS):
                    if not (isinstance(n, int) and n == 0):
                        pe.wait_ge(copied_low, 3 * n - 2 + b)
                    for k in range(k0, k1):
                        m = rows_of(k)
                        ins = pe.transpose(turned[b][0:m, (k - k0) * P:(k - k0 + 1) * P],
                                           p[h % 2][:, k * P:k * P + m], g.ident[:, :])
                    ins.then_inc(turn_ready[b], 1)

            def values(t, h):
                n = number(t, h)
                pe.wait_ge(out_used, n)
                pe.wait_ge(copied_low, 3 * n + 3)
                for k in range(NT):
                    m = rows_of(k)
                    ins = pe.matmul(out[:, 0:2 * P], v[0:m, k, h, :, :].rearrange("p a k -> p (a k)"),
                                    att_t[h % 2][0:m, :, k, :], start=(k == 0), stop=(k == NT - 1))
                ins.then_inc(out_ready, 1)

            def project(t, h):
                n = number(t, h)
                pe.wait_ge(out_used, n + 1)
                pe.wait_ge(proj_used, n)
                pe.matmul(proj[:, 0:D], o_t[h % 2][:, :], wo[:, h, :], start=True, stop=True).then_inc(proj_ready, 1)

            def head(new, one, two, three):
                if new is not None:
                    score(*new)
                if one is not None:
                    turn(*one)
                if three is not None:
                    project(*three)
                if two is not None:
                    values(*two)

            finish(tiles(pe, NT, lagged(head)), head)

        def pieces(x, b):
            k0, k1 = GROUPS[b]
            full = k1 - (k1 == NT)
            high, low = att_t[x][:, 0, :, :], att_t[x][:, 1, :, :]
            yield (turned[b][:, 0:(full - k0) * P].rearrange("p (k n) -> p k n", n=P), high[:, k0:full, :],
                   low[:, k0:full, :])
            if full < k1:
                yield (turned[b][0:TAIL, (full - k0) * P:(full - k0 + 1) * P], high[0:TAIL, full, :],
                       low[0:TAIL, full, :])

        @block.scalar
        def _(act):
            def head(new, one, two, three):
                if one is not None:
                    n, h = number(*one), one[1]
                    for b in range(3):
                        act.wait_ge(turn_ready[b], n + 1)
                        for bank, high, _ in pieces(h % 2, b):
                            ins = act.copy(high, bank)
                        ins.then_inc(copied_high, 1)
                if new is not None:
                    n, h = number(*new), new[1]
                    act.wait_ge(masked_ready, n + 1)
                    act.activation(p[h % 2][:, :], p[h % 2][:, :], ACT.Exp, scale=-1.0, bias=neg[:, h % 4:h % 4 + 1],
                                   accum_out=total[:, h % 4:h % 4 + 1]).then_inc(exp_done, 1)

            finish(tiles(act, NT, lagged(head)), head)

        @block.vector
        def _(dve):
            def set_diagonal(t):
                i, s, u = t
                dve.wait_ge(adj_in[u], 16 * (s + 1))
                own = mask[u][:, bass.ts(i, P)]
                dve.tensor_tensor(own, own, g.ident[:, :], ALU.max).then_inc(eye_done, 1)

            for e in range(2):
                for to in range(2):
                    own, into = slice(e * HD, (e + 1) * HD), slice(to * HD, (to + 1) * HD)
                    dve.tensor_copy(qs[0][into, 0, :, e, :], qt[own, :, 0:P]).then_inc(first_split, 1)
            dve.wait_ge(first_split, 4)
            for e in range(2):
                for to in range(2):
                    own, into = slice(e * HD, (e + 1) * HD), slice(to * HD, (to + 1) * HD)
                    dve.tensor_tensor(qs[0][into, 1, :, e, :], qt[own, :, 0:P], qs[0][own, 0, :, e, :].bitcast(F32),
                                      ALU.subtract).then_inc(first_split, 1)
            dve.wait_ge(first_split, 8)
            dve.sem_inc(qs_ready[0], 1)
            set_diagonal((0, 0, 0))
            dve.wait_ge(eye_done, 1)
            dve.tensor_scalar(mask[0][:, :], mask[0][:, :], 1.0, MASK / SCALE, ALU.subtract, ALU.mult) \
               .then_inc(mask_ready[0], 1)

            def head(new, one, two, three):
                if three is not None:
                    n, h = number(*three), three[1]
                    dve.wait_ge(out_ready, n + 1)
                    dve.tensor_reduce(o_t[h % 2][:, :], out[:, 0:2 * P].rearrange("p (a n) -> p n a", a=2), AX, ALU.add) \
                       .then_inc(out_used, 1)
                if new is not None:
                    t, h = new
                    i, s, u = t
                    m = number(t, h)
                    dve.wait_ge(scores_ready, m + 1)
                    if h == 0:
                        dve.wait_ge(mask_ready[u], s + 1)
                    dve.sem_inc(masked_begun, 1)
                    dve.tensor_tensor_reduce(out=p[h % 2][:, :], in0=scores[:, 0:N], in1=mask[u][:, 0:N],
                                             scale=-SCALE, scalar=3.0e38, op0=ALU.add, op1=ALU.min,
                                             accum_out=neg[:, h % 4:h % 4 + 1]).then_inc(masked_ready, 1)
                    if h == HEADS - 1:
                        dve.wait_ge(masked_ready, m + 1)
                        dve.sem_inc(mask_used[u], 1)
                    if h == HEADS - 3 and not (isinstance(i, int) and i == NT - 1):
                        set_diagonal((i + 1, s + u, 1 - u))
                if three is not None:
                    n, h = number(*three), three[1]
                    x = g.x[:, three[0][0], :]
                    dve.wait_ge(inv_ready, n + 1)
                    dve.wait_ge(proj_ready, n + 1)
                    dve.scalar_tensor_tensor(x, proj[:, 0:D], inv[:, h % 4:h % 4 + 1], x, ALU.mult, ALU.add) \
                       .then_inc(proj_used, 1)
                if one is not None:
                    for b in range(3):
                        dve.wait_ge(copied_high, 3 * number(*one) + b + 1)
                        for bank, high, low in pieces(one[1] % 2, b):
                            ins = dve.tensor_tensor(low, bank, high.bitcast(F32), ALU.subtract)
                        ins.then_inc(copied_low, 1)
                if two is not None:
                    n, h = number(*two), two[1]
                    dve.reciprocal(inv[:, h % 4:h % 4 + 1], total[:, h % 4:h % 4 + 1]).then_inc(inv_ready, 1)

            finish(tiles(dve, NT, lagged(head)), head)


def gate_stage(nc, g, d, name, hg, ex, ht):
    WA, WB = D + 2, D + 2
    with Stage(nc, name) as st:
        adj = [st.sb(f"adj{u}", [P, NT, P]) for u in range(2)]
        e = [st.sb(f"e{u}", [P, NT, P]) for u in range(2)]
        adj_parts, e_parts = ([[st.sb(f"{x}{u}{part}", [P, NT, P], F32R) for part in range(2)] for u in range(2)]
                              for x in ("adj_parts", "e_parts"))
        z = st.sb("z", [P, NT, P])
        a_left = st.sb("a_left", [P, DC, P])
        a_right = st.sb("a_right", [P, DC, 2])
        bias = st.sb("bias", [P, D])
        gate_bias = st.sb("gate_bias", [P, 2])
        left = st.sb("left", [P, NP])
        right = st.sb("right", [P, NT])
        xa = st.sb("xa", [P, NT, D])
        xb = st.sb("xb", [P, NT, D + 2])
        den = [st.sb(f"den{u}", [P, 1]) for u in range(2)]
        inv = [st.sb(f"inv{u}", [P, 1]) for u in range(2)]
        gate = st.sb("gate", [P, 2, NT])
        pleft = st.banks("pleft", 3)
        pright = st.banks("pright", 1)
        pa = [st.banks(f"pa{u}", 1) for u in range(2)]
        pb = [st.banks(f"pb{u}", 1) for u in range(2)]
        adj_in, adj_ready, e_masked, xa_ready, xb_ready, xa_used, xb_used = (st.sems(x) for x in (
            "adj_in", "adj_ready", "e_masked", "xa_ready", "xb_ready", "xa_used", "xb_used"))
        adj_high, e_high, e_low, begun, biased = (st.sem(x) for x in ("adj_high", "e_high", "e_low", "begun", "biased"))
        loaded, left_ready, left_copied, right_ready, z_step, exp_done, den_step, gate_asked, gate_done, mixed, \
            sig_done = (st.sem(x) for x in (
                "loaded", "left_ready", "left_copied", "right_ready", "z_step", "exp_done", "den_step",
                "gate_asked", "gate_done", "mixed", "sig_done"))
        right_taken = st.sem("right_taken")
        block = st.block()

        @block.sync
        def _(sp):
            sp.dma_start(a_left[:, :, :], d["a_left"]).then_inc(loaded, 16)
            sp.dma_start(a_right[:, :, :], d["a_right"]).then_inc(loaded, 16)
            sp.dma_start(bias[:, :], d["b_gcnb"].to_broadcast([P, D])).then_inc(loaded, 16)
            sp.dma_start(gate_bias[:, :], d["b_gates"].to_broadcast([P, 2])).then_inc(loaded, 16)

            def body(t, _):
                i, s, u = t
                sp.wait_ge(adj_ready[u], s)
                sp.wait_ge(e_masked[u], s)
                sp.dma_start(adj[u][:, :, :], d["adj_t"][bass.ds(i, 1), :, :, :].rearrange("a p k n -> (a p) k n")) \
                  .then_inc(adj_in[u], 16)

            tiles(sp, NT, body)

        @block.tensor
        def _(pe):
            pe.wait_ge(loaded, 64)
            for a in range(0, NP, BANK):
                size = min(BANK, NP - a)
                for c in range(DC):
                    ins = pe.matmul(pleft[:, a:a + size], a_left[:, c, :], ht[:, c, a:a + size],
                                    start=(c == 0), stop=(c == DC - 1))
            ins.then_inc(left_ready, 1)
            for k in range(NT):
                for c in range(DC):
                    ins = pe.matmul(pright[:, 2 * k:2 * k + 2], ht[:, c, k * P:(k + 1) * P], a_right[:, c, :],
                                    start=(c == 0), stop=(c == DC - 1))
            ins.then_inc(right_ready, 1)

            def body(t, _):
                i, s, u = t
                pe.wait_ge(adj_ready[u], s + 1)
                pe.wait_ge(xb_used[u], s)
                for k in range(NT):
                    n = rows_of(k)
                    ins = parts_product(pe, pb[u][:, 0:WB], [x[0:n, k, :] for x in adj_parts[u]],
                                        [hg[0:n, k, 0, part, 1 + D:1 + D + WB] for part in range(2)],
                                        k == 0, k == NT - 1)
                ins.then_inc(xb_ready[u], 1)
                pe.wait_ge(e_low, i + 1)
                pe.wait_ge(xa_used[u], s)
                for k in range(NT):
                    n = rows_of(k)
                    ins = parts_product(pe, pa[u][:, 0:WA], [x[0:n, k, :] for x in e_parts[u]],
                                        [hg[0:n, k, 0, part, 0:WA] for part in range(2)], k == 0, k == NT - 1)
                ins.then_inc(xa_ready[u], 1)

            tiles(pe, NT, body)

        @block.gpsimd
        def _(pool):
            pool.wait_ge(loaded, 64)

            def add_bias(t):
                i, s, u = t
                pool.wait_ge(xb_used[u], s + 1)
                pool.sem_inc(begun, 1)
                own = xb[:, bass.ds(i, 1), 0:D]
                pool.tensor_tensor(own, own, bias[:, :].unsqueeze(1), ALU.add).then_inc(biased, 1)

            def body(t, prev):
                i, s, u = t
                pool.wait_ge(adj_high, i + 1)
                pool.sem_inc(begun, 1)
                high, low = adj_parts[u]
                pool.tensor_tensor(low[:, :, :], adj[u][:, :, :], high[:, :, :].bitcast(F32), ALU.subtract) \
                    .then_inc(adj_ready[u], 1)
                if prev is not None:
                    add_bias(prev)

            add_bias(tiles(pool, NT, body))

        @block.scalar
        def _(act):
            act.wait_ge(left_ready, 1)
            act.copy(left[:, :], pleft[:, 0:NP]).then_inc(left_copied, 1)

            def xb_out(t):
                i, s, u = t
                act.wait_ge(xb_ready[u], s + 1)
                act.copy(xb[:, i, :], pb[u][:, 0:WB]).then_inc(xb_used[u], 1)

            def exponent(t):
                i, s, u = t
                act.wait_ge(z_step, 2 * i + 2)
                if not (isinstance(i, int) and i < 2):
                    act.wait_ge(e_low, i - 1)
                act.activation(e[u][:, :, :], z[:, :, :], ACT.Exp, scale=-1.0).then_inc(exp_done, 1)

            def body(t, prev):
                i, s, u = t
                act.wait_ge(adj_in[u], 16 * (s + 1))
                act.wait_ge(xb_ready[u], s)
                act.copy(adj_parts[u][0][:, :, :], adj[u][:, :, :]).then_inc(adj_high, 1)
                if prev is None:
                    exponent(t)
                else:
                    xb_out(prev)
                act.wait_ge(e_masked[u], s + 1)
                act.wait_ge(xa_ready[u], s)
                act.copy(e_parts[u][0][:, :, :], e[u][:, :, :]).then_inc(e_high, 1)
                if not (isinstance(i, int) and i == NT - 1):
                    exponent((i + 1, s + u, 1 - u))

            xb_out(tiles(act, NT, body))
            act.wait_ge(gate_asked, 2)
            act.activation(gate[:, :, :], gate[:, :, :], ACT.Sigmoid).then_inc(gate_done, 1)
            act.wait_ge(mixed, 2 * NT)
            act.activation(xa[:, :, :], xa[:, :, :], ACT.Sigmoid).then_inc(sig_done, 1)

        @block.vector
        def _(dve):
            dve.wait_ge(loaded, 64)
            dve.wait_ge(right_ready, 1)
            dve.tensor_copy(right[:, :], pright[:, 0:2 * NT].rearrange("p (n a) -> p n a", a=2)[:, :, 0]) \
               .then_inc(right_taken, 1)
            dve.wait_ge(right_taken, 1)
            dve.wait_ge(left_copied, 1)

            def xa_out(t):
                i, s, u = t
                dve.wait_ge(xa_ready[u], s + 1)
                dve.tensor_scalar(den[u][:, :], pa[u][:, 0:1], 1e-5, None, ALU.add).then_inc(den_step, 1)
                dve.wait_ge(den_step, 2 * i + 1)
                dve.reciprocal(inv[u][:, :], den[u][:, :]).then_inc(den_step, 1)
                dve.wait_ge(den_step, 2 * i + 2)
                dve.tensor_scalar(xa[:, i, :], pa[u][:, 1:D + 1], inv[u][:, 0:1], None, ALU.mult) \
                   .then_inc(xa_used[u], 1)

            def exponent(t):
                i, s, u = t
                dve.wait_ge(exp_done, i)
                dve.tensor_tensor(z[:, :, :], each(left[:, bass.ts(i, P)], NT), over(right[:, :], P), ALU.add) \
                   .then_inc(z_step, 1)
                dve.wait_ge(z_step, 2 * i + 1)
                dve.scalar_tensor_tensor(z[:, :, :], z[:, :, :], 0.01, z[:, :, :], ALU.mult, ALU.max) \
                   .then_inc(z_step, 1)

            def body(t, prev):
                i, s, u = t
                if prev is None:
                    exponent(t)
                dve.wait_ge(adj_in[u], 16 * (s + 1))
                dve.wait_ge(exp_done, i + 1)
                dve.scalar_tensor_tensor(e[u][:, :, :], adj[u][:, :, :], 0.0, e[u][:, :, :], ALU.not_equal, ALU.mult) \
                   .then_inc(e_masked[u], 1)
                if not (isinstance(i, int) and i == NT - 1):
                    exponent((i + 1, s + u, 1 - u))
                if prev is not None:
                    xa_out(prev)
                dve.wait_ge(e_high, i + 1)
                high, low = e_parts[u]
                dve.tensor_tensor(low[:, :, :], e[u][:, :, :], high[:, :, :].bitcast(F32), ALU.subtract) \
                   .then_inc(e_low, 1)

            xa_out(tiles(dve, NT, body))
            dve.wait_ge(xb_used[0], NT - NT // 2)
            dve.wait_ge(xb_used[1], NT // 2)
            dve.wait_ge(xa_used[0], NT - NT // 2)
            dve.wait_ge(xa_used[1], NT // 2)
            for k in range(2):
                dve.scalar_tensor_tensor(gate[:, k, :], xb[:, :, D + k], gate_bias[:, k:k + 1], ex[:, :, 2 + k],
                                         ALU.add, ALU.add).then_inc(gate_asked, 1)
            dve.wait_ge(gate_done, 1)
            for i in range(NT):
                dve.tensor_scalar(xa[:, i, :], xa[:, i, :], gate[:, 0, i:i + 1], None, ALU.mult).then_inc(mixed, 1)
            dve.wait_ge(biased, NT)
            for i in range(NT):
                dve.wait_ge(mixed, NT + i)
                dve.scalar_tensor_tensor(xa[:, i, :], xb[:, i, 0:D], gate[:, 1, i:i + 1], xa[:, i, :],
                                         ALU.mult, ALU.add).then_inc(mixed, 1)
            dve.wait_ge(sig_done, 1)
            dve.tensor_tensor(g.x[:, :, :], g.x[:, :, :], xa[:, :, :], ALU.add).then_inc(mixed, 1)
            dve.wait_ge(mixed, 2 * NT + 1)


def build(nc, d, out):
    with ExitStack() as ctx:
        def sb(name, shape, dt=F32):
            return ctx.enter_context(nc.sbuf_tensor(name, shape, dt))

        g = Shared(x=sb("x", [P, NT, D]), stats=sb("stats", [P, NT, 6]),
                  ident=sb("ident", [P, P]), ones=sb("ones", [P, P]),
                  zeros=sb("zeros", [P, D]), before=sb("before", [P, P]), iota=sb("iota", [P, IOTA]),
                  past_end=sb("past_end", [P, NT]),
                  cleared=[nc.alloc_semaphore(f"cleared{n}") for n in range(len(SLOTS))])
        start_stage(nc, g, d)
        with ExitStack() as layer:
            def lsb(name, shape):
                return layer.enter_context(nc.sbuf_tensor(name, shape, F32))

            vr = lsb("vr", [P, NT, 2 * D])
            xt = [layer.enter_context(nc.sbuf_tensor(f"xt{part}", [P, DC, NP], F32R)) for part in range(2)]
            qt, kt = lsb("qt", [P, DC, NP]), lsb("kt", [P, DC, N])
            v1 = lsb("v1", [P, NT, D])
            project_stage(nc, g, "proj0", g.x, True, d["w_vr0"], 2 * D, vr, d_bias=d["b_vr0"], xt=xt,
                          d_cols=(d["w_qk0"], d["b_qk0"]), cols=[(qt, NP, True, False), (kt, N, True, False)])
            hidden = vr[:, :, D:2 * D]
            attention_stage(nc, g, d, "att0", qt, kt, vr, hidden, 0)
            project_stage(nc, g, "proj1", hidden, False, d["w_v1"], D, v1, d_bias=d["b_v1"], xt=xt,
                          d_cols=(d["w_qk1"], d["b_qk1"]), cols=[(qt, NP, True, False), (kt, N, True, False)])
            attention_stage(nc, g, d, "att1", qt, kt, v1, hidden, 1)
        rest(nc, g, d, out)


def mixture(nc, g, d, n, gated, over_all, known=False, result=None):
    E, H, S = EXPERTS[n], HIDDEN[n], SLOTS[n]
    with ExitStack() as part:
        def psb(name, shape, dt=F32):
            return part.enter_context(nc.sbuf_tensor(f"mix{n}_{name}", shape, dt))

        xn = psb("xn", [P, NT, D])
        logits = psb("logits", [P, NT, E])
        r = Routing(psb("slot", [P, 2, NT], U32), psb("weight", [P, 2, NT]), psb("expert", [1, S], I32),
                    psb("side", [1, S], I32), psb("upto", [1, E], I32))
        project_stage(nc, g, f"gate{n}", g.x, True, d[f"w_gate{n}"], E, logits,
                      d_bias=d.get(f"b_gate{n}"), xn=xn, known=known)
        with ExitStack() as loaded:
            weights = Weights(nc, loaded, f"weights{n}", H, d[f"w_up{n}"], d[f"w_down{n}"], d.get(f"b_down{n}"))
            route_stage(nc, g, f"route{n}", E, S, logits, xn, d["slot_rows"][n], g.cleared[n], weights, r, over_all)
            expert_stage(nc, g, f"expert{n}", E, H, gated, S, d["slot_rows"][n], d["slot_out"][n], weights, r)
        if n == 0:
            combine_stage(nc, g, f"combine{n}", d["slot_out"][n], r, xn, d["gamma"], d["beta"])
        else:
            combine_stage(nc, g, f"combine{n}", d["slot_out"][n], r, result=result)


def rest(nc, g, d, out):
    mixture(nc, g, d, 0, False, 1, known=True)
    with ExitStack() as part:
        hidden = part.enter_context(nc.sbuf_tensor("hidden1", [P, NT, 1, 2, D], F32R))
        project_stage(nc, g, "proj2", g.x, True, d["w_spread"], D, hidden)
        spread_stage(nc, g, d, "spread", hidden, d["b_spread"])
    shift_stage(nc, g, "shift")
    with ExitStack() as part:
        def psb(name, shape, dt=F32):
            return part.enter_context(nc.sbuf_tensor(f"heads_{name}", shape, dt))

        FV = HEADS * HD
        v = psb("v", [P, NT, HEADS, 2, HD], F32R)
        qt, kt = psb("qt", [P, FV // P, NP]), psb("kt", [2 * HD, HEADS, N], F32R)
        with ExitStack() as inner:
            xt = [inner.enter_context(nc.sbuf_tensor(f"heads_xt{part}", [P, DC, NP], F32R)) for part in range(2)]
            project_stage(nc, g, "proj3", g.x, True, d["w_v2"], FV, v, xt=xt, d_cols=(d["w_qk2"], None),
                          cols=[(qt, NP, None, False), (kt, N, None, True)])
        heads_stage(nc, g, d, "heads", qt, kt, v, d["w_o2"])
    mixture(nc, g, d, 1, True, 0)
    with ExitStack() as part:
        def psb(name, shape):
            return part.enter_context(nc.sbuf_tensor(f"gat_{name}", shape, F32))

        hg = part.enter_context(nc.sbuf_tensor("gat_hg", [P, NT, 1, 2, 2 * D + 4], F32R))
        ex = psb("ex", [P, NT, 4])
        ht = psb("ht", [P, DC, NP])
        with ExitStack() as inner:
            xt = [inner.enter_context(nc.sbuf_tensor(f"gat_xt{part}", [P, DC, NP], F32R)) for part in range(2)]
            project_stage(nc, g, "proj4", g.x, True, d["w_hg"], 2 * D, hg[:, :, :, :, 1:2 * D + 1], xt=xt,
                          d_extra=d["w_gates"], extra=ex, d_cols=(d["w_sa"], None), cols=[(ht, NP, None, False)],
                          known=True)
        with Stage(nc, "ends") as st:
            written = st.sem("written")
            block = st.block()

            @block.vector
            def _(dve):
                last = slice(2 * D + 1, 2 * D + 3)
                ones = g.ones[:, 0:NT].unsqueeze(2)
                dve.tensor_copy(hg[:, :, 0, 0, 0:1], ones).then_inc(written, 1)
                dve.tensor_tensor(hg[:, :, 0, 1, 0:1], ones, ones, ALU.subtract).then_inc(written, 1)
                dve.tensor_copy(hg[:, :, 0, 0, last], ex[:, :, 0:2]).then_inc(written, 1)
                dve.wait_ge(written, 3)
                dve.tensor_tensor(hg[:, :, 0, 1, last], ex[:, :, 0:2], hg[:, :, 0, 0, last].bitcast(F32),
                                  ALU.subtract).then_inc(written, 1)
                dve.wait_ge(written, 4)

        gate_stage(nc, g, d, "gat", hg, ex, ht)
    mixture(nc, g, d, 2, True, 0, result=out)




def layouts(np, a):
    def rows(w):
        return np.ascontiguousarray(w.reshape(-1, P, w.shape[1]).transpose(1, 0, 2))

    def cols(*bs):
        return np.ascontiguousarray(np.concatenate(bs).reshape(-1, P).T)

    f32 = np.float32
    x = np.zeros((NP, D), f32)
    x[:N] = a["x"]
    adj = np.zeros((NP, NP), f32)
    adj[:N, :N] = a["adj"]
    arrays = {
        "x": rows(x),
        "adj_rows": adj.reshape(NT, P, NP),
        "w_vr0": rows(np.concatenate([a["L0_gnn_wv0"].T, a["L0_gnn_wres"].T], 1)),
        "b_vr0": np.concatenate([a["L0_gnn_bv0"], a["L0_gnn_bres"]])[None],
        "w_qk0": rows(np.concatenate([a["L0_gnn_wq0"].T, a["L0_gnn_wk0"].T], 1)),
        "b_qk0": cols(a["L0_gnn_bq0"], a["L0_gnn_bk0"]),
        "w_v1": rows(a["L0_gnn_wv1"].T),
        "b_v1": a["L0_gnn_bv1"][None],
        "w_qk1": rows(np.concatenate([a["L0_gnn_wq1"].T, a["L0_gnn_wk1"].T], 1)),
        "b_qk1": cols(a["L0_gnn_bq1"], a["L0_gnn_bk1"]),
    }
    arrays["adj_t"] = adj.reshape(NT, P, NT, P).transpose(0, 3, 2, 1)

    def tiled(w):
        return w.reshape(w.shape[0], -1, P, w.shape[2]).transpose(0, 2, 1, 3).reshape(w.shape[0], P, -1)

    arrays.update(
        w_gate0=rows(a["L0_ffn_Wg"]), b_gate0=a["L0_ffn_bg"][None],
        w_up0=np.concatenate([tiled(a["L0_ffn_W1"]), tiled(a["L0_ffn_b1"][:, :, None])], 2), w_down0=tiled(a["L0_ffn_W2"]),
        b_down0=a["L0_ffn_b2"],
        gamma=a["L0_ffn_gamma"][None], beta=a["L0_ffn_beta"][None],
        w_spread=rows(a["L1_gnn_W"].transpose(1, 0, 2).reshape(D, D)), b_spread=a["L1_gnn_b"].reshape(1, D),
        w_v2=rows(a["L2_gnn_Wvs"].transpose(1, 0, 2).reshape(D, HEADS * HD)),
        w_qk2=rows(np.concatenate([a[f"L2_gnn_{w}"].transpose(1, 0, 2).reshape(D, HEADS * HD) for w in ("Wqs", "Wks")], 1)),
        w_o2=np.concatenate([a["L2_gnn_Wo"].transpose(1, 0, 2)] * 2, 0),
        w_gate1=rows(a["L2_ffn_gate_w"]),
        w_up1=tiled(np.concatenate([a["L2_ffn_W1"], a["L2_ffn_W3"]], 2)), w_down1=tiled(a["L2_ffn_W2"]),
        w_hg=rows(np.concatenate([a["L3_gnn_W_sa"], a["L3_gnn_W_gcnb"]], 1)),
        w_sa=rows(a["L3_gnn_W_sa"]),
        w_gates=rows(np.concatenate([a["L3_gnn_Wa"].reshape(2, D), a["L3_gnn_Wb"].reshape(2, D)])[[0, 2, 1, 3]].T),
        a_left=rows(np.repeat(a["L3_gnn_a_sa"][0, :D, None], P, 1)),
        a_right=rows(np.repeat(a["L3_gnn_a_sa"][0, D:, None], 2, 1)),
        b_gcnb=a["L3_gnn_b_gcnb"][None],
        b_gates=np.concatenate([a["L3_gnn_ba"], a["L3_gnn_bb"]])[None],
        w_gate2=rows(a["L3_ffn_gate_w"].T),
        w_up2=tiled(np.concatenate([a["L3_ffn_w1"].transpose(0, 2, 1), a["L3_ffn_w3"].transpose(0, 2, 1)], 2)),
        w_down2=tiled(a["L3_ffn_w2"].transpose(0, 2, 1)),
    )
    return arrays


def kernel(**inputs):
    import numpy as np
    import concourse.bacc as bacc
    from concourse.bass_utils import run_bass_kernel_spmd

    nc = bacc.Bacc("TRN2", target_bir_lowering=False, num_devices=1)
    arrays = {k: np.ascontiguousarray(v) for k, v in
              layouts(np, {k: np.asarray(v) for k, v in inputs.items()}).items()}
    d = {k: nc.dram_tensor(f"in_{k}", v.shape, mybir.dt.from_np(v.dtype), kind="ExternalInput").ap()
         for k, v in arrays.items()}
    d["slot_rows"] = [nc.dram_tensor(f"slot_rows{n}", (s * P, D), F32, kind="Internal").ap() for n, s in enumerate(SLOTS)]
    d["slot_out"] = [nc.dram_tensor(f"slot_out{n}", (s * P, D), F32, kind="Internal").ap() for n, s in enumerate(SLOTS)]
    out = nc.dram_tensor("out", (N, D), F32, kind="ExternalOutput").ap()
    build(nc, d, out)
    return run_bass_kernel_spmd(nc, [{f"in_{k}": v for k, v in arrays.items()}], core_ids=[0]).results[0]["out"]
```
